# Optimizing a Trainium2 kernel written in Bass

```python
import numpy as np
import jax
import jax.numpy as jnp

def _softmax(x, axis=-1):
    return jax.nn.softmax(x, axis=axis)

def _gelu(x):
    return jax.nn.gelu(x, approximate=True)

def _silu(x):
    return jax.nn.silu(x)

def _sigmoid(x):
    return jax.nn.sigmoid(x)

def _layernorm(x, axis=-1, eps=1e-05):
    m = jnp.mean(x, axis=axis, keepdims=True)
    v = jnp.var(x, axis=axis, keepdims=True)
    return (x - m) / jnp.sqrt(v + eps)

def _scatter_add(tgt, idx, src, axis=0):
    return tgt.at[idx].add(src)

def _segment_sum(src, seg, n):
    return jax.ops.segment_sum(src, seg, n)
kernel_name = 'mk_conv_attn_hybrid_d2_conv_nhwc128_r2_5cfb89'

def setup_inputs(seed: int=0):
    np.random.seed(seed)
    _w = jnp.asarray

    def _rec_inputs():
        import jax
        import jax.numpy as jnp
        _gk = jax.random.key(seed)
        x = -0.000929 + 1 * jax.random.normal(jax.random.fold_in(_gk, 1), (2, 32, 32, 64), jnp.float32)
        return x
    x = _rec_inputs()

    def _L0_conv_setup():
        import jax, jax.numpy as jnp
        import numpy as np
        NUM_HEADS = 4
        KERNEL = 7

        def _layernorm(x, g, b, eps=1e-05):
            m = x.mean(-1, keepdims=True)
            v = ((x - m) ** 2).mean(-1, keepdims=True)
            return (x - m) * jax.lax.rsqrt(v + eps) * g + b

        def _window_idx(L, k):
            start = np.clip(np.arange(L) - k // 2, 0, L - k)
            idx = start[:, None] + np.arange(k)[None, :]
            rel = idx - np.arange(L)[:, None] + (k - 1)
            return (jnp.asarray(idx), jnp.asarray(rel))

        def _neighborhood_attention(x, qkv_w, qkv_b, rpb, proj_w, proj_b):
            B, H, W, C = x.shape
            nh, k = (NUM_HEADS, KERNEL)
            hd = C // nh
            qkv = (x @ qkv_w + qkv_b).reshape(B, H, W, 3, nh, hd)
            qkv = jnp.transpose(qkv, (3, 0, 4, 1, 2, 5))
            q = qkv[0] * hd ** (-0.5)
            key = qkv[1]
            val = qkv[2]
            idx_i, rel_i = _window_idx(H, k)
            idx_j, rel_j = _window_idx(W, k)
            kwin = key[:, :, idx_i][:, :, :, :, idx_j]
            vwin = val[:, :, idx_i][:, :, :, :, idx_j]
            attn = jnp.einsum('nhijc,nhiajbc->nhijab', q, kwin)
            bias = rpb[:, rel_i][..., rel_j]
            bias = jnp.transpose(bias, (0, 1, 3, 2, 4))
            attn = attn + bias[None]
            attn = jax.nn.softmax(attn.reshape(B, nh, H, W, k * k), axis=-1)
            attn = attn.reshape(B, nh, H, W, k, k)
            out = jnp.einsum('nhijab,nhiajbc->nhijc', attn, vwin)
            out = jnp.transpose(out, (0, 2, 3, 1, 4)).reshape(B, H, W, C)
            return out @ proj_w + proj_b
        B, H, W, C = (2, 32, 32, 64)
        hidden = int(C * 4.0)
        k2 = 2 * KERNEL - 1
        key = jax.random.key(seed)
        ks = jax.random.split(key, 8)
        s = 0.02
        return {'x': jax.random.normal(ks[0], (B, H, W, C), jnp.float32), 'norm1_g': jnp.ones((C,), jnp.float32), 'norm1_b': jnp.zeros((C,), jnp.float32), 'qkv_w': jax.random.normal(ks[1], (C, 3 * C), jnp.float32) * s, 'qkv_b': jnp.zeros((3 * C,), jnp.float32), 'rpb': jax.random.normal(ks[2], (NUM_HEADS, k2, k2), jnp.float32) * s, 'proj_w': jax.random.normal(ks[3], (C, C), jnp.float32) * s, 'proj_b': jnp.zeros((C,), jnp.float32), 'norm2_g': jnp.ones((C,), jnp.float32), 'norm2_b': jnp.zeros((C,), jnp.float32), 'fc1_w': jax.random.normal(ks[4], (C, hidden), jnp.float32) * s, 'fc1_b': jnp.zeros((hidden,), jnp.float32), 'fc2_w': jax.random.normal(ks[5], (hidden, C), jnp.float32) * s, 'fc2_b': jnp.zeros((C,), jnp.float32)}
    _L0_conv_all = _L0_conv_setup()
    _L0_conv_in = {k: v for k, v in _L0_conv_all.items() if k in ('norm1_g', 'norm1_b', 'qkv_w', 'qkv_b', 'rpb', 'proj_w', 'proj_b', 'norm2_g', 'norm2_b', 'fc1_w', 'fc1_b', 'fc2_w', 'fc2_b')}
    del _L0_conv_all

    def _L1_attn_setup():
        import jax, jax.numpy as jnp
        import numpy as np
        EMB = 64
        HEADS = 8
        B, T = (4, 1024)
        key = jax.random.key(seed)
        ks = jax.random.split(key, 6)
        s_in = 1.0 / np.sqrt(EMB)
        s_un = 1.0 / np.sqrt(EMB * HEADS)
        return {'x': jax.random.normal(ks[0], (B, T, EMB), dtype=jnp.float32), 'Wq': jax.random.normal(ks[1], (EMB, EMB * HEADS), dtype=jnp.float32) * s_in, 'Wk': jax.random.normal(ks[2], (EMB, EMB * HEADS), dtype=jnp.float32) * s_in, 'Wv': jax.random.normal(ks[3], (EMB, EMB * HEADS), dtype=jnp.float32) * s_in, 'Wu': jax.random.normal(ks[4], (EMB * HEADS, EMB), dtype=jnp.float32) * s_un, 'bu': jnp.zeros((EMB,), dtype=jnp.float32)}
    _L1_attn_all = _L1_attn_setup()
    _L1_attn_in = {k: v for k, v in _L1_attn_all.items() if k in ('Wq', 'Wk', 'Wv', 'Wu', 'bu')}
    del _L1_attn_all

    def _L1_ffn_setup():
        import jax, jax.numpy as jnp
        import numpy as np
        NB, NOPS = (33, 19)
        D, H = (64, 256)
        B, S = (8, 512)
        CARRY_OPS = [0, 1, 2, 10, 11, 12, 13]

        def _build_masks():
            am = np.zeros((NB, NOPS), dtype=bool)
            fm = np.zeros((NB, NOPS), dtype=bool)
            fm[0, :] = True
            for b in range(1, 8):
                am[b, CARRY_OPS] = True
                fm[b, CARRY_OPS] = True
            am[8, [14, 15, 8, 9]] = True
            fm[8, [14, 15, 8, 9]] = True
            for b in range(16, 32):
                fm[b, [3, 4]] = True
            am[32, [10, 11, 12, 13]] = True
            fm[32, [5, 6, 7, 2, 4, 10, 11, 12, 13]] = True
            return (jnp.asarray(am), jnp.asarray(fm))
        key = jax.random.key(seed)
        ks = jax.random.split(key, 9)
        sd = 1.0 / np.sqrt(D)
        sh = 1.0 / np.sqrt(H)
        am, fm = _build_masks()
        return {'x': jax.random.normal(ks[0], (B, S, D), jnp.float32), 'ffn_w1': jax.random.normal(ks[1], (NB, NOPS, D, H), jnp.float32) * sd, 'ffn_b1': jnp.zeros((NB, NOPS, H), jnp.float32), 'ffn_w2': jax.random.normal(ks[2], (NB, NOPS, H, D), jnp.float32) * sh, 'ffn_b2': jnp.zeros((NB, NOPS, D), jnp.float32), 'wq': jax.random.normal(ks[3], (NB, NOPS, D, D), jnp.float32) * sd, 'wk': jax.random.normal(ks[4], (NB, NOPS, D, D), jnp.float32) * sd, 'wv': jax.random.normal(ks[5], (NB, NOPS, D, D), jnp.float32) * sd, 'wo': jax.random.normal(ks[6], (NB, NOPS, D, D), jnp.float32) * sd, 'attn_mask': am, 'ffn_mask': fm}
    _L1_ffn_all = _L1_ffn_setup()
    _L1_ffn_in = {k: v for k, v in _L1_ffn_all.items() if k in ('ffn_w1', 'ffn_b1', 'ffn_w2', 'ffn_b2', 'wq', 'wk', 'wv', 'wo', 'attn_mask', 'ffn_mask')}
    del _L1_ffn_all
    return {'x': x, 'L0_conv_norm1_g': _L0_conv_in['norm1_g'], 'L0_conv_norm1_b': _L0_conv_in['norm1_b'], 'L0_conv_qkv_w': _L0_conv_in['qkv_w'], 'L0_conv_qkv_b': _L0_conv_in['qkv_b'], 'L0_conv_rpb': _L0_conv_in['rpb'], 'L0_conv_proj_w': _L0_conv_in['proj_w'], 'L0_conv_proj_b': _L0_conv_in['proj_b'], 'L0_conv_norm2_g': _L0_conv_in['norm2_g'], 'L0_conv_norm2_b': _L0_conv_in['norm2_b'], 'L0_conv_fc1_w': _L0_conv_in['fc1_w'], 'L0_conv_fc1_b': _L0_conv_in['fc1_b'], 'L0_conv_fc2_w': _L0_conv_in['fc2_w'], 'L0_conv_fc2_b': _L0_conv_in['fc2_b'], 'L1_attn_Wq': _L1_attn_in['Wq'], 'L1_attn_Wk': _L1_attn_in['Wk'], 'L1_attn_Wv': _L1_attn_in['Wv'], 'L1_attn_Wu': _L1_attn_in['Wu'], 'L1_attn_bu': _L1_attn_in['bu'], 'L1_ffn_ffn_w1': _L1_ffn_in['ffn_w1'], 'L1_ffn_ffn_b1': _L1_ffn_in['ffn_b1'], 'L1_ffn_ffn_w2': _L1_ffn_in['ffn_w2'], 'L1_ffn_ffn_b2': _L1_ffn_in['ffn_b2'], 'L1_ffn_wq': _L1_ffn_in['wq'], 'L1_ffn_wk': _L1_ffn_in['wk'], 'L1_ffn_wv': _L1_ffn_in['wv'], 'L1_ffn_wo': _L1_ffn_in['wo'], 'L1_ffn_attn_mask': _L1_ffn_in['attn_mask'], 'L1_ffn_ffn_mask': _L1_ffn_in['ffn_mask']}

def reference(x, L0_conv_norm1_g, L0_conv_norm1_b, L0_conv_qkv_w, L0_conv_qkv_b, L0_conv_rpb, L0_conv_proj_w, L0_conv_proj_b, L0_conv_norm2_g, L0_conv_norm2_b, L0_conv_fc1_w, L0_conv_fc1_b, L0_conv_fc2_w, L0_conv_fc2_b, L1_attn_Wq, L1_attn_Wk, L1_attn_Wv, L1_attn_Wu, L1_attn_bu, L1_ffn_ffn_w1, L1_ffn_ffn_b1, L1_ffn_ffn_w2, L1_ffn_ffn_b2, L1_ffn_wq, L1_ffn_wk, L1_ffn_wv, L1_ffn_wo, L1_ffn_attn_mask, L1_ffn_ffn_mask):
    import jax
    import jax.numpy as jnp

    def _L0_conv_ref(x, norm1_g, norm1_b, qkv_w, qkv_b, rpb, proj_w, proj_b, norm2_g, norm2_b, fc1_w, fc1_b, fc2_w, fc2_b):
        import jax, jax.numpy as jnp
        import numpy as np
        NUM_HEADS = 4
        KERNEL = 7

        def _layernorm(x, g, b, eps=1e-05):
            m = x.mean(-1, keepdims=True)
            v = ((x - m) ** 2).mean(-1, keepdims=True)
            return (x - m) * jax.lax.rsqrt(v + eps) * g + b

        def _window_idx(L, k):
            start = np.clip(np.arange(L) - k // 2, 0, L - k)
            idx = start[:, None] + np.arange(k)[None, :]
            rel = idx - np.arange(L)[:, None] + (k - 1)
            return (jnp.asarray(idx), jnp.asarray(rel))

        def _neighborhood_attention(x, qkv_w, qkv_b, rpb, proj_w, proj_b):
            B, H, W, C = x.shape
            nh, k = (NUM_HEADS, KERNEL)
            hd = C // nh
            qkv = (x @ qkv_w + qkv_b).reshape(B, H, W, 3, nh, hd)
            qkv = jnp.transpose(qkv, (3, 0, 4, 1, 2, 5))
            q = qkv[0] * hd ** (-0.5)
            key = qkv[1]
            val = qkv[2]
            idx_i, rel_i = _window_idx(H, k)
            idx_j, rel_j = _window_idx(W, k)
            kwin = key[:, :, idx_i][:, :, :, :, idx_j]
            vwin = val[:, :, idx_i][:, :, :, :, idx_j]
            attn = jnp.einsum('nhijc,nhiajbc->nhijab', q, kwin)
            bias = rpb[:, rel_i][..., rel_j]
            bias = jnp.transpose(bias, (0, 1, 3, 2, 4))
            attn = attn + bias[None]
            attn = jax.nn.softmax(attn.reshape(B, nh, H, W, k * k), axis=-1)
            attn = attn.reshape(B, nh, H, W, k, k)
            out = jnp.einsum('nhijab,nhiajbc->nhijc', attn, vwin)
            out = jnp.transpose(out, (0, 2, 3, 1, 4)).reshape(B, H, W, C)
            return out @ proj_w + proj_b
        h = _neighborhood_attention(_layernorm(x, norm1_g, norm1_b), qkv_w, qkv_b, rpb, proj_w, proj_b)
        x = x + h
        y = _layernorm(x, norm2_g, norm2_b)
        y = jax.nn.gelu(y @ fc1_w + fc1_b, approximate=False)
        y = y @ fc2_w + fc2_b
        return x + y

    def _L1_attn_ref(x, Wq, Wk, Wv, Wu, bu):
        import jax, jax.numpy as jnp
        import numpy as np
        EMB = 64
        HEADS = 8
        B, T = (4, 1024)
        b, t, e = x.shape
        h = HEADS
        scale = e ** (-0.25)
        q = (x @ Wq).reshape(b, t, h, e) * scale
        k = (x @ Wk).reshape(b, t, h, e) * scale
        v = (x @ Wv).reshape(b, t, h, e)
        dot = jnp.einsum('bqhe,bkhe->bhqk', q, k)
        att = jax.nn.softmax(dot, axis=-1)
        out = jnp.einsum('bhqk,bkhe->bqhe', att, v).reshape(b, t, h * e)
        return out @ Wu + bu

    def _L1_ffn_ref(x, ffn_w1, ffn_b1, ffn_w2, ffn_b2, wq, wk, wv, wo, attn_mask, ffn_mask):
        import jax, jax.numpy as jnp
        import numpy as np
        NB, NOPS = (33, 19)
        D, H = (64, 256)
        B, S = (8, 512)
        CARRY_OPS = [0, 1, 2, 10, 11, 12, 13]

        def _build_masks():
            am = np.zeros((NB, NOPS), dtype=bool)
            fm = np.zeros((NB, NOPS), dtype=bool)
            fm[0, :] = True
            for b in range(1, 8):
                am[b, CARRY_OPS] = True
                fm[b, CARRY_OPS] = True
            am[8, [14, 15, 8, 9]] = True
            fm[8, [14, 15, 8, 9]] = True
            for b in range(16, 32):
                fm[b, [3, 4]] = True
            am[32, [10, 11, 12, 13]] = True
            fm[32, [5, 6, 7, 2, 4, 10, 11, 12, 13]] = True
            return (jnp.asarray(am), jnp.asarray(fm))
        scale = jnp.asarray(1.0 / np.sqrt(D), x.dtype)

        def step(h, p):
            op = jnp.argmax(h[0, 0, :NOPS])
            q = h @ p['wq'][op]
            k = h @ p['wk'][op]
            v = h @ p['wv'][op]
            attn = jax.nn.softmax(jnp.einsum('bqd,bkd->bqk', q, k) * scale, axis=-1)
            y = jnp.einsum('bqk,bkd->bqd', attn, v) @ p['wo'][op]
            h = jnp.where(p['am'][op], y, h)
            z = jax.nn.relu(h @ p['w1'][op] + p['b1'][op]) @ p['w2'][op] + p['b2'][op]
            h = jnp.where(p['fm'][op], z, h)
            return (h, None)
        xs = {'w1': ffn_w1, 'b1': ffn_b1, 'w2': ffn_w2, 'b2': ffn_b2, 'wq': wq, 'wk': wk, 'wv': wv, 'wo': wo, 'am': attn_mask, 'fm': ffn_mask}
        out, _ = jax.lax.scan(step, x, xs)
        return out

    def _gn(v, G=32, eps=1e-05):
        B_, H_, W_, C_ = v.shape
        g = v.reshape(B_, H_, W_, G, C_ // G)
        m = jnp.mean(g, axis=(1, 2, 4), keepdims=True)
        s = jnp.var(g, axis=(1, 2, 4), keepdims=True)
        return ((g - m) / jnp.sqrt(s + eps)).reshape(v.shape)

    def _ln_c(v, eps=1e-06):
        m = jnp.mean(v, axis=-1, keepdims=True)
        s = jnp.var(v, axis=-1, keepdims=True)
        return (v - m) / jnp.sqrt(s + eps)

    def _ln_t(v, eps=1e-05):
        m = jnp.mean(v, axis=-1, keepdims=True)
        s = jnp.var(v, axis=-1, keepdims=True)
        return (v - m) / jnp.sqrt(s + eps)

    def _to_tokens(v):
        B_, H_, W_, C_ = v.shape
        return v.reshape(B_, H_ * W_, C_)

    def _from_tokens(t, like):
        return t.reshape(like.shape)
    x = _L0_conv_ref(x, L0_conv_norm1_g, L0_conv_norm1_b, L0_conv_qkv_w, L0_conv_qkv_b, L0_conv_rpb, L0_conv_proj_w, L0_conv_proj_b, L0_conv_norm2_g, L0_conv_norm2_b, L0_conv_fc1_w, L0_conv_fc1_b, L0_conv_fc2_w, L0_conv_fc2_b)
    t = _to_tokens(x)
    t = t + _L1_attn_ref(_ln_t(t), L1_attn_Wq, L1_attn_Wk, L1_attn_Wv, L1_attn_Wu, L1_attn_bu)
    t = t + _L1_ffn_ref(_ln_t(t), L1_ffn_ffn_w1, L1_ffn_ffn_b1, L1_ffn_ffn_w2, L1_ffn_ffn_b2, L1_ffn_wq, L1_ffn_wk, L1_ffn_wv, L1_ffn_wo, L1_ffn_attn_mask, L1_ffn_ffn_mask)
    x = _from_tokens(t, x)
    return x

_drawn_inputs = setup_inputs


def setup_inputs(seed=0):
    import zlib

    import numpy as np

    out = dict(_drawn_inputs(seed))
    spreads = {'L0_conv_norm1_g': (1.0, 0.6),
     'L0_conv_norm1_b': (0.0, 0.8),
     'L0_conv_qkv_b': (0.0, 0.428),
     'L0_conv_proj_b': (0.0, 0.1),
     'L0_conv_norm2_g': (1.0, 0.6),
     'L0_conv_norm2_b': (0.0, 2.0),
     'L0_conv_fc1_b': (0.0, 0.341),
     'L0_conv_fc2_b': (0.0, 0.1),
     'L1_attn_bu': (0.0, 0.1),
     'L1_ffn_ffn_b1': (0.0, 0.1),
     'L1_ffn_ffn_b2': (0.0, 0.1)}
    factors = {'L0_conv_qkv_w': 8.0,
     'L0_conv_rpb': 8.0,
     'L0_conv_proj_w': 3.396,
     'L1_ffn_wq': 3.912,
     'L1_ffn_wk': 3.83}
    for name, (base, spread) in spreads.items():
        noise = np.random.default_rng([zlib.crc32(name.encode()), seed]).standard_normal(out[name].shape)
        drawn = base * np.exp(spread * noise) if base else spread * noise
        out[name] = jnp.asarray(drawn.astype(out[name].dtype))
    for name, factor in factors.items():
        out[name] = (out[name] * factor).astype(out[name].dtype)
    return out
```

```python
from contextlib import ExitStack

import concourse.bass as bass
from concourse import mybir

F32 = mybir.dt.float32
I32 = mybir.dt.int32
U8 = mybir.dt.uint8
ALU = mybir.AluOpType
ACT = mybir.ActivationFunctionType
AX = mybir.AxisListType

P = 128
B, HH, WW, C = 2, 32, 32, 64
TOK = HH * WW
NT = TOK // P
BLK = 512
NB = TOK // BLK
EPS = 1e-5
NEG = -1e30

NH0, WIN = 4, 7
HD0 = C // NH0
ROWS = P // WW
REL = 2 * WIN - 1
HID = 4 * C
UN0 = NT * NH0

NH1 = 8
NPAIR = NH1 // 2
GRP = 8
QT = BLK // P

NSTEP, NOPS = 33, 19
FH = 256
NONE = 4 * 64
LN = 6
NCTL = 14

WLOADS = 16 * (13 + 14)


def window_keys(t):
    first = min(max(ROWS * t - WIN // 2, 0), HH - WIN)
    last = min(max(ROWS * t + ROWS - 1 - WIN // 2, 0), HH - WIN) + WIN - 1
    return first, last - first + 1, (0 if t == 0 else 2 if t == NT - 1 else 1)


def key_chunks(t):
    first, rows, kind = window_keys(t)
    at, n = first * WW, rows * WW
    out = []
    while n > 0:
        k = min(P, n)
        slot = NT + at // P if kind == 0 else (at - WW) // P
        out.append((at, k, slot))
        at, n = at + k, n - k
    return out


VTILES = [(WW + P * j, min(P, TOK - WW - P * j)) for j in range(NT)] + [(0, P), (P, 3 * WW)]

LAG_PV, LAG_OUT, LAG_Y, LAG_YD = 10, 18, 19, 22


def build(nc, a, out):
    ctx = ExitStack()
    with ctx:
        def sb(name, shape, dt=F32):
            return ctx.enter_context(nc.sbuf_tensor(name, shape, dt))

        def sem(name):
            return ctx.enter_context(nc.semaphore(name))

        PS = ctx.enter_context(nc.psum_tensor("PS", [P, 8, 512], F32))
        LO, HI, OB, YB = PS[:, 4, :], PS[:, 5, :], PS[:, 6, :], PS[:, 7, :]

        ident = sb("ident", [P, P])
        shift = sb("shift", [REL, ROWS + 1, WW])
        colmask = sb("colmask", [P, WW])
        steps4 = sb("steps4", [1, NSTEP])
        opnum = sb("opnum", [1, NOPS])

        wq0 = sb("wq0", [C, NH0, 32])
        wk0 = sb("wk0", [C, NH0, 32])
        wv0 = sb("wv0", [C, C])
        bq0 = sb("bq0", [P, 1])
        bq0s = sb("bq0s", [P, 1])
        bk0 = sb("bk0", [P, 1])
        bv0 = sb("bv0", [P, C])
        norm = sb("norm", [C, 4])
        rpbT = sb("rpbT", [REL, NH0 * REL])
        pw0 = sb("pw0", [P, C])
        pb0 = sb("pb0", [P, C])
        fc1 = sb("fc1", [C, HID])
        fb1 = sb("fb1", [P, 2])
        fc2 = sb("fc2", [P, 2, C])
        fb2 = sb("fb2", [P, C])
        bu1 = sb("bu1", [P, C])
        wu1 = sb("wu1", [P, NPAIR, C])
        wq1 = sb("wq1", [C, P])
        wk1 = sb("wk1", [C, P])
        wv1 = sb("wv1", [C, P])
        wu = sb("wu", [P, C])

        xall = sb("xall", [P, B * NT, C])
        x2 = sb("x2", [P, B * NT, C])
        xn = sb("xn", [P, NT, C])
        xsq = sb("xsq", [P, NT, C])
        mean = sb("mean", [P, NT])
        var = sb("var", [P, NT])
        rstd = sb("rstd", [P, NT])
        minus_half = sb("minus_half", [P, NT])
        xb = sb("xb", [P, NT, C])
        x1 = sb("x1", [P, NT, C])
        xT = sb("xT", [C, TOK])
        qT0 = sb("qT0", [P, TOK])
        kT0 = sb("kT0", [P, TOK])
        V0 = sb("V0", [P, NT + 2, NH0, 32])
        tall = sb("tall", [P, NH0 * REL, WW])
        tabs = [sb(f"table{k}", [P, NH0, n, WW]) for k, n in enumerate((WIN, WIN + ROWS - 1, WIN))]
        OT0 = sb("OT0", [P, 2, P])
        PT0 = sb("PT0", [P, 4, 3, P])
        G0 = sb("G0", [P, 2, TOK])
        aT = sb("aT", [C, B * TOK])
        prob = sb("prob", [P, 3, TOK])
        negm = sb("negm", [P, 4])
        rsum = sb("rsum", [P, 4])
        rinv = sb("rinv", [P, 4])
        qT = sb("qT", [P, B * TOK])
        kT = sb("kT", [P, B * TOK])
        V = sb("V", [P, B * NT, P])
        PT = sb("PT", [P, 2, 2, NT, BLK])
        OT = sb("OT", [P, 2, BLK])

        mask8 = sb("mask8", [1, 2, NSTEP, NOPS], U8)
        codes = sb("codes", [1, NSTEP, NOPS])
        codew = sb("codew", [1, NSTEP, NOPS])
        code = sb("code", [1, NSTEP])
        key = sb("key", [1, NSTEP])
        dead = sb("dead", [1, NSTEP])
        row = sb("row", [1, C])
        top = sb("top", [1, 1])
        hit = sb("hit", [1, NOPS])
        cand = sb("cand", [1, NOPS])
        opf = sb("opf", [1, 1])
        nextf = sb("nextf", [1, 1])
        count_i = sb("count_i", [1, NSTEP], I32)
        control = sb("control", [1, NSTEP + 1, 2], I32)
        wqs = sb("wqs", [C, C])
        wks = sb("wks", [C, C])
        wvs = sb("wvs", [C, C])
        wos = sb("wos", [P, C])
        w1s = sb("w1s", [C, FH])
        w2s = sb("w2s", [P, 2, C])
        b1s = sb("b1s", [P, 2])
        b2s = sb("b2s", [C, 1])
        Z = PT[:, 0, :, :, :].rearrange("p l k q -> p (l k q)")[:, 0:2 * B * TOK].rearrange("p (h t) -> p h t", h=2)

        gate = sem("gate")
        x_loaded = sem("x_loaded")
        zeroed = sem("zeroed")
        w_loaded = sem("w_loaded")
        late_loaded = sem("late_loaded")
        ident_made = sem("ident_made")
        pool_chain = sem("pool_chain")
        consts_made = sem("consts_made")
        bias_expanded = sem("bias_expanded")
        bias_masked = sem("bias_masked")
        bq_scaled = sem("bq_scaled")
        tables_made = sem("tables_made")
        codes_made = sem("codes_made")
        stored = sem("stored")

        def ring(name):
            return {k: sem(f"{name}_piece_{k}") for k in
                    ("lo_filled", "lo_drained", "hi_filled", "hi_drained", "mid_filled", "mid_drained",
                     "y_filled", "y_drained")}

        def core(name):
            return {k: sem(f"{name}_{k}") for k in
                    ("scored", "maxed", "exped", "inverted", "scaled", "lo_turned", "hi_turned",
                     "lo_drained", "hi_drained", "out_summed", "out_drained", "y_filled", "y_drained")}

        r0, c0 = ring("nat"), core("nat")
        ln0 = sem("nat_ln_chain")
        normed = sem("nat_normed")
        biased = sem("nat_biased")
        stage1_done = sem("stage1_done")
        r1, c1 = ring("glob"), core("glob")
        pair_loaded = sem("pair_loaded")
        pair_used = sem("pair_used")
        ln3 = sem("state_ln_chain")
        normed3 = sem("state_normed")
        r3 = ring("state")
        r2, c2 = ring("routed"), core("routed")
        rf = ring("ffn")
        rstd_made = sem("rstd_made")
        control_ready = sem("control_ready")
        ctl_chain = sem("ctl_chain")
        row_turned = sem("row_turned")
        attn_loaded = sem("attn_loaded")
        ffn_loaded = sem("ffn_loaded")
        re = ring("end")
        result = sem("result")

        scores2 = [PS[:, 2 * k:2 * k + 2, :].rearrange("p a b -> p (a b)") for k in range(2)]

        block = ctx.enter_context(nc.Block())

        N0 = dict(lo=5 + NB, hi=5 + 2, mid=NB, y=2)
        N1 = dict(lo=6, hi=6)
        N2 = dict(lo=3, hi=3, y=4)
        NF = dict(lo=4 + 2, hi=4 + 2)

        def nat_drain(copy, func, bank, u):
            t = u // NH0
            chunks = key_chunks(t)
            full = len(chunks) - 1
            k = chunks[-1][1]
            args = (func,) if func is not None else ()
            copy(PT0[:, u % 4, 0:full, :], bank[:, 0:full * P].rearrange("p (n q) -> p n q", n=full), *args)
            return copy(PT0[0:k, u % 4, full, :], bank[0:k, full * P:(full + 1) * P], *args)

        def scan(e, attend, feed, after):
            word = e.alloc_register("word")
            na = e.alloc_register("attended")
            nf = e.alloc_register("fed")
            nu = e.alloc_register("updates")
            for r in (na, nf, nu):
                e.reg_mov(r, 0)
            e.wait_ge(control_ready, 1)
            e.sem_inc(gate, 1)
            e.reg_load(word, control[0:1, 0:1, 0:1])
            with e.Fori(0, NSTEP) as step:
                w = e.snap(word, min_val=0, max_val=2 * NONE)
                with e.If(e.snap(w // 4) == step):
                    flags = e.snap(e.snap(word, min_val=0, max_val=2 * NONE) % 4)
                    slot = e.snap(nu, min_val=0, max_val=NSTEP - 1)
                    if attend:
                        with e.If(flags >= 2):
                            attend(e.snap(na, min_val=0, max_val=NSTEP - 1), step, slot)
                            e.reg_add(na, na, 1)
                    if feed:
                        with e.If(e.snap(flags % 2) == 1):
                            feed(e.snap(nf, min_val=0, max_val=NSTEP - 1), step, slot)
                            e.reg_add(nf, nf, 1)
                    e.reg_add(nu, nu, 1)
                    now = e.snap(nu, min_val=1, max_val=NSTEP)
                    if after:
                        after(now)
                    e.wait_ge(control_ready, now + 1)
                    e.sem_inc(gate, 1)
                    e.reg_load(word, control[0:1, bass.ds(now, 1), 0:1])

        def pe_attention(pe, s, base, ngroups, y_of):
            n = GRP * ngroups
            bu, bg = base(n), base(ngroups)

            def score(u):
                g, lane, qt = u // GRP, u % 2, (u % GRP) // 2
                if u >= 2:
                    pe.wait_ge(s["exped"], bu + (u - 1))
                rows = slice(64 * lane, 64 * lane + 64)
                q0 = (g * QT + qt) * P
                k0 = (g // 2) * TOK
                for j in range(NB):
                    mm = pe.matmul(scores2[u % 2][:, j * BLK:(j + 1) * BLK], qT[rows, q0:q0 + P],
                                   kT[rows, k0 + j * BLK:k0 + (j + 1) * BLK], start=True, stop=True)
                mm.then_inc(s["scored"], 1)

            def turn(u):
                pe.wait_ge(s["scaled"], bu + (u + 1))
                for half, bank, filled, drained in ((0, LO, "lo_turned", "lo_drained"),
                                                    (1, HI, "hi_turned", "hi_drained")):
                    if u >= 1:
                        pe.wait_ge(s[drained], bu + u)
                    for k in range(4):
                        kt = 4 * half + k
                        tr = pe.transpose(bank[:, k * P:(k + 1) * P],
                                          prob[:, u % 3, kt * P:(kt + 1) * P], ident[:, :])
                    tr.then_inc(s[filled], 1)

            def values(g, k):
                if k == 0:
                    pe.wait_ge(s["lo_drained"], bu + GRP * (g + 1))
                    pe.wait_ge(s["hi_drained"], bu + GRP * (g + 1))
                    if g >= 1:
                        pe.wait_ge(s["out_drained"], bg + g)
                for lane in range(2):
                    cols = slice(64 * lane, 64 * lane + 64)
                    mm = pe.matmul(OB[64 * lane:64 * lane + 64, :], V[:, (g // 2) * NT + k, cols],
                                   PT[:, g % 2, lane, k, :], start=(k == 0), stop=(k == NT - 1))
                if k == NT - 1:
                    mm.then_inc(s["out_summed"], 1)

            score(0)
            score(1)
            for i in range(n + LAG_Y + 3):
                if i + 2 < n:
                    score(i + 2)
                if 1 <= i <= n:
                    turn(i - 1)
                for g in range(ngroups):
                    k = i - GRP * g - LAG_PV
                    if 0 <= k < NT - 1:
                        values(g, k)
                    if k == NT - 2:
                        values(g, NT - 1)
                    if i == GRP * g + LAG_Y:
                        pe.wait_ge(s["out_drained"], bg + (g + 1))
                        y_of(g, bg)

        @block.tensor
        def _(pe):
            pe.wait_ge(w_loaded, WLOADS)
            pe.wait_ge(consts_made, 1)
            for j in range(WW):
                bank, slot = j // 9, j % 9
                mm = pe.matmul(PS[:, bank, slot * NH0 * REL:(slot + 1) * NH0 * REL],
                               shift[:, :, :].rearrange("c a m -> c (a m)")[:, WW - 1 - j:WW - 1 - j + P], rpbT[:, :], start=True, stop=True)
            mm.then_inc(bias_expanded, 1)
            pe.wait_ge(ident_made, 1)
            pe.wait_ge(bias_masked, 1)

            with pe.Fori(0, B) as img:
                blo, bhi, bmid, by = (pe.snap(img * N0[k]) for k in ("lo", "hi", "mid", "y"))
                bun = pe.snap(img * UN0)
                bnt = pe.snap(img * NT)
                bln = pe.snap(img * 3)
                cnt = dict(lo=0, hi=0, mid=0, y=0)
                bases = dict(lo=blo, hi=bhi, mid=bmid, y=by)

                def fill(which, mms):
                    n = cnt[which]
                    if n:
                        pe.wait_ge(r0[which + "_drained"], bases[which] + n)
                        pe.sem_inc(gate, 1)
                    mms().then_inc(r0[which + "_filled"], 1)
                    cnt[which] = n + 1

                def turn_norm(n):
                    pe.wait_ge(normed, bln + n)
                    pe.sem_inc(gate, 1)
                    for blk, (which, bank) in enumerate((("lo", LO), ("hi", HI))):
                        def tr():
                            for j in range(QT):
                                m = pe.transpose(bank[0:C, j * P:(j + 1) * P], xn[:, blk * QT + j, :], ident[:, :])
                            return m
                        fill(which, tr)

                turn_norm(1)
                for w in (wq0, wk0):
                    for blk, (which, bank) in enumerate((("lo", LO), ("hi", HI))):
                        if w is wq0:
                            pe.wait_ge(r0[which + "_drained"], bases[which] + 1)
                            pe.sem_inc(gate, 1)
                        fill(which, lambda: pe.matmul(bank, w[:, :, :].rearrange("c h d -> c (h d)"),
                                                      xT[:, blk * BLK:(blk + 1) * BLK], start=True, stop=True))

                def value_tiles(tiles):
                    def go():
                        for n, j in enumerate(tiles):
                            t0, k = VTILES[j]
                            m = pe.matmul(HI[0:k, n * C:(n + 1) * C], xT[:, t0:t0 + k], wv0[:, :],
                                          start=True, stop=True)
                        return m
                    return go
                fill("hi", value_tiles(range(NT)))
                fill("hi", value_tiles(range(NT, NT + 2)))
                pe.wait_ge(r0["lo_drained"], blo + cnt["lo"])
                pe.wait_ge(r0["hi_drained"], bhi + cnt["hi"])
                pe.wait_ge(tables_made, 3)
                pe.sem_inc(gate, 1)

                def score(u):
                    t, h = u // NH0, u % NH0
                    first, rows, kind = window_keys(t)
                    if u >= 4:
                        pe.wait_ge(c0["exped"], bun + (u - 3))
                    bank = PS[:, u % 4, 0:rows * WW]
                    hr = slice(32 * h, 32 * h + 32)
                    pe.matmul(bank, qT0[hr, t * P:(t + 1) * P], kT0[hr, first * WW:(first + rows) * WW],
                              start=True, stop=False)
                    pe.matmul(bank, ident[:, :], tabs[kind][:, h, :, :].rearrange("p a b -> p (a b)"),
                              start=False, stop=True).then_inc(c0["scored"], 1)

                def turn(u):
                    t = u // NH0
                    pe.wait_ge(c0["scaled"], bun + (u + 1))
                    half = ("lo", "hi")[u % 2]
                    bank = (LO, HI)[u % 2]
                    if u >= 2:
                        pe.wait_ge(c0[half + "_drained"], base_half + u // 2)
                    for n, (_, k, _) in enumerate(key_chunks(t)):
                        tr = pe.transpose(bank[0:k, n * P:(n + 1) * P], prob[:, u % 3, n * P:n * P + k], ident[:, :])
                    tr.then_inc(c0[half + "_turned"], 1)

                def values(u):
                    t, h = u // NH0, u % NH0
                    half = ("lo", "hi")[u % 2]
                    pe.wait_ge(c0[half + "_drained"], base_half + (u // 2 + 1))
                    if h == 0 and t >= 1:
                        pe.wait_ge(c0["out_drained"], bnt + t)
                    chunks = key_chunks(t)
                    for n, (_, k, slot) in enumerate(chunks):
                        mm = pe.matmul(OB[32 * h:32 * h + 32, 0:P], V0[0:k, slot, h, :], PT0[0:k, u % 4, n, :],
                                       start=(n == 0), stop=(n == len(chunks) - 1))
                    if h == NH0 - 1:
                        mm.then_inc(c0["out_summed"], 1)

                base_half = pe.snap(img * (UN0 // 2))
                score(0)
                score(1)
                for i in range(UN0 + 7):
                    if i + 2 < UN0:
                        score(i + 2)
                    if 1 <= i <= UN0:
                        turn(i - 1)
                    if 3 <= i < UN0 + 3:
                        values(i - 3)
                    if i >= 9 and (i - 9) % NH0 == 0:
                        t = (i - 9) // NH0
                        pe.wait_ge(c0["out_drained"], bnt + (t + 1))
                        mm = pe.matmul(YB[:, t * C:(t + 1) * C], OT0[:, t % 2, :], pw0[:, :], start=True, stop=True)
                        if t == NT - 1:
                            mm.then_inc(r0["y_filled"], 1)
                cnt["y"] = 1

                turn_norm(2)
                pe.wait_ge(r0["lo_drained"], blo + cnt["lo"])
                pe.wait_ge(r0["hi_drained"], bhi + cnt["hi"])
                pe.sem_inc(gate, 1)
                for blk in range(NB):
                    for half, (which, bank) in enumerate((("lo", LO), ("mid", OB))):
                        fill(which, lambda: pe.matmul(bank, fc1[:, half * P:(half + 1) * P],
                                                      xT[:, blk * BLK:(blk + 1) * BLK], start=True, stop=True))
                pe.wait_ge(r0["lo_drained"], blo + cnt["lo"])
                pe.wait_ge(r0["mid_drained"], bmid + cnt["mid"])
                pe.wait_ge(r0["y_drained"], by + 1)
                for t in range(NT):
                    for half in range(2):
                        mm = pe.matmul(YB[:, t * C:(t + 1) * C], G0[:, half, t * P:(t + 1) * P], fc2[:, half, :],
                                       start=(half == 0), stop=(half == 1))
                mm.then_inc(r0["y_filled"], 1)
                turn_norm(3)
                pe.wait_ge(r0["lo_drained"], blo + cnt["lo"])
                pe.wait_ge(r0["hi_drained"], bhi + cnt["hi"])
                pe.sem_inc(gate, 1)
                assert cnt["lo"] == N0["lo"] and cnt["hi"] == N0["hi"] and cnt["mid"] == N0["mid"]

            with pe.Fori(0, NPAIR) as pair:
                base = lambda k: pe.snap(pair * k)
                blo, bhi = base(N1["lo"]), base(N1["hi"])
                cnt = [0, 0]
                pe.wait_ge(pair_loaded, base(64) + 64)
                pe.sem_inc(gate, 1)

                def piece(mms):
                    side = sum(cnt) % 2
                    which, bank, bs = (("lo", LO, blo), ("hi", HI, bhi))[side]
                    if cnt[side]:
                        pe.wait_ge(r1[which + "_drained"], bs + cnt[side])
                        pe.sem_inc(gate, 1)
                    mms(bank).then_inc(r1[which + "_filled"], 1)
                    cnt[side] += 1

                for w in (wq1, wk1):
                    for blk in range(B * NB):
                        piece(lambda bank: pe.matmul(bank, w[:, :], aT[:, blk * BLK:(blk + 1) * BLK],
                                                     start=True, stop=True))
                for blk in range(B * NB):
                    def go(bank):
                        for j in range(QT):
                            t = blk * QT + j
                            m = pe.matmul(bank[:, j * P:(j + 1) * P], aT[:, t * P:(t + 1) * P], wv1[:, :],
                                          start=True, stop=True)
                        return m
                    piece(go)
                pe.wait_ge(r1["lo_drained"], blo + N1["lo"])
                pe.wait_ge(r1["hi_drained"], bhi + N1["hi"])
                pe.sem_inc(gate, 1)

                def y_of(g, bg):
                    if g >= 1:
                        pe.wait_ge(c1["y_drained"], bg + g)
                    for j in range(QT):
                        mm = pe.matmul(YB[:, j * C:(j + 1) * C], OT[:, g % 2, j * P:(j + 1) * P], wu[:, :],
                                       start=True, stop=True)
                    mm.then_inc(c1["y_filled"], 1)

                pe_attention(pe, c1, base, 2 * B, y_of)
                pe.wait_ge(c1["y_drained"], base(2 * B) + 2 * B)
                pe.sem_inc(pair_used, 1)

            pe.wait_ge(normed3, 1)
            for blk in range(B * NB):
                if blk % NB == 0 and blk:
                    pe.wait_ge(normed3, 1 + blk // NB)
                which, bank = (("lo", LO), ("hi", HI))[blk % 2]
                if blk >= 2:
                    pe.wait_ge(r3[which + "_drained"], blk // 2)
                for j in range(QT):
                    m = pe.transpose(bank[0:C, j * P:(j + 1) * P], xn[:, (blk % NB) * QT + j, :], ident[:, :])
                m.then_inc(r3[which + "_filled"], 1)
            pe.wait_ge(r3["lo_drained"], 2)
            pe.wait_ge(r3["hi_drained"], 2)

            def show_row():
                pe.transpose(YB[0:1, 0:C], aT[:, 0:1], ident[0:C, 0:C]).then_inc(row_turned, 1)
            show_row()

            def attend(na, step, slot):
                base = lambda k: pe.snap(na * k)
                blo, bhi, by = base(N2["lo"]), base(N2["hi"]), base(N2["y"])
                pe.wait_ge(attn_loaded, base(80) + 80)
                pe.sem_inc(gate, 1)
                for n, w in enumerate((wqs, wks)):
                    for side, (which, bank, bs) in enumerate((("lo", LO, blo), ("hi", HI, bhi))):
                        if n:
                            pe.wait_ge(r2[which + "_drained"], bs + n)
                            pe.sem_inc(gate, 1)
                        for lane in range(2):
                            m = pe.matmul(bank[64 * lane:64 * lane + 64, :], w[:, :],
                                          aT[:, lane * TOK + side * BLK:lane * TOK + (side + 1) * BLK],
                                          start=True, stop=True)
                        m.then_inc(r2[which + "_filled"], 1)
                for side, (which, bank, bs) in enumerate((("lo", LO, blo), ("hi", HI, bhi))):
                    pe.wait_ge(r2[which + "_drained"], bs + 2)
                    pe.sem_inc(gate, 1)
                    for j in range(QT):
                        for lane in range(2):
                            t0 = lane * TOK + (side * QT + j) * P
                            m = pe.matmul(bank[:, j * P + 64 * lane:j * P + 64 * lane + 64], aT[:, t0:t0 + P],
                                          wvs[:, :], start=True, stop=True)
                    m.then_inc(r2[which + "_filled"], 1)
                pe.wait_ge(r2["lo_drained"], blo + 3)
                pe.wait_ge(r2["hi_drained"], bhi + 3)
                pe.sem_inc(gate, 1)

                def y_of(g, bg):
                    for lane in range(2):
                        n = 2 * g + lane
                        if n:
                            pe.wait_ge(c2["y_drained"], by + n)
                        pe.sem_inc(gate, 1)
                        pe.matmul(YB[0:C, :], wos[64 * lane:64 * lane + 64, :], OT[64 * lane:64 * lane + 64, g % 2, :],
                                  start=True, stop=True).then_inc(c2["y_filled"], 1)

                pe_attention(pe, c2, base, 2, y_of)
                pe.wait_ge(c2["y_drained"], by + 4)
                pe.sem_inc(gate, 1)

            def feed(nf, step, slot):
                base = lambda k: pe.snap(nf * k)
                blo, bhi = base(NF["lo"]), base(NF["hi"])
                pe.wait_ge(ffn_loaded, base(64) + 64)
                pe.sem_inc(gate, 1)
                cnt = [0, 0]

                def piece(mms):
                    side = sum(cnt) % 2
                    which, bank, bs = (("lo", LO, blo), ("hi", HI, bhi))[side]
                    if cnt[side]:
                        pe.wait_ge(rf[which + "_drained"], bs + cnt[side])
                        pe.sem_inc(gate, 1)
                    mms(bank).then_inc(rf[which + "_filled"], 1)
                    cnt[side] += 1
                for blk in range(B * NB):
                    for half in range(2):
                        piece(lambda bank: pe.matmul(bank, w1s[:, half * P:(half + 1) * P],
                                                     aT[:, blk * BLK:(blk + 1) * BLK], start=True, stop=True))
                pe.wait_ge(rf["lo_drained"], blo + cnt[0])
                pe.wait_ge(rf["hi_drained"], bhi + cnt[1])
                pe.sem_inc(gate, 1)
                for blk in range(B * NB):
                    def go(bank):
                        for half in range(2):
                            m = pe.matmul(bank[0:C, :], w2s[:, half, :], Z[:, half, blk * BLK:(blk + 1) * BLK],
                                          start=(half == 0), stop=(half == 1))
                        return m
                    piece(go)
                pe.wait_ge(rf["lo_drained"], blo + NF["lo"])
                pe.wait_ge(rf["hi_drained"], bhi + NF["hi"])
                pe.sem_inc(gate, 1)

            scan(pe, attend, feed, lambda now: show_row())

            for blk in range(B * NB):
                which, bank = (("lo", LO), ("hi", HI))[blk % 2]
                if blk >= 2:
                    pe.wait_ge(re[which + "_drained"], blk // 2)
                for j in range(QT):
                    t = blk * QT + j
                    m = pe.transpose(bank[:, j * C:(j + 1) * C], aT[:, t * P:(t + 1) * P], ident[0:C, 0:C])
                m.then_inc(re[which + "_filled"], 1)

        def act_attention(act, s, base, ngroups):
            n = GRP * ngroups
            bu, bg = base(n), base(ngroups)
            for i in range(n + LAG_OUT + 3):
                if i < n:
                    act.wait_ge(s["maxed"], bu + (i + 1))
                    if i >= 3:
                        act.wait_ge(s["hi_turned"], bu + (i - 2))
                    act.activation(prob[:, i % 3, :], scores2[i % 2], ACT.Exp, bias=negm[:, i % 4:i % 4 + 1],
                                   scale=1.0, accum_out=rsum[:, i % 4:i % 4 + 1]).then_inc(s["exped"], 1)
                u = i - 2
                if 0 <= u < n:
                    g, lane, qt = u // GRP, u % 2, (u % GRP) // 2
                    act.wait_ge(s["lo_turned"], bu + (u + 1))
                    act.activation(PT[:, g % 2, lane, 0:4, qt * P:(qt + 1) * P],
                                   LO.rearrange("p (k q) -> p k q", k=4), ACT.Copy).then_inc(s["lo_drained"], 1)
                for g in range(ngroups):
                    if i == GRP * g + LAG_OUT:
                        act.wait_ge(s["out_summed"], bg + (g + 1))
                        act.activation(OT[:, g % 2, :], OB, ACT.Copy).then_inc(s["out_drained"], 1)

        @block.scalar
        def _(act):
            act.dma_start(norm[:, 0:1], a["L0_conv_norm1_g"].rearrange("(c o) -> c o", o=1)).then_inc(w_loaded, 16)
            act.dma_start(norm[:, 1:2], a["L0_conv_norm1_b"].rearrange("(c o) -> c o", o=1)).then_inc(w_loaded, 16)
            act.dma_start(norm[:, 2:3], a["L0_conv_norm2_g"].rearrange("(c o) -> c o", o=1)).then_inc(w_loaded, 16)
            act.dma_start(norm[:, 3:4], a["L0_conv_norm2_b"].rearrange("(c o) -> c o", o=1)).then_inc(w_loaded, 16)
            act.dma_start(fb1[:, :], a["L0_conv_fc1_b"].rearrange("(h p) -> p h", p=P),
                          allow_slow_non_contiguous=True).then_inc(w_loaded, 16)
            qb = a["L0_conv_qkv_b"]
            for n, dst in enumerate((bq0, bk0)):
                for h in range(NH0):
                    src = qb[n * C + h * HD0:n * C + (h + 1) * HD0].rearrange("(c o) -> c o", o=1)
                    if n == 0 and h == 0:
                        act.wait_ge(zeroed, 1)
                    act.dma_start(dst[32 * h:32 * h + HD0, :], src).then_inc(w_loaded, 16)
            act.wait_ge(w_loaded, WLOADS)
            act.activation(bq0s[:, :], bq0[:, :], ACT.Copy, scale=HD0 ** -0.5).then_inc(bq_scaled, 1)
            act.wait_ge(bq_scaled, 1)

            with act.Fori(0, B) as img:
                blo, bmid, bun, bnt = (act.snap(img * k) for k in (N0["lo"], N0["mid"], UN0, NT))
                bhalf = act.snap(img * (UN0 // 2))
                cnt = dict(lo=0, mid=0)

                def drain(which, out, func, **kw):
                    cnt[which] += 1
                    act.wait_ge(r0[which + "_filled"], (blo if which == "lo" else bmid) + cnt[which])
                    bank = LO if which == "lo" else OB
                    src = bank if out.shape[0] == P else bank[0:out.shape[0], :]
                    act.activation(out, src, func, **kw).then_inc(r0[which + "_drained"], 1)

                drain("lo", xT[:, 0:BLK], ACT.Identity, scale=norm[:, 0:1], bias=norm[:, 1:2])
                drain("lo", qT0[:, 0:BLK], ACT.Identity, scale=HD0 ** -0.5, bias=bq0s[:, 0:1])
                drain("lo", kT0[:, 0:BLK], ACT.Identity, scale=1.0, bias=bk0[:, 0:1])

                for i in range(UN0 + 8):
                    if i < UN0:
                        w = window_keys(i // NH0)[1] * WW
                        act.wait_ge(c0["maxed"], bun + (i + 1))
                        if i >= 3:
                            j = i - 3
                            act.wait_ge(c0[("lo", "hi")[j % 2] + "_turned"], bhalf + (j // 2 + 1))
                        act.activation(prob[:, i % 3, 0:w], PS[:, i % 4, 0:w], ACT.Exp,
                                       bias=negm[:, i % 4:i % 4 + 1], scale=1.0,
                                       accum_out=rsum[:, i % 4:i % 4 + 1]).then_inc(c0["exped"], 1)
                    u = i - 2
                    if 0 <= u < UN0 and u % 2 == 0:
                        act.wait_ge(c0["lo_turned"], bhalf + (u // 2 + 1))
                        nat_drain(act.activation, ACT.Copy, LO, u).then_inc(c0["lo_drained"], 1)
                    if i >= 7 and (i - 7) % NH0 == 0 and (i - 7) // NH0 < NT:
                        t = (i - 7) // NH0
                        act.wait_ge(c0["out_summed"], bnt + (t + 1))
                        act.activation(OT0[:, t % 2, :], OB[:, 0:P], ACT.Copy).then_inc(c0["out_drained"], 1)

                drain("lo", xT[:, 0:BLK], ACT.Identity, scale=norm[:, 2:3], bias=norm[:, 3:4])
                for blk in range(NB):
                    for half, which in enumerate(("lo", "mid")):
                        drain(which, G0[:, half, blk * BLK:(blk + 1) * BLK], ACT.Gelu, bias=fb1[:, half:half + 1],
                              scale=1.0)
                drain("lo", aT[:, bass.ds(img * TOK, BLK)], ACT.Copy)
                assert cnt["lo"] == N0["lo"] and cnt["mid"] == N0["mid"]

            with act.Fori(0, NPAIR) as pair:
                base = lambda k: act.snap(pair * k)
                blo = base(N1["lo"])
                n = 0
                for dst in (qT, kT):
                    for blk in (0, 2):
                        n += 1
                        act.wait_ge(r1["lo_filled"], blo + n)
                        act.activation(dst[:, blk * BLK:(blk + 1) * BLK], LO, ACT.Copy,
                                       scale=C ** -0.25).then_inc(r1["lo_drained"], 1)
                for blk in (0, 2):
                    n += 1
                    act.wait_ge(r1["lo_filled"], blo + n)
                    act.activation(V[:, blk * QT:(blk + 1) * QT, :], LO.rearrange("p (t c) -> p t c", t=QT),
                                   ACT.Copy).then_inc(r1["lo_drained"], 1)
                act_attention(act, c1, base, 2 * B)

            for n in range(2):
                act.wait_ge(r3["lo_filled"], n + 1)
                act.activation(aT[:, 2 * n * BLK:(2 * n + 1) * BLK], LO[0:C, :], ACT.Copy).then_inc(r3["lo_drained"], 1)

            def attend(na, step, slot):
                base = lambda k: act.snap(na * k)
                blo = base(N2["lo"])
                for n, (dst, sc) in enumerate(((qT, C ** -0.5), (kT, 1.0))):
                    act.wait_ge(r2["lo_filled"], blo + (n + 1))
                    act.activation(dst[:, 0:BLK], LO, ACT.Copy, scale=sc).then_inc(r2["lo_drained"], 1)
                act.wait_ge(r2["lo_filled"], blo + 3)
                act.activation(V[:, 0:QT, :], LO.rearrange("p (t c) -> p t c", t=QT), ACT.Copy)\
                   .then_inc(r2["lo_drained"], 1)
                act_attention(act, c2, base, 2)

            def feed(nf, step, slot):
                blo = act.snap(nf * NF["lo"])
                act.wait_ge(ffn_loaded, act.snap(nf * 64) + 64)
                n = 0
                for blk in range(B * NB):
                    n += 1
                    act.wait_ge(rf["lo_filled"], blo + n)
                    act.activation(Z[:, 0, blk * BLK:(blk + 1) * BLK], LO, ACT.Relu, bias=b1s[:, 0:1], scale=1.0)\
                       .then_inc(rf["lo_drained"], 1)
                for blk in (0, 2):
                    n += 1
                    act.wait_ge(rf["lo_filled"], blo + n)
                    act.activation(aT[:, blk * BLK:(blk + 1) * BLK], LO[0:C, :], ACT.Identity, bias=b2s[:, 0:1],
                                   scale=1.0).then_inc(rf["lo_drained"], 1)

            scan(act, attend, feed, None)

        @block.gpsimd
        def _(pool):
            chain = [0]

            def link(ins):
                chain[0] += 1
                ins.then_inc(pool_chain, 1)
                pool.wait_ge(pool_chain, chain[0])

            pool.memset(wq0[:, :, :], 0.0)
            pool.memset(wk0[:, :, :], 0.0)
            pool.memset(bq0[:, :], 0.0)
            pool.memset(bk0[:, :], 0.0)
            link(pool.memset(pw0[:, :], 0.0))
            pool.sem_inc(zeroed, 1)
            link(pool.memset(shift[:, :, :], 0.0))
            for base in (-(WW - 1 + WIN - 1), 1 - (WIN - 1)):
                link(pool.affine_select(out=shift[:, :, :], in_=shift[:, :, :], compare_op=ALU.not_equal, fill=1.0,
                                        base=base, pattern=[[0, ROWS + 1], [1, WW]], channel_multiplier=1))
            pool.memset(V0[:, :, :, :], 0.0)
            link(pool.memset(colmask[:, :], 0.0))
            for g in range(ROWS):
                part = colmask[WW * g:WW * (g + 1), :]
                lo = part[:, 0:WW - WIN]
                link(pool.affine_select(out=lo, in_=lo, compare_op=ALU.is_ge, fill=NEG, base=WIN // 2,
                                        pattern=[[1, WW - WIN]], channel_multiplier=-1))
                hi = part[:, WIN:WW]
                link(pool.affine_select(out=hi, in_=hi, compare_op=ALU.is_ge, fill=NEG, base=WIN // 2 - WIN,
                                        pattern=[[-1, WW - WIN]], channel_multiplier=1))
            link(pool.memset(minus_half[:, :], -0.5))
            pool.sem_inc(consts_made, 1)
            link(pool.memset(ident[:, :], 0.0))
            link(pool.affine_select(out=ident[:, :], in_=ident[:, :], compare_op=ALU.not_equal, fill=1.0, base=0,
                                    pattern=[[-1, P]], channel_multiplier=1))
            pool.sem_inc(ident_made, 1)
            link(pool.iota(count_i[:, :], [[1, NSTEP]], base=0, channel_multiplier=0))
            link(pool.tensor_copy(steps4[:, :], count_i[:, :]))
            link(pool.tensor_copy(opnum[:, :], count_i[:, 0:NOPS]))
            link(pool.tensor_scalar(steps4[:, :], steps4[:, :], 4.0, None, ALU.mult))
            pool.sem_inc(consts_made, 1)
            link(pool.memset(tabs[1][:, :, :, :], NEG))
            pool.wait_ge(bias_masked, 1)
            toff = tall[:, :, :].rearrange("p (h r) c -> p h r c", h=NH0)
            for kind, t in ((0, 0), (1, 1), (2, NT - 1)):
                first = window_keys(t)[0]
                for di in range(ROWS):
                    i = ROWS * t + di
                    start = min(max(i - WIN // 2, 0), HH - WIN)
                    r = start - i + WIN - 1
                    part = slice(WW * di, WW * (di + 1))
                    link(pool.tensor_copy(tabs[kind][part, :, start - first:start - first + WIN, :],
                                          toff[part, :, r:r + WIN, :]))
                pool.sem_inc(tables_made, 1)

            def scale_units(s, bu, n, width):
                for u in range(n):
                    pool.wait_ge(s["inverted"], bu + (u + 1))
                    pool.sem_inc(gate, 1)
                    w = width(u)
                    pool.tensor_scalar(prob[:, u % 3, 0:w], prob[:, u % 3, 0:w], rinv[:, u % 4:u % 4 + 1], None,
                                       ALU.mult).then_inc(s["scaled"], 1)

            def power(chain, links):
                pool.wait_ge(chain, links)
                pool.sem_inc(gate, 1)
                pool.tensor_tensor(rstd[:, :], var[:, :], minus_half[:, :], ALU.pow).then_inc(rstd_made, 1)

            with pool.Fori(0, B) as img:
                bln = pool.snap(img * (3 * LN))
                power(ln0, bln + LN)
                scale_units(c0, pool.snap(img * UN0), UN0, lambda u: window_keys(u // NH0)[1] * WW)
                power(ln0, bln + 2 * LN)
                power(ln0, bln + 3 * LN)
            with pool.Fori(0, NPAIR) as pair:
                scale_units(c1, pool.snap(pair * (2 * B * GRP)), 2 * B * GRP, lambda u: TOK)
            for img in range(B):
                power(ln3, (img + 1) * LN)
            scan(pool, lambda na, step, slot: scale_units(c2, pool.snap(na * (2 * GRP)), 2 * GRP, lambda u: TOK),
                 None, None)

        def dve_attention(dve, s, base, ngroups, y_out):
            n = GRP * ngroups
            bu, bg = base(n), base(ngroups)
            for i in range(n + LAG_YD + 2):
                if i < n:
                    dve.wait_ge(s["scored"], bu + (i + 1))
                    dve.tensor_reduce(negm[:, i % 4:i % 4 + 1], scores2[i % 2], AX.X, ALU.max, negate=True)\
                       .then_inc(s["maxed"], 1)
                if 1 <= i <= n:
                    u = i - 1
                    dve.wait_ge(s["exped"], bu + (u + 1))
                    dve.reciprocal(rinv[:, u % 4:u % 4 + 1], rsum[:, u % 4:u % 4 + 1]).then_inc(s["inverted"], 1)
                u = i - 2
                if 0 <= u < n:
                    g, lane, qt = u // GRP, u % 2, (u % GRP) // 2
                    dve.wait_ge(s["hi_turned"], bu + (u + 1))
                    dve.tensor_copy(PT[:, g % 2, lane, 4:8, qt * P:(qt + 1) * P],
                                    HI.rearrange("p (k q) -> p k q", k=4)).then_inc(s["hi_drained"], 1)
                for g in range(ngroups):
                    if i == GRP * g + LAG_YD:
                        y_out(g, bg)

        @block.vector
        def _(dve):
            dve.wait_ge(bias_expanded, 1)
            dve.wait_ge(consts_made, 1)
            n = NH0 * REL
            for bank in range(4):
                j0, k = 9 * bank, min(9, WW - 9 * bank)
                last = dve.tensor_tensor(tall[:, :, j0:j0 + k].rearrange("p n j -> p j n"),
                                         PS[:, bank, 0:k * n].rearrange("p (j n) -> p j n", n=n),
                                         colmask[:, j0:j0 + k].rearrange("p (j o) -> p j o", o=1).to_broadcast([P, k, n]),
                                         ALU.add)
            last.then_inc(bias_masked, 1)

            def bc(v, k=NT):
                return v.rearrange("p (t o) -> p t o", o=1).to_broadcast([P, k, C])

            def rows(v, k=NT):
                return v.rearrange("p (o c) -> p o c", o=1).to_broadcast([P, k, C])

            def layernorm(x, chain, base, n0, powers, done):
                n = [n0]

                def link(ins):
                    n[0] += 1
                    ins.then_inc(chain, 1)
                    dve.wait_ge(chain, base + n[0])
                link(dve.tensor_reduce(mean[:, :], x, AX.X, ALU.add))
                link(dve.tensor_scalar(mean[:, :], mean[:, :], 1.0 / C, None, ALU.mult))
                link(dve.tensor_tensor(xn[:, :, :], x, bc(mean[:, :]), ALU.subtract))
                link(dve.tensor_tensor(xsq[:, :, :], xn[:, :, :], xn[:, :, :], ALU.mult))
                link(dve.tensor_reduce(var[:, :], xsq[:, :, :], AX.X, ALU.add))
                link(dve.tensor_scalar(var[:, :], var[:, :], 1.0 / C, EPS, ALU.mult, ALU.add))
                dve.wait_ge(rstd_made, powers)
                dve.tensor_tensor(xn[:, :, :], xn[:, :, :], bc(rstd[:, :]), ALU.mult).then_inc(done, 1)
                return n[0]

            dve.wait_ge(x_loaded, 16)
            dve.wait_ge(w_loaded, WLOADS)
            with dve.Fori(0, B) as img:
                bln, bhi, by, bun, bnt = (dve.snap(img * k) for k in (3 * LN, N0["hi"], N0["y"], UN0, NT))
                bhalf = dve.snap(img * (UN0 // 2))
                bb = dve.snap(img * 4)
                brs = dve.snap(img * 3)
                cnt = [0]

                def filled():
                    cnt[0] += 1
                    dve.wait_ge(r0["hi_filled"], bhi + cnt[0])

                xin = xall[:, bass.ds(img * NT, NT), :]
                layernorm(xin, ln0, bln, 0, brs + 1, normed)
                filled()
                dve.tensor_scalar(xT[:, BLK:TOK], HI[0:C, :], norm[:, 0:1], norm[:, 1:2], ALU.mult, ALU.add)\
                   .then_inc(r0["hi_drained"], 1)
                dve.tensor_tensor(xb[:, :, :], xin, rows(pb0[:, :]), ALU.add).then_inc(biased, 1)
                filled()
                dve.tensor_scalar(qT0[:, BLK:TOK], HI, bq0[:, 0:1], HD0 ** -0.5, ALU.add, ALU.mult)\
                   .then_inc(r0["hi_drained"], 1)
                filled()
                dve.tensor_scalar(kT0[:, BLK:TOK], HI, bk0[:, 0:1], None, ALU.add).then_inc(r0["hi_drained"], 1)
                for tiles in (range(NT), range(NT, NT + 2)):
                    filled()
                    t0, full, k = tiles[0], len(tiles) - 1, VTILES[tiles[-1]][1]
                    for p, lo, hi in ((P, 0, full), (k, full, full + 1)):
                        for t in range(lo, hi):
                            d = dve.tensor_tensor(V0[0:p, t0 + t, :, 0:HD0],
                                                  HI[0:p, t * C:(t + 1) * C].rearrange("p (h d) -> p h d", h=NH0),
                                                  bv0[0:p, :].rearrange("p (h d) -> p h d", h=NH0), ALU.add)
                    d.then_inc(r0["hi_drained"], 1)

                for i in range(UN0 + 8):
                    if i < UN0:
                        w = window_keys(i // NH0)[1] * WW
                        dve.wait_ge(c0["scored"], bun + (i + 1))
                        dve.tensor_reduce(negm[:, i % 4:i % 4 + 1], PS[:, i % 4, 0:w], AX.X, ALU.max, negate=True)\
                           .then_inc(c0["maxed"], 1)
                    if 1 <= i <= UN0:
                        u = i - 1
                        dve.wait_ge(c0["exped"], bun + (u + 1))
                        dve.reciprocal(rinv[:, u % 4:u % 4 + 1], rsum[:, u % 4:u % 4 + 1])\
                           .then_inc(c0["inverted"], 1)
                    u = i - 2
                    if 0 <= u < UN0 and u % 2 == 1:
                        dve.wait_ge(c0["hi_turned"], bhalf + (u // 2 + 1))
                        nat_drain(dve.tensor_copy, None, HI, u).then_inc(c0["hi_drained"], 1)

                dve.wait_ge(r0["y_filled"], by + 1)
                dve.wait_ge(biased, bb + 1)
                dve.tensor_tensor(x1[:, :, :], xb[:, :, :], YB.rearrange("p (t c) -> p t c", t=NT), ALU.add)\
                   .then_inc(r0["y_drained"], 1)
                dve.wait_ge(r0["y_drained"], by + 1)
                layernorm(x1[:, :, :], ln0, bln, LN, brs + 2, normed)
                dve.tensor_tensor(xb[:, :, :], x1[:, :, :], rows(fb2[:, :]), ALU.add).then_inc(biased, 1)
                filled()
                dve.tensor_scalar(xT[:, BLK:TOK], HI[0:C, :], norm[:, 2:3], norm[:, 3:4], ALU.mult, ALU.add)\
                   .then_inc(r0["hi_drained"], 1)
                dve.wait_ge(r0["y_filled"], by + 2)
                dve.wait_ge(biased, bb + 2)
                dve.tensor_tensor(x1[:, :, :], xb[:, :, :], YB.rearrange("p (t c) -> p t c", t=NT), ALU.add)\
                   .then_inc(r0["y_drained"], 1)
                dve.wait_ge(r0["y_drained"], by + 2)
                layernorm(x1[:, :, :], ln0, bln, 2 * LN, brs + 3, normed)
                dve.tensor_tensor(x2[:, bass.ds(img * NT, NT), :], x1[:, :, :], rows(bu1[:, :]), ALU.add)\
                   .then_inc(biased, 2)
                filled()
                dve.tensor_copy(aT[:, bass.ds(img * TOK + BLK, BLK)], HI[0:C, :]).then_inc(r0["hi_drained"], 1)
                assert cnt[0] == N0["hi"]
            dve.wait_ge(biased, 4 * B)

            with dve.Fori(0, NPAIR) as pair:
                base = lambda k: dve.snap(pair * k)
                bhi = base(N1["hi"])
                n = 0
                for dst in (qT, kT):
                    for blk in (1, 3):
                        n += 1
                        dve.wait_ge(r1["hi_filled"], bhi + n)
                        dve.tensor_scalar(dst[:, blk * BLK:(blk + 1) * BLK], HI, C ** -0.25, None, ALU.mult)\
                           .then_inc(r1["hi_drained"], 1)
                for blk in (1, 3):
                    n += 1
                    dve.wait_ge(r1["hi_filled"], bhi + n)
                    dve.tensor_copy(V[:, blk * QT:(blk + 1) * QT, :], HI.rearrange("p (t c) -> p t c", t=QT))\
                       .then_inc(r1["hi_drained"], 1)

                def y_out(g, bg):
                    dve.wait_ge(c1["y_filled"], bg + (g + 1))
                    part = x2[:, g * QT:(g + 1) * QT, :]
                    dve.tensor_tensor(part, part, YB[:, 0:QT * C].rearrange("p (t c) -> p t c", t=QT), ALU.add)\
                       .then_inc(c1["y_drained"], 1)
                dve_attention(dve, c1, base, 2 * B, y_out)

            dve.wait_ge(c1["y_drained"], NPAIR * 2 * B)
            for img in range(B):
                if img:
                    dve.wait_ge(r3["hi_filled"], 1)
                layernorm(x2[:, img * NT:(img + 1) * NT, :], ln3, 0, img * LN, 3 * B + img + 1, normed3)
                dve.wait_ge(r3["hi_filled"], img + 1)
                dve.tensor_copy(aT[:, (2 * img + 1) * BLK:(2 * img + 2) * BLK], HI[0:C, :])\
                   .then_inc(r3["hi_drained"], 1)

            cn = [0]

            def link(ins):
                cn[0] += 1
                ins.then_inc(codes_made, 1)
                dve.wait_ge(codes_made, cn[0])
            dve.wait_ge(late_loaded, 32)
            dve.wait_ge(consts_made, 2)
            link(dve.tensor_copy(codes[:, :, :], mask8[:, 0, :, :]))
            link(dve.tensor_copy(codew[:, :, :], mask8[:, 1, :, :]))
            link(dve.scalar_tensor_tensor(codes[:, :, :], codes[:, :, :], 2.0, codew[:, :, :], ALU.mult, ALU.add))
            link(dve.memset(nextf[:, :], -4.0))

            def choose(now):
                base = now * NCTL
                n = [0]

                def link(ins):
                    n[0] += 1
                    ins.then_inc(ctl_chain, 1)
                    dve.wait_ge(ctl_chain, base + n[0])
                dve.wait_ge(row_turned, now + 1)
                link(dve.tensor_copy(row[:, :], YB[0:1, 0:C]))
                link(dve.tensor_reduce(top[:, :], row[:, 0:NOPS], AX.X, ALU.max))
                link(dve.tensor_scalar(cand[:, :], row[:, 0:NOPS], top[:, 0:1], 64.0, ALU.is_lt, ALU.mult))
                link(dve.tensor_tensor(cand[:, :], cand[:, :], opnum[:, :], ALU.add))
                link(dve.tensor_reduce(opf[:, :], cand[:, :], AX.X, ALU.min))
                link(dve.tensor_scalar(hit[:, :], opnum[:, :], opf[:, 0:1], None, ALU.is_equal))
                link(dve.tensor_tensor(codew[:, :, :], codes[:, :, :],
                                       hit[:, :].rearrange("p (o n) -> p o n", o=1).to_broadcast([1, NSTEP, NOPS]),
                                       ALU.mult))
                link(dve.tensor_reduce(code[:, :], codew[:, :, :], AX.X, ALU.add))
                link(dve.tensor_scalar(dead[:, :], steps4[:, :], nextf[:, 0:1], float(NONE), ALU.is_le, ALU.mult))
                link(dve.tensor_scalar(key[:, :], code[:, :], 0.0, float(NONE), ALU.is_equal, ALU.mult))
                link(dve.tensor_tensor(key[:, :], key[:, :], dead[:, :], ALU.max))
                link(dve.tensor_tensor(code[:, :], code[:, :], steps4[:, :], ALU.add))
                link(dve.tensor_tensor(key[:, :], key[:, :], code[:, :], ALU.max))
                link(dve.tensor_reduce(nextf[:, :], key[:, :], AX.X, ALU.min))
                assert n[0] == NCTL
                dve.tensor_copy(control[:, bass.ds(now, 1), 1:2], opf[:, :].rearrange("p (a b) -> p a b", a=1))
                dve.tensor_copy(control[:, bass.ds(now, 1), 0:1], nextf[:, :].rearrange("p (a b) -> p a b", a=1))\
                   .then_inc(control_ready, 1)

            choose(0)

            def attend(na, step, slot):
                base = lambda k: dve.snap(na * k)
                bhi, by = base(N2["hi"]), base(N2["y"])
                for n, (dst, sc) in enumerate(((qT, C ** -0.5), (kT, 1.0))):
                    dve.wait_ge(r2["hi_filled"], bhi + (n + 1))
                    dve.tensor_scalar(dst[:, BLK:2 * BLK], HI, sc, None, ALU.mult).then_inc(r2["hi_drained"], 1)
                dve.wait_ge(r2["hi_filled"], bhi + 3)
                dve.tensor_copy(V[:, QT:2 * QT, :], HI.rearrange("p (t c) -> p t c", t=QT))\
                   .then_inc(r2["hi_drained"], 1)

                def y_out(g, bg):
                    for lane in range(2):
                        dve.wait_ge(c2["y_filled"], by + (2 * g + lane + 1))
                        dve.tensor_copy(aT[:, lane * TOK + g * BLK:lane * TOK + (g + 1) * BLK], YB[0:C, :])\
                           .then_inc(c2["y_drained"], 1)
                dve_attention(dve, c2, base, 2, y_out)

            def feed(nf, step, slot):
                bhi = dve.snap(nf * NF["hi"])
                dve.wait_ge(ffn_loaded, dve.snap(nf * 64) + 64)
                n = 0
                for blk in range(B * NB):
                    n += 1
                    dve.wait_ge(rf["hi_filled"], bhi + n)
                    dve.tensor_scalar(Z[:, 1, blk * BLK:(blk + 1) * BLK], HI, b1s[:, 1:2], 0.0, ALU.add, ALU.max)\
                       .then_inc(rf["hi_drained"], 1)
                for blk in (1, 3):
                    n += 1
                    dve.wait_ge(rf["hi_filled"], bhi + n)
                    dve.tensor_scalar(aT[:, blk * BLK:(blk + 1) * BLK], HI[0:C, :], b2s[:, 0:1], None, ALU.add)\
                       .then_inc(rf["hi_drained"], 1)

            scan(dve, attend, feed, choose)

            for blk in range(B * NB):
                which, bank = (("lo", LO), ("hi", HI))[blk % 2]
                dve.wait_ge(re[which + "_filled"], blk // 2 + 1)
                part = x2[:, blk * QT:(blk + 1) * QT, :]
                dve.tensor_tensor(part, part, bank[:, 0:QT * C].rearrange("p (t c) -> p t c", t=QT), ALU.add)\
                   .then_inc(re[which + "_drained"], 1)

        @block.sync
        def _(sp):
            x_tok = a["x"].rearrange("b i j c -> (b i j) c").rearrange("(g p) c -> p g c", p=P)
            sp.dma_start(xall[:, :, :], x_tok).then_inc(x_loaded, 16)
            loads = 0

            def load(dst, src, **kw):
                sp.dma_start(dst, src, **kw).then_inc(w_loaded, 16)

            qkv = a["L0_conv_qkv_w"]
            load(rpbT[:, :], a["L0_conv_rpb"].rearrange("h r c -> c (h r)"), allow_slow_non_contiguous=True)
            load(wv0[:, :], qkv[:, 2 * C:3 * C])
            sp.wait_ge(zeroed, 1)
            for n, dst in enumerate((wq0, wk0)):
                load(dst[:, :, 0:HD0], qkv[:, n * C:(n + 1) * C].rearrange("c (h d) -> c h d", h=NH0))
            for h in range(NH0):
                load(pw0[32 * h:32 * h + HD0, :], a["L0_conv_proj_w"][h * HD0:(h + 1) * HD0, :])
            for dst, src in ((bv0, a["L0_conv_qkv_b"][2 * C:3 * C]), (pb0, a["L0_conv_proj_b"]),
                             (fb2, a["L0_conv_fc2_b"]), (bu1, a["L1_attn_bu"])):
                load(dst[:, :], src.rearrange("(o c) -> o c", o=1).to_broadcast([P, C]))
            load(fc1[:, :], a["L0_conv_fc1_w"])
            load(fc2[:, :, :], a["L0_conv_fc2_w"].rearrange("(h p) c -> p h c", p=P))
            sp.dma_start(mask8[:, 0, :, :], a["L1_ffn_attn_mask"].rearrange("(o s) n -> o s n", o=1)).then_inc(late_loaded, 16)
            sp.dma_start(mask8[:, 1, :, :], a["L1_ffn_ffn_mask"].rearrange("(o s) n -> o s n", o=1)).then_inc(late_loaded, 16)

            with sp.Fori(0, NPAIR) as pair:
                with sp.If(pair >= 1):
                    sp.wait_ge(pair_used, sp.snap(pair, min_val=0, max_val=NPAIR))
                    sp.sem_inc(gate, 1)
                for dst, name in ((wq1, "L1_attn_Wq"), (wk1, "L1_attn_Wk"), (wv1, "L1_attn_Wv")):
                    sp.dma_start(dst[:, :], a[name][:, bass.ds(pair * P, P)]).then_inc(pair_loaded, 16)
                sp.dma_start(wu[:, :], a["L1_attn_Wu"][bass.ds(pair * P, P), :]).then_inc(pair_loaded, 16)

            def of(step, slot):
                n = sp.value_load(control[0:1, bass.ds(slot, 1), 1:2], min_val=0, max_val=NOPS - 1)
                return lambda name: a["L1_ffn_" + name][bass.ds(step, 1), bass.ds(n, 1)]

            def attend(na, step, slot):
                w = of(step, slot)
                for dst, name in ((wqs[:, :], "wq"), (wks[:, :], "wk"), (wvs[:, :], "wv"),
                                  (wos[0:C, :], "wo"), (wos[C:P, :], "wo")):
                    sp.dma_start(dst, w(name).rearrange("s n c d -> (s n c) d")).then_inc(attn_loaded, 16)

            def feed(nf, step, slot):
                w = of(step, slot)
                sp.dma_start(w1s[:, :], w("ffn_w1").rearrange("s n c d -> (s n c) d")).then_inc(ffn_loaded, 16)
                sp.dma_start(w2s[:, :, :], w("ffn_w2").rearrange("s n (h p) c -> p (s n h) c", p=P))\
                  .then_inc(ffn_loaded, 16)
                sp.dma_start(b1s[:, :], w("ffn_b1").rearrange("s n (h p) -> p (s n h)", p=P),
                             allow_slow_non_contiguous=True).then_inc(ffn_loaded, 16)
                sp.dma_start(b2s[:, :], w("ffn_b2").rearrange("s n (c o) -> (s n c) o", o=1)).then_inc(ffn_loaded, 16)
            scan(sp, attend, feed, None)

            out_tok = out.rearrange("b i j c -> (b i j) c").rearrange("(g p) c -> p g c", p=P)
            for blk in range(B * NB):
                which = ("lo", "hi")[blk % 2]
                sp.wait_ge(re[which + "_drained"], blk // 2 + 1)
                sp.dma_start(out_tok[:, blk * QT:(blk + 1) * QT, :], x2[:, blk * QT:(blk + 1) * QT, :])\
                  .then_inc(stored, 16)
            sp.wait_ge(stored, 16 * B * NB)


def kernel(**inputs):
    import numpy as _np
    import concourse.bacc as _bacc
    from concourse import mybir as _mybir
    from concourse.bass_utils import run_bass_kernel_spmd as _run

    nc = _bacc.Bacc("TRN2", target_bir_lowering=False, num_devices=1)
    arrays, args = {}, {}
    for name in inputs:
        v = _np.ascontiguousarray(inputs[name])
        arrays[f"in_{name}_dram"] = v
        args[name] = nc.dram_tensor(f"in_{name}_dram", v.shape, _mybir.dt.from_np(v.dtype), kind="ExternalInput").ap()
    out = nc.dram_tensor("out_0_dram", (2, 32, 32, 64), _mybir.dt.float32, kind="ExternalOutput").ap()
    build(nc, args, out)
    r = _run(nc, [arrays], core_ids=[0])
    return r.results[0]["out_0_dram"]
```

```python
from contextlib import ExitStack

import numpy as np

import concourse.bass as bass
from concourse import mybir

F32 = mybir.dt.float32
F16 = mybir.dt.float16
I32 = mybir.dt.int32
U8 = mybir.dt.uint8
ALU = mybir.AluOpType
ACT = mybir.ActivationFunctionType
AX = mybir.AxisListType

P = 128
B, HH, WW, C = 2, 32, 32, 64
TOK = HH * WW
NT = TOK // P
BLK = 512
NB = TOK // BLK
EPS = 1e-5
NEG = -1e30

NH0, WIN = 4, 7
HD0 = C // NH0
ROWS = P // WW
REL = 2 * WIN - 1
HID = 4 * C
UN0 = NT * NH0

NH1 = 8
NPAIR = NH1 // 2
GRP = 8
QT = BLK // P

NSTEP, NOPS = 33, 19
FH = 256
NONE = 4 * 64
LN = 6
NCTL = 14

WLOADS = 16 * (13 + 14)


def window_keys(t):
    first = min(max(ROWS * t - WIN // 2, 0), HH - WIN)
    last = min(max(ROWS * t + ROWS - 1 - WIN // 2, 0), HH - WIN) + WIN - 1
    return first, last - first + 1, (0 if t == 0 else 2 if t == NT - 1 else 1)


def key_chunks(t):
    first, rows, kind = window_keys(t)
    at, n = first * WW, rows * WW
    out = []
    while n > 0:
        k = min(P, n)
        slot = NT + at // P if kind == 0 else (at - WW) // P
        out.append((at, k, slot))
        at, n = at + k, n - k
    return out


VTILES = [(WW + P * j, min(P, TOK - WW - P * j)) for j in range(NT)] + [(0, P), (P, 3 * WW)]

LAG_PV, LAG_OUT, LAG_Y, LAG_YD = 10, 18, 19, 22


def build(nc, a, out):
    ctx = ExitStack()
    with ctx:
        def sb(name, shape, dt=F32):
            return ctx.enter_context(nc.sbuf_tensor(name, shape, dt))

        def sem(name):
            return ctx.enter_context(nc.semaphore(name))

        PS = ctx.enter_context(nc.psum_tensor("PS", [P, 8, 512], F32))
        LO, HI, OB, YB = PS[:, 4, :], PS[:, 5, :], PS[:, 6, :], PS[:, 7, :]

        ident = sb("ident", [P, P])
        shift = sb("shift", [REL, ROWS + 1, WW])
        colmask = sb("colmask", [P, WW])
        steps4 = sb("steps4", [1, NSTEP])
        opnum = sb("opnum", [1, NOPS])

        wq0 = sb("wq0", [C, NH0, 32])
        wk0 = sb("wk0", [C, NH0, 32])
        wv0 = sb("wv0", [C, C])
        bq0 = sb("bq0", [P, 1])
        bq0s = sb("bq0s", [P, 1])
        bk0 = sb("bk0", [P, 1])
        bv0 = sb("bv0", [P, C])
        norm = sb("norm", [C, 4])
        rpbT = sb("rpbT", [REL, NH0 * REL])
        pw0 = sb("pw0", [P, C])
        pb0 = sb("pb0", [P, C])
        fc1 = sb("fc1", [C, HID])
        fb1 = sb("fb1", [P, 2])
        fc2 = sb("fc2", [P, 2, C])
        fb2 = sb("fb2", [P, C])
        bu1 = sb("bu1", [P, C])
        wu1 = sb("wu1", [P, NPAIR, 2, C])
        w1 = sb("w1", [P, 3, NH1, C])
        wqk = sb("wqk", [P, 2, 2, NH1, 2, C], F16)
        wv1 = sb("wv1", [P, 2, NH1 * C], F16)

        xall = sb("xall", [P, B * NT, C])
        x2 = sb("x2", [P, B * NT, C])
        xn = sb("xn", [P, NT, C])
        xsq = sb("xsq", [P, NT, C])
        mean = sb("mean", [P, NT])
        var = sb("var", [P, NT])
        rstd = sb("rstd", [P, NT])
        minus_half = sb("minus_half", [P, NT])
        xb = sb("xb", [P, NT, C])
        x1 = sb("x1", [P, NT, C])
        xT = sb("xT", [C, TOK])
        qT0 = sb("qT0", [P, TOK])
        kT0 = sb("kT0", [P, TOK])
        V0 = sb("V0", [P, NT + 2, NH0, 32])
        OT0 = sb("OT0", [P, 2, P])
        aS = sb("aS", [P, B * TOK], F16)
        aT = sb("aT", [C, B * TOK])
        prob = sb("prob", [P, 3, TOK])
        negm = sb("negm", [P, 4])
        maxp = sb("maxp", [P, 4])
        sbias = sb("sbias", [P, 3, (WIN + ROWS - 1) * WW])
        rsum = sb("rsum", [P, 4])
        rinv = sb("rinv", [P, 4])
        V = sb("V", [P, B * NT, P])
        PT = sb("PT", [P, 2, 2, NT, BLK])
        OT = sb("OT", [P, 2, BLK])
        qS = sb("qS", [P, 2, 2, B * TOK], F16)
        kS = sb("kS", [P, 2, B * TOK], F16)
        sums = sb("sums", [P, 2 * B, QT, 2])
        weight = sb("weight", [P, 2 * B, QT, 2])
        yw = sb("yw", [P, QT, 2, C])

        mask8 = sb("mask8", [1, 2, NSTEP, NOPS], U8)
        codes = sb("codes", [1, NSTEP, NOPS])
        codew = sb("codew", [1, NSTEP, NOPS])
        code = sb("code", [1, NSTEP])
        key = sb("key", [1, NSTEP])
        dead = sb("dead", [1, NSTEP])
        row = sb("row", [1, C])
        top = sb("top", [1, 1])
        hit = sb("hit", [1, NOPS])
        cand = sb("cand", [1, NOPS])
        opf = sb("opf", [1, 1])
        nextf = sb("nextf", [1, 1])
        count_i = sb("count_i", [1, NSTEP], I32)
        control = sb("control", [1, NSTEP + 1, 2], I32)
        wqs = sb("wqs", [C, C])
        wks = sb("wks", [C, C])
        wvs = sb("wvs", [C, C])
        wos = sb("wos", [P, C])
        w1s = sb("w1s", [C, FH])
        w2s = sb("w2s", [P, 2, C])
        b1s = sb("b1s", [P, 2])
        b2s = sb("b2s", [C, 1])
        qT, kT = qT0, kT0
        PTrow = PT[:, :, :, :, :].rearrange("p g l k q -> p (g l k q)")
        Z = PTrow[:, 0:2 * B * TOK].rearrange("p (h t) -> p h t", h=2)
        used = [0]

        def part_of_PT(*shape):
            n, names = int(np.prod(shape)), "abcd"[:len(shape)]
            used[0] += n
            return PTrow[:, used[0] - n:used[0]].rearrange(
                f"p ({' '.join(names)}) -> p {' '.join(names)}", **dict(zip(names, shape)))
        G0 = part_of_PT(2, TOK)
        tall = part_of_PT(NH0 * REL, WW)
        tabs = [part_of_PT(NH0, n, WW) for n in (WIN, WIN + ROWS - 1, WIN)]
        PT0 = part_of_PT(4, 3, P)
        xn2 = part_of_PT(NT, 2, C)

        gate = sem("gate")
        x_loaded = sem("x_loaded")
        zeroed = sem("zeroed")
        w_loaded = sem("w_loaded")
        late_loaded = sem("late_loaded")
        ident_made = sem("ident_made")
        pool_chain = sem("pool_chain")
        consts_made = sem("consts_made")
        bias_expanded = sem("bias_expanded")
        bias_masked = sem("bias_masked")
        bq_scaled = sem("bq_scaled")
        tables_made = sem("tables_made")
        codes_made = sem("codes_made")
        stored = sem("stored")

        def ring(name):
            return {k: sem(f"{name}_piece_{k}") for k in
                    ("lo_filled", "lo_drained", "hi_filled", "hi_drained", "mid_filled", "mid_drained",
                     "y_filled", "y_drained")}

        def core(name):
            return {k: sem(f"{name}_{k}") for k in
                    ("scored", "biased", "maxed", "exped", "inverted", "scaled", "lo_turned", "hi_turned",
                     "lo_drained", "hi_drained", "out_summed", "out_drained", "y_filled", "y_drained")}

        r0, c0 = ring("nat"), core("nat")
        ln0 = sem("nat_ln_chain")
        normed = sem("nat_normed")
        biased = sem("nat_residual_biased")
        stage1_done = sem("stage1_done")
        c1 = core("glob")
        weights_loaded = sem("glob_weights_loaded")
        weights_split = sem("glob_weights_split")
        piece_filled = sem("glob_piece_filled")
        piece_high = sem("glob_piece_high_made")
        piece_drained = sem("glob_piece_drained")
        weighed = sem("glob_weighed")
        input_high = sem("glob_input_high_made")
        ln3 = sem("state_ln_chain")
        normed3 = sem("state_normed")
        r3 = ring("state")
        r2, c2 = ring("routed"), core("routed")
        rf = ring("ffn")
        rstd_made = sem("rstd_made")
        control_ready = sem("control_ready")
        ctl_chain = sem("ctl_chain")
        row_turned = sem("row_turned")
        attn_loaded = sem("attn_loaded")
        ffn_loaded = sem("ffn_loaded")
        re = ring("end")
        result = sem("result")

        scores2 = [PS[:, 2 * k:2 * k + 2, :].rearrange("p a b -> p (a b)") for k in range(2)]

        block = ctx.enter_context(nc.Block())

        N0 = dict(lo=5 + NB, hi=5 + 2, mid=NB, y=2)
        N2 = dict(lo=3, hi=3, y=4)
        NF = dict(lo=4 + 2, hi=4 + 2)

        def nat_drain(copy, func, bank, u):
            t = u // NH0
            chunks = key_chunks(t)
            full = len(chunks) - 1
            k = chunks[-1][1]
            args = (func,) if func is not None else ()
            copy(PT0[:, u % 4, 0:full, :], bank[:, 0:full * P].rearrange("p (n q) -> p n q", n=full), *args)
            return copy(PT0[0:k, u % 4, full, :], bank[0:k, full * P:(full + 1) * P], *args)

        def scan(e, attend, feed, after):
            word = e.alloc_register("word")
            na = e.alloc_register("attended")
            nf = e.alloc_register("fed")
            nu = e.alloc_register("updates")
            for r in (na, nf, nu):
                e.reg_mov(r, 0)
            e.wait_ge(control_ready, 1)
            e.sem_inc(gate, 1)
            e.reg_load(word, control[0:1, 0:1, 0:1])
            with e.Fori(0, NSTEP) as step:
                w = e.snap(word, min_val=0, max_val=2 * NONE)
                with e.If(e.snap(w // 4) == step):
                    flags = e.snap(e.snap(word, min_val=0, max_val=2 * NONE) % 4)
                    slot = e.snap(nu, min_val=0, max_val=NSTEP - 1)
                    if attend:
                        with e.If(flags >= 2):
                            attend(e.snap(na, min_val=0, max_val=NSTEP - 1), step, slot)
                            e.reg_add(na, na, 1)
                    if feed:
                        with e.If(e.snap(flags % 2) == 1):
                            feed(e.snap(nf, min_val=0, max_val=NSTEP - 1), step, slot)
                            e.reg_add(nf, nf, 1)
                    e.reg_add(nu, nu, 1)
                    now = e.snap(nu, min_val=1, max_val=NSTEP)
                    if after:
                        after(now)
                    e.wait_ge(control_ready, now + 1)
                    e.sem_inc(gate, 1)
                    e.reg_load(word, control[0:1, bass.ds(now, 1), 0:1])

        def bias_table(emit, copy, kind, *args):
            t = (0, 1, NT - 1)[kind]
            first = window_keys(t)[0]
            toff = tall[:, :, :].rearrange("p (h r) c -> p h r c", h=NH0)
            for di in range(ROWS):
                i = ROWS * t + di
                start = min(max(i - WIN // 2, 0), HH - WIN)
                r = start - i + WIN - 1
                part = slice(WW * di, WW * (di + 1))
                emit(copy(tabs[kind][part, :, start - first:start - first + WIN, :], toff[part, :, r:r + WIN, :], *args))

        PIECES = []
        for img in range(B):
            PIECES += [(what, lane, img * NB + b) for what in ("k", "q") for lane in range(2) for b in range(NB)]
            PIECES += [("v", None, img * NB + b) for b in range(NB)]
        NPC = len(PIECES)

        def pieces_of_step(i):
            n = 2 * (i - (GRP * 2 * B + 1))
            return [m for m in (n, n + 1) if 0 <= m < NPC]

        def pe_attention(pe, s, base, ngroups, ready, score_mms, y_of, tail=None):
            n = GRP * ngroups
            bu, bg = base(n), base(ngroups)

            def score(u):
                g, lane, qt = u // GRP, u % 2, (u % GRP) // 2
                if u >= 2:
                    pe.wait_ge(s["exped"], bu + (u - 1))
                score_mms(scores2[u % 2], lane, (g * QT + qt) * P, (g // 2) * TOK).then_inc(s["scored"], 1)

            def turn(u):
                pe.wait_ge(s[ready], bu + (u + 1))
                for half, bank, filled, drained in ((0, LO, "lo_turned", "lo_drained"),
                                                    (1, HI, "hi_turned", "hi_drained")):
                    if u >= 1:
                        pe.wait_ge(s[drained], bu + u)
                    for k in range(4):
                        kt = 4 * half + k
                        tr = pe.transpose(bank[:, k * P:(k + 1) * P],
                                          prob[:, u % 3, kt * P:(kt + 1) * P], ident[:, :])
                    tr.then_inc(s[filled], 1)

            def values(g, k):
                if k == 0:
                    pe.wait_ge(s["lo_drained"], bu + GRP * (g + 1))
                    pe.wait_ge(s["hi_drained"], bu + GRP * (g + 1))
                    if g >= 1:
                        pe.wait_ge(s["out_drained"], bg + g)
                for lane in range(2):
                    cols = slice(64 * lane, 64 * lane + 64)
                    mm = pe.matmul(OB[64 * lane:64 * lane + 64, :], V[:, (g // 2) * NT + k, cols],
                                   PT[:, g % 2, lane, k, :], start=(k == 0), stop=(k == NT - 1))
                if k == NT - 1:
                    mm.then_inc(s["out_summed"], 1)

            score(0)
            score(1)
            for i in range(n + LAG_Y + 3):
                if i + 2 < n:
                    score(i + 2)
                if 1 <= i <= n:
                    turn(i - 1)
                for g in range(ngroups):
                    k = i - GRP * g - LAG_PV
                    if 0 <= k < NT - 1:
                        values(g, k)
                    if k == NT - 2:
                        values(g, NT - 1)
                    if i == GRP * g + LAG_Y:
                        pe.wait_ge(s["out_drained"], bg + (g + 1))
                        y_of(g, bg)
                if tail:
                    tail(i)

        @block.tensor
        def _(pe):
            pe.wait_ge(w_loaded, WLOADS)
            pe.wait_ge(consts_made, 1)
            for j in range(WW):
                bank, slot = j // 9, j % 9
                mm = pe.matmul(PS[:, bank, slot * NH0 * REL:(slot + 1) * NH0 * REL],
                               shift[:, :, :].rearrange("c a m -> c (a m)")[:, WW - 1 - j:WW - 1 - j + P], rpbT[:, :], start=True, stop=True)
            mm.then_inc(bias_expanded, 1)
            pe.wait_ge(ident_made, 1)
            pe.wait_ge(bias_masked, 1)

            with pe.Fori(0, B) as img:
                blo, bhi, bmid, by = (pe.snap(img * N0[k]) for k in ("lo", "hi", "mid", "y"))
                bun = pe.snap(img * UN0)
                bnt = pe.snap(img * NT)
                bln = pe.snap(img * 3)
                cnt = dict(lo=0, hi=0, mid=0, y=0)
                bases = dict(lo=blo, hi=bhi, mid=bmid, y=by)

                def fill(which, mms):
                    n = cnt[which]
                    if n:
                        pe.wait_ge(r0[which + "_drained"], bases[which] + n)
                        pe.sem_inc(gate, 1)
                    mms().then_inc(r0[which + "_filled"], 1)
                    cnt[which] = n + 1

                def turn_norm(n, twice=False):
                    pe.wait_ge(normed, bln + n)
                    pe.sem_inc(gate, 1)
                    for blk, (which, bank) in enumerate((("lo", LO), ("hi", HI))):
                        def tr():
                            for j in range(QT):
                                rows, src = (P, xn2[:, blk * QT + j].rearrange("p l c -> p (l c)")) if twice \
                                    else (C, xn[:, blk * QT + j, :])
                                m = pe.transpose(bank[0:rows, j * P:(j + 1) * P], src, ident[:, :])
                            return m
                        fill(which, tr)

                turn_norm(1)
                for w in (wq0, wk0):
                    for blk, (which, bank) in enumerate((("lo", LO), ("hi", HI))):
                        if w is wq0:
                            pe.wait_ge(r0[which + "_drained"], bases[which] + 1)
                            pe.sem_inc(gate, 1)
                        fill(which, lambda: pe.matmul(bank, w[:, :, :].rearrange("c h d -> c (h d)"),
                                                      xT[:, blk * BLK:(blk + 1) * BLK], start=True, stop=True))

                def value_tiles(tiles):
                    def go():
                        for n, j in enumerate(tiles):
                            t0, k = VTILES[j]
                            m = pe.matmul(HI[0:k, n * C:(n + 1) * C], xT[:, t0:t0 + k], wv0[:, :],
                                          start=True, stop=True)
                        return m
                    return go
                fill("hi", value_tiles(range(NT)))
                fill("hi", value_tiles(range(NT, NT + 2)))
                pe.wait_ge(r0["lo_drained"], blo + cnt["lo"])
                pe.wait_ge(r0["hi_drained"], bhi + cnt["hi"])
                pe.sem_inc(gate, 1)

                def score(u):
                    t, h = u // NH0, u % NH0
                    first, rows, kind = window_keys(t)
                    if u >= 4:
                        pe.wait_ge(c0["biased"], bun + (u - 3))
                    bank = PS[:, u % 4, 0:rows * WW]
                    hr = slice(32 * h, 32 * h + 32)
                    pe.matmul(bank, qT0[hr, t * P:(t + 1) * P], kT0[hr, first * WW:(first + rows) * WW],
                              start=True, stop=True).then_inc(c0["scored"], 1)

                def turn(u):
                    t = u // NH0
                    pe.wait_ge(c0["scaled"], bun + (u + 1))
                    half = ("lo", "hi")[u % 2]
                    bank = (LO, HI)[u % 2]
                    if u >= 2:
                        pe.wait_ge(c0[half + "_drained"], base_half + u // 2)
                    for n, (_, k, _) in enumerate(key_chunks(t)):
                        tr = pe.transpose(bank[0:k, n * P:(n + 1) * P], prob[:, u % 3, n * P:n * P + k], ident[:, :])
                    tr.then_inc(c0[half + "_turned"], 1)

                def values(u):
                    t, h = u // NH0, u % NH0
                    half = ("lo", "hi")[u % 2]
                    pe.wait_ge(c0[half + "_drained"], base_half + (u // 2 + 1))
                    if h == 0 and t >= 1:
                        pe.wait_ge(c0["out_drained"], bnt + t)
                    chunks = key_chunks(t)
                    for n, (_, k, slot) in enumerate(chunks):
                        mm = pe.matmul(OB[32 * h:32 * h + 32, 0:P], V0[0:k, slot, h, :], PT0[0:k, u % 4, n, :],
                                       start=(n == 0), stop=(n == len(chunks) - 1))
                    if h == NH0 - 1:
                        mm.then_inc(c0["out_summed"], 1)

                base_half = pe.snap(img * (UN0 // 2))
                score(0)
                score(1)
                for i in range(UN0 + 7):
                    if i + 2 < UN0:
                        score(i + 2)
                    if 1 <= i <= UN0:
                        turn(i - 1)
                    if 3 <= i < UN0 + 3:
                        values(i - 3)
                    if i >= 9 and (i - 9) % NH0 == 0:
                        t = (i - 9) // NH0
                        pe.wait_ge(c0["out_drained"], bnt + (t + 1))
                        mm = pe.matmul(YB[:, t * C:(t + 1) * C], OT0[:, t % 2, :], pw0[:, :], start=True, stop=True)
                        if t == NT - 1:
                            mm.then_inc(r0["y_filled"], 1)
                cnt["y"] = 1

                turn_norm(2)
                pe.wait_ge(r0["lo_drained"], blo + cnt["lo"])
                pe.wait_ge(r0["hi_drained"], bhi + cnt["hi"])
                pe.sem_inc(gate, 1)
                for blk in range(NB):
                    for half, (which, bank) in enumerate((("lo", LO), ("mid", OB))):
                        fill(which, lambda: pe.matmul(bank, fc1[:, half * P:(half + 1) * P],
                                                      xT[:, blk * BLK:(blk + 1) * BLK], start=True, stop=True))
                pe.wait_ge(r0["lo_drained"], blo + cnt["lo"])
                pe.wait_ge(r0["mid_drained"], bmid + cnt["mid"])
                pe.wait_ge(r0["y_drained"], by + 1)
                for t in range(NT):
                    for half in range(2):
                        mm = pe.matmul(YB[:, t * C:(t + 1) * C], G0[:, half, t * P:(t + 1) * P], fc2[:, half, :],
                                       start=(half == 0), stop=(half == 1))
                mm.then_inc(r0["y_filled"], 1)
                turn_norm(3, twice=True)
                pe.wait_ge(r0["lo_drained"], blo + cnt["lo"])
                pe.wait_ge(r0["hi_drained"], bhi + cnt["hi"])
                pe.sem_inc(gate, 1)
                assert cnt["lo"] == N0["lo"] and cnt["hi"] == N0["hi"] and cnt["mid"] == N0["mid"]

            pe.wait_ge(weights_loaded, 16 * 8)
            pe.wait_ge(weights_split, 1)

            def project(pair, n, base):
                what, lane, blk = PIECES[n]
                bank = PS[:, n % 4, :]
                if n >= 4:
                    pe.wait_ge(piece_drained, base + (n - 3))
                    pe.sem_inc(gate, 1)
                if what == "v":
                    for j in range(QT):
                        t = blk * QT + j
                        for part in range(2):
                            m = pe.matmul(bank[:, j * P:(j + 1) * P], aS[:, t * P:(t + 1) * P],
                                          wv1[:, part, bass.ds(pair * P, P)], start=(part == 0), stop=(part == 1))
                else:
                    for part in range(2):
                        w = wqk[:, "qk".index(what), part, bass.ds(pair * 2 + lane, 1), :, :]
                        m = pe.matmul(bank, w.rearrange("p h a c -> p (h a c)"), aS[:, blk * BLK:(blk + 1) * BLK],
                                      start=(part == 0), stop=(part == 1))
                m.then_inc(piece_filled, 1)

            for n in range(NPC):
                project(0, n, 0)

            def glob_pair(pair, last):
                base = lambda k: pair * k if last else pe.snap(pair * k)
                nxt = None if last else pe.snap(pair + 1)
                bp = None if last else pe.snap(pair * NPC + NPC)
                pe.wait_ge(piece_drained, base(NPC) + NPC)
                pe.sem_inc(gate, 1)

                def score_mms(bank, lane, q0, k0):
                    for part in range(2):
                        for j in range(NB):
                            mm = pe.matmul(bank[:, j * BLK:(j + 1) * BLK], qS[:, part, lane, q0:q0 + P],
                                           kS[:, lane, k0 + j * BLK:k0 + (j + 1) * BLK],
                                           start=(part == 0), stop=(part == 1))
                    return mm

                def y_of(g, bg):
                    if g >= 1:
                        pe.wait_ge(c1["y_drained"], bg + g)
                    for j in range(QT):
                        mm = pe.matmul(YB[:, j * P:(j + 1) * P], OT[:, g % 2, j * P:(j + 1) * P],
                                       wu1[:, bass.ds(pair, 1), :, :].rearrange("p n l c -> p (n l c)"),
                                       start=True, stop=True)
                    mm.then_inc(c1["y_filled"], 1)

                def tail(i):
                    for n in pieces_of_step(i):
                        if n == 0:
                            pe.wait_ge(c1["exped"], base(GRP * 2 * B) + GRP * 2 * B)
                            pe.sem_inc(gate, 1)
                        project(nxt, n, bp)

                pe_attention(pe, c1, base, 2 * B, "exped", score_mms, y_of, None if last else tail)
                pe.wait_ge(c1["y_drained"], base(2 * B) + 2 * B)

            with pe.Fori(0, NPAIR - 1) as pair:
                glob_pair(pair, False)
            glob_pair(NPAIR - 1, True)

            pe.wait_ge(normed3, 1)
            for blk in range(B * NB):
                if blk % NB == 0 and blk:
                    pe.wait_ge(normed3, 1 + blk // NB)
                which, bank = (("lo", LO), ("hi", HI))[blk % 2]
                if blk >= 2:
                    pe.wait_ge(r3[which + "_drained"], blk // 2)
                for j in range(QT):
                    m = pe.transpose(bank[0:C, j * P:(j + 1) * P], xn[:, (blk % NB) * QT + j, :], ident[:, :])
                m.then_inc(r3[which + "_filled"], 1)
            pe.wait_ge(r3["lo_drained"], 2)
            pe.wait_ge(r3["hi_drained"], 2)

            def show_row():
                pe.transpose(YB[0:1, 0:C], aT[:, 0:1], ident[0:C, 0:C]).then_inc(row_turned, 1)
            show_row()

            def attend(na, step, slot):
                base = lambda k: pe.snap(na * k)
                blo, bhi, by = base(N2["lo"]), base(N2["hi"]), base(N2["y"])
                pe.wait_ge(attn_loaded, base(80) + 80)
                pe.sem_inc(gate, 1)
                for n, w in enumerate((wqs, wks)):
                    for side, (which, bank, bs) in enumerate((("lo", LO, blo), ("hi", HI, bhi))):
                        if n:
                            pe.wait_ge(r2[which + "_drained"], bs + n)
                            pe.sem_inc(gate, 1)
                        for lane in range(2):
                            m = pe.matmul(bank[64 * lane:64 * lane + 64, :], w[:, :],
                                          aT[:, lane * TOK + side * BLK:lane * TOK + (side + 1) * BLK],
                                          start=True, stop=True)
                        m.then_inc(r2[which + "_filled"], 1)
                for side, (which, bank, bs) in enumerate((("lo", LO, blo), ("hi", HI, bhi))):
                    pe.wait_ge(r2[which + "_drained"], bs + 2)
                    pe.sem_inc(gate, 1)
                    for j in range(QT):
                        for lane in range(2):
                            t0 = lane * TOK + (side * QT + j) * P
                            m = pe.matmul(bank[:, j * P + 64 * lane:j * P + 64 * lane + 64], aT[:, t0:t0 + P],
                                          wvs[:, :], start=True, stop=True)
                    m.then_inc(r2[which + "_filled"], 1)
                pe.wait_ge(r2["lo_drained"], blo + 3)
                pe.wait_ge(r2["hi_drained"], bhi + 3)
                pe.sem_inc(gate, 1)

                def y_of(g, bg):
                    for lane in range(2):
                        n = 2 * g + lane
                        if n:
                            pe.wait_ge(c2["y_drained"], by + n)
                        pe.sem_inc(gate, 1)
                        pe.matmul(YB[0:C, :], wos[64 * lane:64 * lane + 64, :], OT[64 * lane:64 * lane + 64, g % 2, :],
                                  start=True, stop=True).then_inc(c2["y_filled"], 1)

                def score_mms(bank, lane, q0, k0):
                    rows = slice(64 * lane, 64 * lane + 64)
                    for j in range(NB):
                        mm = pe.matmul(bank[:, j * BLK:(j + 1) * BLK], qT[rows, q0:q0 + P],
                                       kT[rows, k0 + j * BLK:k0 + (j + 1) * BLK], start=True, stop=True)
                    return mm

                pe_attention(pe, c2, base, 2, "scaled", score_mms, y_of)
                pe.wait_ge(c2["y_drained"], by + 4)
                pe.sem_inc(gate, 1)

            def feed(nf, step, slot):
                base = lambda k: pe.snap(nf * k)
                blo, bhi = base(NF["lo"]), base(NF["hi"])
                pe.wait_ge(ffn_loaded, base(64) + 64)
                pe.sem_inc(gate, 1)
                cnt = [0, 0]

                def piece(mms):
                    side = sum(cnt) % 2
                    which, bank, bs = (("lo", LO, blo), ("hi", HI, bhi))[side]
                    if cnt[side]:
                        pe.wait_ge(rf[which + "_drained"], bs + cnt[side])
                        pe.sem_inc(gate, 1)
                    mms(bank).then_inc(rf[which + "_filled"], 1)
                    cnt[side] += 1
                for blk in range(B * NB):
                    for half in range(2):
                        piece(lambda bank: pe.matmul(bank, w1s[:, half * P:(half + 1) * P],
                                                     aT[:, blk * BLK:(blk + 1) * BLK], start=True, stop=True))
                pe.wait_ge(rf["lo_drained"], blo + cnt[0])
                pe.wait_ge(rf["hi_drained"], bhi + cnt[1])
                pe.sem_inc(gate, 1)
                for blk in range(B * NB):
                    def go(bank):
                        for half in range(2):
                            m = pe.matmul(bank[0:C, :], w2s[:, half, :], Z[:, half, blk * BLK:(blk + 1) * BLK],
                                          start=(half == 0), stop=(half == 1))
                        return m
                    piece(go)
                pe.wait_ge(rf["lo_drained"], blo + NF["lo"])
                pe.wait_ge(rf["hi_drained"], bhi + NF["hi"])
                pe.sem_inc(gate, 1)

            scan(pe, attend, feed, lambda now: show_row())

            for blk in range(B * NB):
                which, bank = (("lo", LO), ("hi", HI))[blk % 2]
                if blk >= 2:
                    pe.wait_ge(re[which + "_drained"], blk // 2)
                for j in range(QT):
                    t = blk * QT + j
                    m = pe.transpose(bank[:, j * C:(j + 1) * C], aT[:, t * P:(t + 1) * P], ident[0:C, 0:C])
                m.then_inc(re[which + "_filled"], 1)

        def act_attention(act, s, base, ngroups, sum_of, tail=None):
            n = GRP * ngroups
            bu, bg = base(n), base(ngroups)
            for i in range(n + LAG_YD):
                if i < n:
                    act.wait_ge(s["maxed"], bu + (i + 1))
                    if i >= 3:
                        act.wait_ge(s["hi_turned"], bu + (i - 2))
                    act.activation(prob[:, i % 3, :], scores2[i % 2], ACT.Exp, bias=negm[:, i % 4:i % 4 + 1],
                                   scale=1.0, accum_out=sum_of(i)).then_inc(s["exped"], 1)
                u = i - 2
                if 0 <= u < n:
                    g, lane, qt = u // GRP, u % 2, (u % GRP) // 2
                    act.wait_ge(s["lo_turned"], bu + (u + 1))
                    act.activation(PT[:, g % 2, lane, 0:4, qt * P:(qt + 1) * P],
                                   LO.rearrange("p (k q) -> p k q", k=4), ACT.Copy).then_inc(s["lo_drained"], 1)
                for g in range(ngroups):
                    if i == GRP * g + LAG_OUT:
                        act.wait_ge(s["out_summed"], bg + (g + 1))
                        act.activation(OT[:, g % 2, :], OB, ACT.Copy).then_inc(s["out_drained"], 1)
                if tail:
                    tail(i)

        @block.scalar
        def _(act):
            act.dma_start(norm[:, 0:1], a["L0_conv_norm1_g"].rearrange("(c o) -> c o", o=1)).then_inc(w_loaded, 16)
            act.dma_start(norm[:, 1:2], a["L0_conv_norm1_b"].rearrange("(c o) -> c o", o=1)).then_inc(w_loaded, 16)
            act.dma_start(norm[:, 2:3], a["L0_conv_norm2_g"].rearrange("(c o) -> c o", o=1)).then_inc(w_loaded, 16)
            act.dma_start(norm[:, 3:4], a["L0_conv_norm2_b"].rearrange("(c o) -> c o", o=1)).then_inc(w_loaded, 16)
            act.dma_start(fb1[:, :], a["L0_conv_fc1_b"].rearrange("(h p) -> p h", p=P),
                          allow_slow_non_contiguous=True).then_inc(w_loaded, 16)
            qb = a["L0_conv_qkv_b"]
            for n, dst in enumerate((bq0, bk0)):
                for h in range(NH0):
                    src = qb[n * C + h * HD0:n * C + (h + 1) * HD0].rearrange("(c o) -> c o", o=1)
                    if n == 0 and h == 0:
                        act.wait_ge(zeroed, 1)
                    act.dma_start(dst[32 * h:32 * h + HD0, :], src).then_inc(w_loaded, 16)
            act.wait_ge(w_loaded, WLOADS)
            act.activation(bq0s[:, :], bq0[:, :], ACT.Copy, scale=HD0 ** -0.5).then_inc(bq_scaled, 1)
            act.wait_ge(bq_scaled, 1)

            act.wait_ge(bias_masked, 1)
            bias_table(lambda ins: ins.then_inc(tables_made, 1), act.activation, 0, ACT.Copy)

            with act.Fori(0, B) as img:
                blo, bmid, bun, bnt = (act.snap(img * k) for k in (N0["lo"], N0["mid"], UN0, NT))
                bhalf = act.snap(img * (UN0 // 2))
                cnt = dict(lo=0, mid=0)

                def drain(which, out, func, **kw):
                    cnt[which] += 1
                    act.wait_ge(r0[which + "_filled"], (blo if which == "lo" else bmid) + cnt[which])
                    bank = LO if which == "lo" else OB
                    src = bank if out.shape[0] == P else bank[0:out.shape[0], :]
                    act.activation(out, src, func, **kw).then_inc(r0[which + "_drained"], 1)

                drain("lo", xT[:, 0:BLK], ACT.Identity, scale=norm[:, 0:1], bias=norm[:, 1:2])
                drain("lo", qT0[:, 0:BLK], ACT.Identity, scale=HD0 ** -0.5, bias=bq0s[:, 0:1])
                drain("lo", kT0[:, 0:BLK], ACT.Identity, scale=1.0, bias=bk0[:, 0:1])

                for i in range(UN0 + 8):
                    if i < UN0:
                        w = window_keys(i // NH0)[1] * WW
                        act.wait_ge(c0["maxed"], bun + (i + 1))
                        if i >= 3:
                            j = i - 3
                            act.wait_ge(c0[("lo", "hi")[j % 2] + "_turned"], bhalf + (j // 2 + 1))
                        act.activation(prob[:, i % 3, 0:w], sbias[:, i % 3, 0:w], ACT.Exp,
                                       bias=negm[:, i % 4:i % 4 + 1], scale=1.0,
                                       accum_out=rsum[:, i % 4:i % 4 + 1]).then_inc(c0["exped"], 1)
                    u = i - 2
                    if 0 <= u < UN0 and u % 2 == 0:
                        act.wait_ge(c0["lo_turned"], bhalf + (u // 2 + 1))
                        nat_drain(act.activation, ACT.Copy, LO, u).then_inc(c0["lo_drained"], 1)
                    if i >= 7 and (i - 7) % NH0 == 0 and (i - 7) // NH0 < NT:
                        t = (i - 7) // NH0
                        act.wait_ge(c0["out_summed"], bnt + (t + 1))
                        act.activation(OT0[:, t % 2, :], OB[:, 0:P], ACT.Copy).then_inc(c0["out_drained"], 1)

                drain("lo", xT[:, 0:BLK], ACT.Identity, scale=norm[:, 2:3], bias=norm[:, 3:4])
                for blk in range(NB):
                    for half, which in enumerate(("lo", "mid")):
                        drain(which, G0[:, half, blk * BLK:(blk + 1) * BLK], ACT.Gelu, bias=fb1[:, half:half + 1],
                              scale=1.0)
                for blk, which in enumerate(("lo", "hi")):
                    if which == "lo":
                        act.wait_ge(r0["lo_filled"], blo + N0["lo"])
                    else:
                        act.wait_ge(r0["hi_filled"], act.snap(img * N0["hi"]) + N0["hi"])
                    act.activation(aS[:, bass.ds(img * TOK + blk * BLK, BLK)], (LO, HI)[blk], ACT.Copy)\
                       .then_inc(input_high, 1)
                cnt["lo"] += 1
                assert cnt["lo"] == N0["lo"] and cnt["mid"] == N0["mid"]

            def high_part(n, base):
                what, lane, blk = PIECES[n]
                bank = PS[:, n % 4, :]
                act.wait_ge(piece_filled, base + (n + 1))
                if what == "v":
                    half = QT // 2
                    ins = act.activation(V[:, blk * QT:blk * QT + half, :],
                                         bank[:, 0:half * P].rearrange("p (t c) -> p t c", t=half), ACT.Copy)
                else:
                    dst = kS[:, lane] if what == "k" else qS[:, 0, lane]
                    ins = act.activation(dst[:, blk * BLK:(blk + 1) * BLK], bank, ACT.Copy, scale=C ** -0.25)
                ins.then_inc(piece_high, 1)

            for n in range(NPC):
                high_part(n, 0)

            def glob_pair(pair, last):
                base = lambda k: pair * k if last else act.snap(pair * k)
                bp = None if last else act.snap(pair * NPC + NPC)

                def tail(i):
                    for n in pieces_of_step(i):
                        high_part(n, bp)

                def sum_of(i):
                    return sums[:, i // GRP, (i % GRP) // 2, i % 2:i % 2 + 1]

                act_attention(act, c1, base, 2 * B, sum_of, None if last else tail)

            with act.Fori(0, NPAIR - 1) as pair:
                glob_pair(pair, False)
            glob_pair(NPAIR - 1, True)

            for n in range(2):
                act.wait_ge(r3["lo_filled"], n + 1)
                act.activation(aT[:, 2 * n * BLK:(2 * n + 1) * BLK], LO[0:C, :], ACT.Copy).then_inc(r3["lo_drained"], 1)

            def attend(na, step, slot):
                base = lambda k: act.snap(na * k)
                blo = base(N2["lo"])
                for n, (dst, sc) in enumerate(((qT, C ** -0.5), (kT, 1.0))):
                    act.wait_ge(r2["lo_filled"], blo + (n + 1))
                    act.activation(dst[:, 0:BLK], LO, ACT.Copy, scale=sc).then_inc(r2["lo_drained"], 1)
                act.wait_ge(r2["lo_filled"], blo + 3)
                act.activation(V[:, 0:QT, :], LO.rearrange("p (t c) -> p t c", t=QT), ACT.Copy)\
                   .then_inc(r2["lo_drained"], 1)
                act_attention(act, c2, base, 2, lambda i: rsum[:, i % 4:i % 4 + 1])

            def feed(nf, step, slot):
                blo = act.snap(nf * NF["lo"])
                act.wait_ge(ffn_loaded, act.snap(nf * 64) + 64)
                n = 0
                for blk in range(B * NB):
                    n += 1
                    act.wait_ge(rf["lo_filled"], blo + n)
                    act.activation(Z[:, 0, blk * BLK:(blk + 1) * BLK], LO, ACT.Relu, bias=b1s[:, 0:1], scale=1.0)\
                       .then_inc(rf["lo_drained"], 1)
                for blk in (0, 2):
                    n += 1
                    act.wait_ge(rf["lo_filled"], blo + n)
                    act.activation(aT[:, blk * BLK:(blk + 1) * BLK], LO[0:C, :], ACT.Identity, bias=b2s[:, 0:1],
                                   scale=1.0).then_inc(rf["lo_drained"], 1)

            scan(act, attend, feed, None)

        @block.gpsimd
        def _(pool):
            chain = [0]

            def link(ins):
                chain[0] += 1
                ins.then_inc(pool_chain, 1)
                pool.wait_ge(pool_chain, chain[0])

            pool.memset(wq0[:, :, :], 0.0)
            pool.memset(wk0[:, :, :], 0.0)
            pool.memset(bq0[:, :], 0.0)
            pool.memset(bk0[:, :], 0.0)
            pool.memset(wu1[:, :, :, :], 0.0)
            link(pool.memset(pw0[:, :], 0.0))
            pool.sem_inc(zeroed, 1)
            link(pool.memset(shift[:, :, :], 0.0))
            for base in (-(WW - 1 + WIN - 1), 1 - (WIN - 1)):
                link(pool.affine_select(out=shift[:, :, :], in_=shift[:, :, :], compare_op=ALU.not_equal, fill=1.0,
                                        base=base, pattern=[[0, ROWS + 1], [1, WW]], channel_multiplier=1))
            pool.memset(V0[:, :, :, :], 0.0)
            link(pool.memset(colmask[:, :], 0.0))
            for g in range(ROWS):
                part = colmask[WW * g:WW * (g + 1), :]
                lo = part[:, 0:WW - WIN]
                link(pool.affine_select(out=lo, in_=lo, compare_op=ALU.is_ge, fill=NEG, base=WIN // 2,
                                        pattern=[[1, WW - WIN]], channel_multiplier=-1))
                hi = part[:, WIN:WW]
                link(pool.affine_select(out=hi, in_=hi, compare_op=ALU.is_ge, fill=NEG, base=WIN // 2 - WIN,
                                        pattern=[[-1, WW - WIN]], channel_multiplier=1))
            link(pool.memset(minus_half[:, :], -0.5))
            pool.sem_inc(consts_made, 1)
            link(pool.memset(ident[:, :], 0.0))
            link(pool.affine_select(out=ident[:, :], in_=ident[:, :], compare_op=ALU.not_equal, fill=1.0, base=0,
                                    pattern=[[-1, P]], channel_multiplier=1))
            pool.sem_inc(ident_made, 1)
            link(pool.iota(count_i[:, :], [[1, NSTEP]], base=0, channel_multiplier=0))
            link(pool.tensor_copy(steps4[:, :], count_i[:, :]))
            link(pool.tensor_copy(opnum[:, :], count_i[:, 0:NOPS]))
            link(pool.tensor_scalar(steps4[:, :], steps4[:, :], 4.0, None, ALU.mult))
            pool.sem_inc(consts_made, 1)
            link(pool.memset(tabs[1][:, :, :, :], NEG))
            pool.sem_inc(consts_made, 1)
            pool.wait_ge(bias_masked, 1)
            bias_table(link, pool.tensor_copy, 2)
            pool.sem_inc(tables_made, 1)

            def power(chain, links):
                pool.wait_ge(chain, links)
                pool.sem_inc(gate, 1)
                pool.tensor_tensor(rstd[:, :], var[:, :], minus_half[:, :], ALU.pow).then_inc(rstd_made, 1)

            pool.wait_ge(weights_loaded, 16 * 8)
            twice = [w1[:, n].rearrange("p h (o c) -> p h o c", o=1).to_broadcast([P, NH1, 2, C]) for n in range(2)]
            for n in range(2):
                link(pool.tensor_copy(wqk[:, n, 0], twice[n]))
            wv = w1[:, 2].rearrange("p h c -> p (h c)")
            link(pool.tensor_copy(wv1[:, 0, :], wv))
            for n in range(2):
                link(pool.tensor_tensor(wqk[:, n, 1], twice[n], wqk[:, n, 0], ALU.subtract))
            link(pool.tensor_tensor(wv1[:, 1, :], wv, wv1[:, 0, :], ALU.subtract))
            pool.sem_inc(weights_split, 1)

            with pool.Fori(0, B) as img:
                bln = pool.snap(img * (3 * LN))
                power(ln0, bln + LN)
                power(ln0, bln + 2 * LN)
                power(ln0, bln + 3 * LN)
            for img in range(B):
                power(ln3, (img + 1) * LN)

        def dve_attention(dve, s, base, ngroups, scale, y_out, tail=None):
            n = GRP * ngroups
            bu, bg = base(n), base(ngroups)
            for i in range(n + LAG_YD + 2):
                if i < n:
                    dve.wait_ge(s["scored"], bu + (i + 1))
                    dve.tensor_reduce(negm[:, i % 4:i % 4 + 1], scores2[i % 2], AX.X, ALU.max, negate=True)\
                       .then_inc(s["maxed"], 1)
                if scale and 1 <= i <= n:
                    u = i - 1
                    dve.wait_ge(s["exped"], bu + (u + 1))
                    dve.reciprocal(rinv[:, u % 4:u % 4 + 1], rsum[:, u % 4:u % 4 + 1]).then_inc(s["inverted"], 1)
                u = i - 2
                if 0 <= u < n:
                    g, lane, qt = u // GRP, u % 2, (u % GRP) // 2
                    dve.wait_ge(s["hi_turned"], bu + (u + 1))
                    dve.tensor_copy(PT[:, g % 2, lane, 4:8, qt * P:(qt + 1) * P],
                                    HI.rearrange("p (k q) -> p k q", k=4)).then_inc(s["hi_drained"], 1)
                if scale and 1 <= i <= n:
                    u = i - 1
                    dve.wait_ge(s["inverted"], bu + (u + 1))
                    dve.tensor_scalar(prob[:, u % 3, :], prob[:, u % 3, :], rinv[:, u % 4:u % 4 + 1], None,
                                      ALU.mult).then_inc(s["scaled"], 1)
                for g in range(ngroups):
                    if i == GRP * g + LAG_YD:
                        y_out(g, bg)
                if tail:
                    tail(i)

        @block.vector
        def _(dve):
            dve.wait_ge(bias_expanded, 1)
            dve.wait_ge(consts_made, 1)
            n = NH0 * REL
            for bank in range(4):
                j0, k = 9 * bank, min(9, WW - 9 * bank)
                last = dve.tensor_tensor(tall[:, :, j0:j0 + k].rearrange("p n j -> p j n"),
                                         PS[:, bank, 0:k * n].rearrange("p (j n) -> p j n", n=n),
                                         colmask[:, j0:j0 + k].rearrange("p (j o) -> p j o", o=1).to_broadcast([P, k, n]),
                                         ALU.add)
            last.then_inc(bias_masked, 1)
            dve.wait_ge(bias_masked, 1)
            dve.wait_ge(consts_made, 3)
            bias_table(lambda ins: ins.then_inc(tables_made, 1), dve.tensor_copy, 1)

            def bc(v, k=NT):
                return v.rearrange("p (t o) -> p t o", o=1).to_broadcast([P, k, C])

            def rows(v, k=NT):
                return v.rearrange("p (o c) -> p o c", o=1).to_broadcast([P, k, C])

            def layernorm(x, chain, base, n0, powers, done, twice=False):
                n = [n0]

                def link(ins):
                    n[0] += 1
                    ins.then_inc(chain, 1)
                    dve.wait_ge(chain, base + n[0])
                link(dve.tensor_reduce(mean[:, :], x, AX.X, ALU.add))
                link(dve.tensor_scalar(mean[:, :], mean[:, :], 1.0 / C, None, ALU.mult))
                link(dve.tensor_tensor(xn[:, :, :], x, bc(mean[:, :]), ALU.subtract))
                link(dve.tensor_tensor(xsq[:, :, :], xn[:, :, :], xn[:, :, :], ALU.mult))
                link(dve.tensor_reduce(var[:, :], xsq[:, :, :], AX.X, ALU.add))
                link(dve.tensor_scalar(var[:, :], var[:, :], 1.0 / C, EPS, ALU.mult, ALU.add))
                dve.wait_ge(rstd_made, powers)
                if twice:
                    for k in range(2):
                        last = dve.tensor_tensor(xn2[:, :, k, :], xn[:, :, :], bc(rstd[:, :]), ALU.mult)
                else:
                    last = dve.tensor_tensor(xn[:, :, :], xn[:, :, :], bc(rstd[:, :]), ALU.mult)
                last.then_inc(done, 1)
                return n[0]

            dve.wait_ge(x_loaded, 16)
            dve.wait_ge(w_loaded, WLOADS)
            with dve.Fori(0, B) as img:
                bln, bhi, by, bun, bnt = (dve.snap(img * k) for k in (3 * LN, N0["hi"], N0["y"], UN0, NT))
                bhalf = dve.snap(img * (UN0 // 2))
                bb = dve.snap(img * 4)
                brs = dve.snap(img * 3)
                cnt = [0]

                def filled():
                    cnt[0] += 1
                    dve.wait_ge(r0["hi_filled"], bhi + cnt[0])

                xin = xall[:, bass.ds(img * NT, NT), :]
                layernorm(xin, ln0, bln, 0, brs + 1, normed)
                filled()
                dve.tensor_scalar(xT[:, BLK:TOK], HI[0:C, :], norm[:, 0:1], norm[:, 1:2], ALU.mult, ALU.add)\
                   .then_inc(r0["hi_drained"], 1)
                dve.tensor_tensor(xb[:, :, :], xin, rows(pb0[:, :]), ALU.add).then_inc(biased, 1)
                filled()
                dve.tensor_scalar(qT0[:, BLK:TOK], HI, bq0[:, 0:1], HD0 ** -0.5, ALU.add, ALU.mult)\
                   .then_inc(r0["hi_drained"], 1)
                filled()
                dve.tensor_scalar(kT0[:, BLK:TOK], HI, bk0[:, 0:1], None, ALU.add).then_inc(r0["hi_drained"], 1)
                for tiles in (range(NT), range(NT, NT + 2)):
                    filled()
                    t0, full, k = tiles[0], len(tiles) - 1, VTILES[tiles[-1]][1]
                    for p, lo, hi in ((P, 0, full), (k, full, full + 1)):
                        for t in range(lo, hi):
                            d = dve.tensor_tensor(V0[0:p, t0 + t, :, 0:HD0],
                                                  HI[0:p, t * C:(t + 1) * C].rearrange("p (h d) -> p h d", h=NH0),
                                                  bv0[0:p, :].rearrange("p (h d) -> p h d", h=NH0), ALU.add)
                    d.then_inc(r0["hi_drained"], 1)

                dve.wait_ge(tables_made, 2 * ROWS + 1)
                for i in range(UN0 + 8):
                    if i < UN0:
                        w = window_keys(i // NH0)[1] * WW
                        dve.wait_ge(c0["scored"], bun + (i + 1))
                        kind = window_keys(i // NH0)[2]
                        dve.sem_inc(gate, 1)
                        dve.tensor_tensor_reduce(sbias[:, i % 3, 0:w], PS[:, i % 4, 0:w],
                                                 tabs[kind][:, i % NH0, :, :].rearrange("p a b -> p (a b)"),
                                                 1.0, 3 * NEG, ALU.add, ALU.max, maxp[:, i % 4:i % 4 + 1])\
                           .then_inc(c0["biased"], 1)
                    if 1 <= i <= UN0:
                        u = i - 1
                        dve.wait_ge(c0["exped"], bun + (u + 1))
                        dve.reciprocal(rinv[:, u % 4:u % 4 + 1], rsum[:, u % 4:u % 4 + 1])\
                           .then_inc(c0["inverted"], 1)
                    if i < UN0:
                        dve.wait_ge(c0["biased"], bun + (i + 1))
                        dve.tensor_scalar(negm[:, i % 4:i % 4 + 1], maxp[:, i % 4:i % 4 + 1], -1.0, None, ALU.mult)\
                           .then_inc(c0["maxed"], 1)
                    u = i - 2
                    if 0 <= u < UN0 and u % 2 == 1:
                        dve.wait_ge(c0["hi_turned"], bhalf + (u // 2 + 1))
                        nat_drain(dve.tensor_copy, None, HI, u).then_inc(c0["hi_drained"], 1)
                    if 1 <= i <= UN0:
                        u = i - 1
                        w = window_keys(u // NH0)[1] * WW
                        dve.wait_ge(c0["inverted"], bun + (u + 1))
                        dve.tensor_scalar(prob[:, u % 3, 0:w], prob[:, u % 3, 0:w], rinv[:, u % 4:u % 4 + 1], None,
                                          ALU.mult).then_inc(c0["scaled"], 1)

                dve.wait_ge(r0["y_filled"], by + 1)
                dve.wait_ge(biased, bb + 1)
                dve.tensor_tensor(x1[:, :, :], xb[:, :, :], YB.rearrange("p (t c) -> p t c", t=NT), ALU.add)\
                   .then_inc(r0["y_drained"], 1)
                dve.wait_ge(r0["y_drained"], by + 1)
                layernorm(x1[:, :, :], ln0, bln, LN, brs + 2, normed)
                dve.tensor_tensor(xb[:, :, :], x1[:, :, :], rows(fb2[:, :]), ALU.add).then_inc(biased, 1)
                filled()
                dve.tensor_scalar(xT[:, BLK:TOK], HI[0:C, :], norm[:, 2:3], norm[:, 3:4], ALU.mult, ALU.add)\
                   .then_inc(r0["hi_drained"], 1)
                dve.wait_ge(r0["y_filled"], by + 2)
                dve.wait_ge(biased, bb + 2)
                dve.tensor_tensor(x1[:, :, :], xb[:, :, :], YB.rearrange("p (t c) -> p t c", t=NT), ALU.add)\
                   .then_inc(r0["y_drained"], 1)
                dve.wait_ge(r0["y_drained"], by + 2)
                layernorm(x1[:, :, :], ln0, bln, 2 * LN, brs + 3, normed, twice=True)
                dve.tensor_tensor(x2[:, bass.ds(img * NT, NT), :], x1[:, :, :], rows(bu1[:, :]), ALU.add)\
                   .then_inc(biased, 2)
                for blk, (which, bank) in enumerate((("lo", LO), ("hi", HI))):
                    dve.wait_ge(input_high, dve.snap(img * NB) + (blk + 1))
                    low = aS[C:P, bass.ds(img * TOK + blk * BLK, BLK)]
                    dve.tensor_tensor(low, bank[C:P, :], low, ALU.subtract).then_inc(r0[which + "_drained"], 1)
                cnt[0] += 1
                assert cnt[0] == N0["hi"]
            dve.wait_ge(biased, 4 * B)

            def low_part(n, base):
                what, lane, blk = PIECES[n]
                bank = PS[:, n % 4, :]
                dve.wait_ge(piece_high, base + (n + 1))
                toks = slice(blk * BLK, (blk + 1) * BLK)
                if what == "v":
                    half = QT // 2
                    ins = dve.tensor_copy(V[:, blk * QT + half:(blk + 1) * QT, :],
                                          bank[:, half * P:].rearrange("p (t c) -> p t c", t=half))
                elif what == "k":
                    low = kS[C:P, lane, toks]
                    ins = dve.scalar_tensor_tensor(low, bank[C:P, :], C ** -0.25, low, ALU.mult, ALU.subtract)
                else:
                    ins = dve.scalar_tensor_tensor(qS[:, 1, lane, toks], bank, C ** -0.25, qS[:, 0, lane, toks],
                                                   ALU.mult, ALU.subtract)
                ins.then_inc(piece_drained, 1)

            for n in range(NPC):
                low_part(n, 0)

            def glob_pair(pair, last):
                base = lambda k: pair * k if last else dve.snap(pair * k)
                bp = None if last else dve.snap(pair * NPC + NPC)
                bw = base(3 * 2 * B)

                def y_out(g, bg):
                    dve.reciprocal(weight[:, g], sums[:, g]).then_inc(weighed, 1)
                    dve.wait_ge(c1["y_filled"], bg + (g + 1))
                    dve.wait_ge(weighed, bw + (3 * g + 1))
                    dve.tensor_tensor(yw[:, :, :, :], YB.rearrange("p (t l c) -> p t l c", t=QT, l=2),
                                      weight[:, g].rearrange("p t (l o) -> p t l o", o=1).to_broadcast([P, QT, 2, C]),
                                      ALU.mult).then_inc(c1["y_drained"], 1)
                    part = x2[:, g * QT:(g + 1) * QT, :]
                    dve.wait_ge(c1["y_drained"], bg + (g + 1))
                    dve.tensor_tensor(part, part, yw[:, :, 0, :], ALU.add).then_inc(weighed, 1)
                    dve.wait_ge(weighed, bw + (3 * g + 2))
                    dve.tensor_tensor(part, part, yw[:, :, 1, :], ALU.add).then_inc(weighed, 1)

                def tail(i):
                    for n in pieces_of_step(i):
                        low_part(n, bp)

                dve_attention(dve, c1, base, 2 * B, False, y_out, None if last else tail)

            with dve.Fori(0, NPAIR - 1) as pair:
                glob_pair(pair, False)
            glob_pair(NPAIR - 1, True)

            dve.wait_ge(weighed, 3 * NPAIR * 2 * B)
            for img in range(B):
                if img:
                    dve.wait_ge(r3["hi_filled"], 1)
                layernorm(x2[:, img * NT:(img + 1) * NT, :], ln3, 0, img * LN, 3 * B + img + 1, normed3)
                dve.wait_ge(r3["hi_filled"], img + 1)
                dve.tensor_copy(aT[:, (2 * img + 1) * BLK:(2 * img + 2) * BLK], HI[0:C, :])\
                   .then_inc(r3["hi_drained"], 1)

            cn = [0]

            def link(ins):
                cn[0] += 1
                ins.then_inc(codes_made, 1)
                dve.wait_ge(codes_made, cn[0])
            dve.wait_ge(late_loaded, 32)
            dve.wait_ge(consts_made, 2)
            link(dve.tensor_copy(codes[:, :, :], mask8[:, 0, :, :]))
            link(dve.tensor_copy(codew[:, :, :], mask8[:, 1, :, :]))
            link(dve.scalar_tensor_tensor(codes[:, :, :], codes[:, :, :], 2.0, codew[:, :, :], ALU.mult, ALU.add))
            link(dve.memset(nextf[:, :], -4.0))

            def choose(now):
                base = now * NCTL
                n = [0]

                def link(ins):
                    n[0] += 1
                    ins.then_inc(ctl_chain, 1)
                    dve.wait_ge(ctl_chain, base + n[0])
                dve.wait_ge(row_turned, now + 1)
                link(dve.tensor_copy(row[:, :], YB[0:1, 0:C]))
                link(dve.tensor_reduce(top[:, :], row[:, 0:NOPS], AX.X, ALU.max))
                link(dve.tensor_scalar(cand[:, :], row[:, 0:NOPS], top[:, 0:1], 64.0, ALU.is_lt, ALU.mult))
                link(dve.tensor_tensor(cand[:, :], cand[:, :], opnum[:, :], ALU.add))
                link(dve.tensor_reduce(opf[:, :], cand[:, :], AX.X, ALU.min))
                link(dve.tensor_scalar(hit[:, :], opnum[:, :], opf[:, 0:1], None, ALU.is_equal))
                link(dve.tensor_tensor(codew[:, :, :], codes[:, :, :],
                                       hit[:, :].rearrange("p (o n) -> p o n", o=1).to_broadcast([1, NSTEP, NOPS]),
                                       ALU.mult))
                link(dve.tensor_reduce(code[:, :], codew[:, :, :], AX.X, ALU.add))
                link(dve.tensor_scalar(dead[:, :], steps4[:, :], nextf[:, 0:1], float(NONE), ALU.is_le, ALU.mult))
                link(dve.tensor_scalar(key[:, :], code[:, :], 0.0, float(NONE), ALU.is_equal, ALU.mult))
                link(dve.tensor_tensor(key[:, :], key[:, :], dead[:, :], ALU.max))
                link(dve.tensor_tensor(code[:, :], code[:, :], steps4[:, :], ALU.add))
                link(dve.tensor_tensor(key[:, :], key[:, :], code[:, :], ALU.max))
                link(dve.tensor_reduce(nextf[:, :], key[:, :], AX.X, ALU.min))
                assert n[0] == NCTL
                dve.tensor_copy(control[:, bass.ds(now, 1), 1:2], opf[:, :].rearrange("p (a b) -> p a b", a=1))
                dve.tensor_copy(control[:, bass.ds(now, 1), 0:1], nextf[:, :].rearrange("p (a b) -> p a b", a=1))\
                   .then_inc(control_ready, 1)

            choose(0)

            def attend(na, step, slot):
                base = lambda k: dve.snap(na * k)
                bhi, by = base(N2["hi"]), base(N2["y"])
                for n, (dst, sc) in enumerate(((qT, C ** -0.5), (kT, 1.0))):
                    dve.wait_ge(r2["hi_filled"], bhi + (n + 1))
                    dve.tensor_scalar(dst[:, BLK:2 * BLK], HI, sc, None, ALU.mult).then_inc(r2["hi_drained"], 1)
                dve.wait_ge(r2["hi_filled"], bhi + 3)
                dve.tensor_copy(V[:, QT:2 * QT, :], HI.rearrange("p (t c) -> p t c", t=QT))\
                   .then_inc(r2["hi_drained"], 1)

                def y_out(g, bg):
                    for lane in range(2):
                        dve.wait_ge(c2["y_filled"], by + (2 * g + lane + 1))
                        dve.tensor_copy(aT[:, lane * TOK + g * BLK:lane * TOK + (g + 1) * BLK], YB[0:C, :])\
                           .then_inc(c2["y_drained"], 1)
                dve_attention(dve, c2, base, 2, True, y_out)

            def feed(nf, step, slot):
                bhi = dve.snap(nf * NF["hi"])
                dve.wait_ge(ffn_loaded, dve.snap(nf * 64) + 64)
                n = 0
                for blk in range(B * NB):
                    n += 1
                    dve.wait_ge(rf["hi_filled"], bhi + n)
                    dve.tensor_scalar(Z[:, 1, blk * BLK:(blk + 1) * BLK], HI, b1s[:, 1:2], 0.0, ALU.add, ALU.max)\
                       .then_inc(rf["hi_drained"], 1)
                for blk in (1, 3):
                    n += 1
                    dve.wait_ge(rf["hi_filled"], bhi + n)
                    dve.tensor_scalar(aT[:, blk * BLK:(blk + 1) * BLK], HI[0:C, :], b2s[:, 0:1], None, ALU.add)\
                       .then_inc(rf["hi_drained"], 1)

            scan(dve, attend, feed, choose)

            for blk in range(B * NB):
                which, bank = (("lo", LO), ("hi", HI))[blk % 2]
                dve.wait_ge(re[which + "_filled"], blk // 2 + 1)
                part = x2[:, blk * QT:(blk + 1) * QT, :]
                dve.tensor_tensor(part, part, bank[:, 0:QT * C].rearrange("p (t c) -> p t c", t=QT), ALU.add)\
                   .then_inc(re[which + "_drained"], 1)

        @block.sync
        def _(sp):
            x_tok = a["x"].rearrange("b i j c -> (b i j) c").rearrange("(g p) c -> p g c", p=P)
            sp.dma_start(xall[:, :, :], x_tok).then_inc(x_loaded, 16)
            loads = 0

            def load(dst, src, **kw):
                sp.dma_start(dst, src, **kw).then_inc(w_loaded, 16)

            qkv = a["L0_conv_qkv_w"]
            load(rpbT[:, :], a["L0_conv_rpb"].rearrange("h r c -> c (h r)"), allow_slow_non_contiguous=True)
            load(wv0[:, :], qkv[:, 2 * C:3 * C])
            sp.wait_ge(zeroed, 1)
            for n, dst in enumerate((wq0, wk0)):
                load(dst[:, :, 0:HD0], qkv[:, n * C:(n + 1) * C].rearrange("c (h d) -> c h d", h=NH0))
            for h in range(NH0):
                load(pw0[32 * h:32 * h + HD0, :], a["L0_conv_proj_w"][h * HD0:(h + 1) * HD0, :])
            for dst, src in ((bv0, a["L0_conv_qkv_b"][2 * C:3 * C]), (pb0, a["L0_conv_proj_b"]),
                             (fb2, a["L0_conv_fc2_b"]), (bu1, a["L1_attn_bu"])):
                load(dst[:, :], src.rearrange("(o c) -> o c", o=1).to_broadcast([P, C]))
            load(fc1[:, :], a["L0_conv_fc1_w"])
            load(fc2[:, :, :], a["L0_conv_fc2_w"].rearrange("(h p) c -> p h c", p=P))
            sp.dma_start(mask8[:, 0, :, :], a["L1_ffn_attn_mask"].rearrange("(o s) n -> o s n", o=1)).then_inc(late_loaded, 16)
            sp.dma_start(mask8[:, 1, :, :], a["L1_ffn_ffn_mask"].rearrange("(o s) n -> o s n", o=1)).then_inc(late_loaded, 16)

            for n, name in enumerate(("L1_attn_Wq", "L1_attn_Wk", "L1_attn_Wv")):
                for part in range(2):
                    sp.dma_start(w1[part * C:(part + 1) * C, n].rearrange("p h c -> p (h c)"), a[name])\
                      .then_inc(weights_loaded, 16)
            for lane in range(2):
                sp.dma_start(wu1[lane * C:(lane + 1) * C, :, lane, :],
                             a["L1_attn_Wu"].rearrange("(n l p) c -> l p n c", l=2, p=C)[lane])\
                  .then_inc(weights_loaded, 16)

            def of(step, slot):
                n = sp.value_load(control[0:1, bass.ds(slot, 1), 1:2], min_val=0, max_val=NOPS - 1)
                return lambda name: a["L1_ffn_" + name][bass.ds(step, 1), bass.ds(n, 1)]

            def attend(na, step, slot):
                w = of(step, slot)
                for dst, name in ((wqs[:, :], "wq"), (wks[:, :], "wk"), (wvs[:, :], "wv"),
                                  (wos[0:C, :], "wo"), (wos[C:P, :], "wo")):
                    sp.dma_start(dst, w(name).rearrange("s n c d -> (s n c) d")).then_inc(attn_loaded, 16)

            def feed(nf, step, slot):
                w = of(step, slot)
                sp.dma_start(w1s[:, :], w("ffn_w1").rearrange("s n c d -> (s n c) d")).then_inc(ffn_loaded, 16)
                sp.dma_start(w2s[:, :, :], w("ffn_w2").rearrange("s n (h p) c -> p (s n h) c", p=P))\
                  .then_inc(ffn_loaded, 16)
                sp.dma_start(b1s[:, :], w("ffn_b1").rearrange("s n (h p) -> p (s n h)", p=P),
                             allow_slow_non_contiguous=True).then_inc(ffn_loaded, 16)
                sp.dma_start(b2s[:, :], w("ffn_b2").rearrange("s n (c o) -> (s n c) o", o=1)).then_inc(ffn_loaded, 16)
            scan(sp, attend, feed, None)

            out_tok = out.rearrange("b i j c -> (b i j) c").rearrange("(g p) c -> p g c", p=P)
            for blk in range(B * NB):
                which = ("lo", "hi")[blk % 2]
                sp.wait_ge(re[which + "_drained"], blk // 2 + 1)
                sp.dma_start(out_tok[:, blk * QT:(blk + 1) * QT, :], x2[:, blk * QT:(blk + 1) * QT, :])\
                  .then_inc(stored, 16)
            sp.wait_ge(stored, 16 * B * NB)


def kernel(**inputs):
    import numpy as _np
    import concourse.bacc as _bacc
    from concourse import mybir as _mybir
    from concourse.bass_utils import run_bass_kernel_spmd as _run

    nc = _bacc.Bacc("TRN2", target_bir_lowering=False, num_devices=1)
    arrays, args = {}, {}
    for name in inputs:
        v = _np.ascontiguousarray(inputs[name])
        arrays[f"in_{name}_dram"] = v
        args[name] = nc.dram_tensor(f"in_{name}_dram", v.shape, _mybir.dt.from_np(v.dtype), kind="ExternalInput").ap()
    out = nc.dram_tensor("out_0_dram", (2, 32, 32, 64), _mybir.dt.float32, kind="ExternalOutput").ap()
    build(nc, args, out)
    r = _run(nc, [arrays], core_ids=[0])
    return r.results[0]["out_0_dram"]
```

```python
from contextlib import ExitStack

import numpy as np

import concourse.bass as bass
from concourse import mybir

F32 = mybir.dt.float32
F16 = mybir.dt.float16
I32 = mybir.dt.int32
U8 = mybir.dt.uint8
ALU = mybir.AluOpType
ACT = mybir.ActivationFunctionType
AX = mybir.AxisListType

P = 128
B, HH, WW, C = 2, 32, 32, 64
TOK = HH * WW
NT = TOK // P
BLK = 512
NB = TOK // BLK
EPS = 1e-5
NEG = -1e30

NH0, WIN = 4, 7
HD0 = C // NH0
ROWS = P // WW
REL = 2 * WIN - 1
HID = 4 * C
NTILE = B * NT
UN0 = NTILE * NH0

NH1 = 8
NPAIR = NH1 // 2
GRP = 8
QT = BLK // P

NSTEP, NOPS = 33, 19
FH = 256
NONE = 4 * 64
LN = 6
ROUNDS = (3, 3, 4)
NCTL = 12

QKV_LOADS = 16 * (2 + 2)
W_LOADS = 16 * (3 + 9)


def window_keys(t):
    first = min(max(ROWS * t - WIN // 2, 0), HH - WIN)
    last = min(max(ROWS * t + ROWS - 1 - WIN // 2, 0), HH - WIN) + WIN - 1
    return first, last - first + 1, (0 if t == 0 else 2 if t == NT - 1 else 1)


def key_chunks(t):
    first, rows, kind = window_keys(t)
    at, n = first * WW, rows * WW
    out = []
    while n > 0:
        k = min(P, n)
        slot = NT + at // P if kind == 0 else (at - WW) // P
        out.append((at, k, slot))
        at, n = at + k, n - k
    return out


VTILES = [(WW + P * j, min(P, TOK - WW - P * j)) for j in range(NT)] + [(0, P), (P, 3 * WW)]

LAG_SUM, LAG_DRAIN, LAG_PROJ = 6, 7, 8

LAG_PV, LAG_OUT, LAG_Y, LAG_YD = 10, 18, 19, 22


def build(nc, a, out):
    ctx = ExitStack()
    with ctx:
        def sb(name, shape, dt=F32):
            return ctx.enter_context(nc.sbuf_tensor(name, shape, dt))

        def sem(name):
            return ctx.enter_context(nc.semaphore(name))

        PS = ctx.enter_context(nc.psum_tensor("PS", [P, 8, 512], F32))
        LO, HI, OB, YB = PS[:, 4, :], PS[:, 5, :], PS[:, 6, :], PS[:, 7, :]

        ident = sb("ident", [P, P])
        shift = sb("shift", [REL, 2, WW])
        colmask = sb("colmask", [WW, WW])
        steps4 = sb("steps4", [1, NSTEP])
        opfrac = sb("opfrac", [1, NOPS])

        wqkv = sb("wqkv", [C + 1, 3, C])
        wqk0 = sb("wqk0", [C + 1, 2, NH0, 2, HD0])
        low_rows = sb("low_rows", [P, 1])
        norm = sb("norm", [C, 4])
        rpbT = sb("rpbT", [REL, NH0 * REL])
        pw0 = sb("pw0", [P, C])
        pb0 = sb("pb0", [P, C])
        fc1 = sb("fc1", [C, HID])
        fb1 = sb("fb1", [P, 2])
        fc2 = sb("fc2", [P, 2, C])
        fb2 = sb("fb2", [P, C])
        bu1 = sb("bu1", [P, C])
        wu1 = sb("wu1", [P, NPAIR, 2, C])
        w1 = sb("w1", [P, 3, NH1, C])
        wqk = sb("wqk", [P, 2, 2, NH1, 2, C], F16)
        wv1 = sb("wv1", [P, 2, NH1 * C], F16)

        xall = sb("xall", [P, B * NT, C])
        x2 = sb("x2", [P, B * NT, C])
        xn = sb("xn", [P, 2, NT, C])
        xsq = sb("xsq", [P, NT, C])
        mean = sb("mean", [P, NT])
        var = sb("var", [P, NT])
        rstd = sb("rstd", [P, NT])
        minus_half = sb("minus_half", [P, NT])
        xb = sb("xb", [P, B * NT, C])
        q0S = sb("q0S", [P, B, 2, TOK], F16)
        k0S = sb("k0S", [P, B, TOK], F16)
        OT0 = sb("OT0", [P, 2, P])
        aS = sb("aS", [P, B * TOK], F16)
        aT = sb("aT", [C, B * TOK])
        prob = sb("prob", [P, 4, TOK])
        negm = sb("negm", [P, 4])
        maxp = sb("maxp", [P, 4])
        sbias = sb("sbias", [P, 3, (WIN + ROWS - 1) * WW])
        rsum = sb("rsum", [P, 4])
        rinv = sb("rinv", [P, 4])
        V = sb("V", [P, B * NT, P])
        PT = sb("PT", [P, 2, 2, NT, BLK])
        OT = sb("OT", [P, 2, BLK])
        qS = sb("qS", [P, 2, 2, B * TOK], F16)
        kS = sb("kS", [P, 2, B * TOK], F16)
        sums = sb("sums", [P, 2 * B, QT, 2])
        weight = sb("weight", [P, 2 * B, QT, 2])
        yw = sb("yw", [P, QT, 2, C])

        mask8 = sb("mask8", [1, 2, NSTEP, NOPS], U8)
        codes = sb("codes", [1, NSTEP, NOPS])
        codew = sb("codew", [1, NSTEP, NOPS])
        code = sb("code", [1, NSTEP])
        key = sb("key", [1, NSTEP])
        dead = sb("dead", [1, NSTEP])
        row = sb("row", [1, C])
        top = sb("top", [1, 1])
        cand = sb("cand", [1, NOPS])
        opf = sb("opf", [1, 1])
        nextf = sb("nextf", [1, 1])
        count_i = sb("count_i", [1, NSTEP], I32)
        control = sb("control", [1, NSTEP + 1, 2], I32)
        ws = sb("ws", [C, 3, C])
        wsS = sb("wsS", [P, 2, 3, 2, C], F16)
        wos = sb("wos", [P, C])
        w1s = sb("w1s", [C, FH])
        w1S = sb("w1S", [P, 2, FH], F16)
        w2s = sb("w2s", [P, 2, C])
        b1s = sb("b1s", [P, 2])
        b2s = sb("b2s", [P, 1])
        PTrow = PT[:, :, :, :, :].rearrange("p g l k q -> p (g l k q)")
        hS = aS
        Z = PTrow[:, 0:2 * B * TOK].rearrange("p (h t) -> p h t", h=2)
        used = [0]

        def part_of_PT(*shape):
            n, names = int(np.prod(shape)), "abcdef"[:len(shape)]
            used[0] += n
            return PTrow[:, used[0] - n:used[0]].rearrange(
                f"p ({' '.join(names)}) -> p {' '.join(names)}", **dict(zip(names, shape)))
        tall = part_of_PT(NH0 * REL, WW)[0:WW]
        tabs = [part_of_PT(NH0, n, WW) for n in (WIN, WIN + ROWS - 1, WIN)]
        PT0 = part_of_PT(2 * NH0, 3, P)
        used[0] = 2 * NT * BLK
        G0 = part_of_PT(2, TOK)
        xn2 = part_of_PT(NT, 2, C)
        xT = part_of_PT(B, TOK)[0:C + 1]
        V0 = part_of_PT(B, NT + 2, NH0, 32)

        gate = sem("gate")
        x_loaded = [sem(f"x_loaded_{img}") for img in range(B)]
        zeroed = sem("zeroed")
        qkv_loaded = sem("qkv_loaded")
        rpb_loaded = sem("rpb_loaded")
        w_loaded = sem("w_loaded")
        late_loaded = sem("late_loaded")
        ident_made = sem("ident_made")
        ones_made = sem("ones_made")
        pool_chain = sem("pool_chain")
        consts_made = sem("consts_made")
        bias_expanded = sem("bias_expanded")
        bias_masked = sem("bias_masked")
        heads_doubled = sem("heads_doubled")
        tables_made = sem("tables_made")
        last_table_made = sem("last_table_made")
        codes_made = sem("codes_made")
        stored = sem("stored")

        def ring(name):
            return {k: sem(f"{name}_piece_{k}") for k in
                    ("lo_filled", "lo_drained", "hi_filled", "hi_drained")}

        def core(name):
            return {k: sem(f"{name}_{k}") for k in
                    ("scored", "biased", "maxed", "exped", "inverted", "scaled", "lo_turned", "hi_turned",
                     "lo_drained", "hi_drained", "out_summed", "out_drained", "y_filled", "y_drained")}

        c0 = core("nat")
        side_filled = sem("side_filled")
        side_drained = {"act": sem("side_drained_by_scalar"), "dve": sem("side_drained_by_vector")}
        side_high = sem("side_high_made")
        low_rows_made = sem("low_rows_made")
        ln_chain = sem("ln_chain")
        normed = sem("normed")
        biased = sem("nat_residual_biased")
        c1 = core("glob")
        weights_loaded = sem("glob_weights_loaded")
        weights_split = sem("glob_weights_split")
        piece_filled = sem("glob_piece_filled")
        piece_high = sem("glob_piece_high_made")
        piece_drained = sem("glob_piece_drained")
        weighed = sem("glob_weighed")
        r3 = ring("state")
        c2 = core("routed")
        routed_filled = sem("routed_piece_filled")
        routed_high = sem("routed_high_made")
        routed_split = sem("routed_split")
        ffn_high = sem("ffn_high_made")
        ffn_split = sem("ffn_split")
        ffn_out_filled = sem("ffn_out_filled")
        rf = ring("ffn")
        rstd_made = sem("rstd_made")
        control_ready = sem("control_ready")
        ctl_chain = sem("ctl_chain")
        row_turned = sem("row_turned")
        attn_loaded = sem("attn_loaded")
        wo_loaded = sem("wo_loaded")
        ffn_loaded = sem("ffn_loaded")
        re = ring("end")

        scores2 = [PS[:, 2 * k:2 * k + 2, :].rearrange("p a b -> p (a b)") for k in range(2)]

        block = ctx.enter_context(nc.Block())

        N2 = dict(y=B * NB)
        NF = dict(lo=B * NB + 2, hi=B * NB + 2)

        def nat_drain(copy, func, bank, u):
            t = u // NH0 % NT
            chunks = key_chunks(t)
            full = len(chunks) - 1
            k = chunks[-1][1]
            args = (func,) if func is not None else ()
            slot = u % (2 * NH0)
            copy(PT0[:, slot, 0:full, :], bank[:, 0:full * P].rearrange("p (n q) -> p n q", n=full), *args)
            return copy(PT0[0:k, slot, full, :], bank[0:k, full * P:(full + 1) * P], *args)

        SIDE = []

        def plan(img, what, banks, who):
            for n, bank in enumerate(banks):
                SIDE.append(((what, img, n), bank, who[n]))
        for img in range(B):
            plan(img, "x", ((0, 1), (2, 3))[img], ("act", "dve"))
            plan(img, "q", (2, 3), ("dve", "dve"))
            plan(img, "k", ((0, 1), (2, 3))[img], ("dve", "dve"))
            plan(img, "v", (2, 3), ("dve", "dve"))
        for img in range(B):
            b0, b1 = ((2, 3), (6, 7))[img]
            plan(img, "y", (b0, b1), ("act", "dve"))
            plan(img, "h", (b0, b1, b0, b1), ("act",) * 4)
            plan(img, "mlp", (b1,), ("dve",))
            plan(img, "a", (b0, b1), ("dve", "dve"))
        order = {key: n for n, (key, _, _) in enumerate(SIDE)}

        split = [key for key, _, _ in SIDE if key[0] in "qka"]

        def side_bank(key):
            return PS[:, SIDE[order[key]][1], :]

        def side_wait(e, key):
            n = order[key]
            who = SIDE[n][2]
            e.wait_ge(side_drained[who], sum(w == who for _, _, w in SIDE[:n + 1]))

        at_step = {("x", 1): (9, 10), ("q", 1): (12, 13), ("k", 1): (15, 16), ("v", 1): (19, 20),
                   ("y", 0): (47, 48), ("h", 0): (49, 50), ("H", 0): (51, 52), ("mlp", 0): (53, 57),
                   ("a", 0): (65, 66)}
        LN1_STEP = 1
        SUM_STEP = 38
        LN2_STEP, LN3_STEP = SUM_STEP + LN + 1, at_step["mlp", 0][1] + LN + 1

        def scan(e, attend, feed, after):
            word = e.alloc_register("word")
            na = e.alloc_register("attended")
            nf = e.alloc_register("fed")
            nu = e.alloc_register("updates")
            for r in (na, nf, nu):
                e.reg_mov(r, 0)
            e.wait_ge(control_ready, 1)
            e.sem_inc(gate, 1)
            e.reg_load(word, control[0:1, 0:1, 0:1])

            def left():
                return e.snap(word, min_val=0, max_val=2 * NONE) < NONE

            def update():
                now_word = e.snap(word, min_val=0, max_val=4 * NSTEP - 1)
                step = e.snap(now_word // 4)
                flags = e.snap(now_word % 4)
                slot = e.snap(nu, min_val=0, max_val=NSTEP - 1)
                if attend:
                    with e.If(flags >= 2):
                        attend(e.snap(na, min_val=0, max_val=NSTEP - 1), step, slot)
                        e.reg_add(na, na, 1)
                if feed:
                    with e.If(e.snap(flags % 2) == 1):
                        feed(e.snap(nf, min_val=0, max_val=NSTEP - 1), step, slot)
                        e.reg_add(nf, nf, 1)
                e.reg_add(nu, nu, 1)
                now = e.snap(nu, min_val=1, max_val=NSTEP)
                if after:
                    after(now)
                e.wait_ge(control_ready, now + 1)
                e.sem_inc(gate, 1)
                e.reg_load(word, control[0:1, bass.ds(now, 1), 0:1])

            with e.Fori(0, ROUNDS[0]):
                with e.If(left()):
                    with e.Fori(0, ROUNDS[1]):
                        with e.If(left()):
                            with e.Fori(0, ROUNDS[2]):
                                with e.If(left()):
                                    update()

        def bias_table(emit, copy, kind, *args):
            t = (0, 1, NT - 1)[kind]
            first = window_keys(t)[0]
            toff = tall[:, :, :].rearrange("p (h r) c -> p h r c", h=NH0)
            for di in range(ROWS):
                i = ROWS * t + di
                start = min(max(i - WIN // 2, 0), HH - WIN)
                r = start - i + WIN - 1
                part = slice(WW * di, WW * (di + 1))
                emit(di, copy(tabs[kind][part, :, start - first:start - first + WIN, :], toff[:, :, r:r + WIN, :], *args))

        UP, GP = 2 * B * GRP, 2 * B
        TURN, SUM, PROJ = 3, 12, 21
        DRAIN, OUT_DRAIN, Y_DRAIN = 2, 18, 22
        PIECES = []
        for img in range(B):
            PIECES += [(what, lane, img * NB + b) for what in ("k", "q") for lane in range(2) for b in range(NB)]
            PIECES += [("v", None, img * NB + b) for b in range(NB)]
        NPC = len(PIECES)
        HALF = NPC // B
        STATE_STEPS = (2, 4)
        common_steps = [1, 2, 3, 4, 7, 8, 9, 10, 11, 12] + [16, 17, 18, 19, 20, 24, 25, 26, 27, 28]

        N_SPLIT, N_FSPLIT = 4 + HALF, 2 + B * NB

        first_steps = [8, 8, 9, 9, 10, 10, 11, 11, 12, 13] + common_steps[HALF:]
        MLP_STEPS, ADD_STEP, DIVIDE_STEP, INPUT_STEP = 4, 3, 6, 7
        EARLY = 6

        SHARED = sum(t < SUM for t in first_steps)

        def bank_of(pair, m):
            return OB if isinstance(pair, int) and pair == 0 and m < SHARED and m % 2 == 0 else YB

        def steps_of(pair, last):
            steps = first_steps if isinstance(pair, int) and pair == 0 else common_steps
            return steps[:HALF] if last else steps

        def pieces_at(i, pair, last):
            return [m for m, t in enumerate(steps_of(pair, last)) if t == i]

        def pieces_before(i, pair, last):
            return sum(t < i for t in steps_of(pair, last))

        def product(pair, k, e):
            return pair * k if isinstance(pair, int) else e.snap(pair * k)

        def pe_attention(pe, s, base, ngroups, y_of):
            n = GRP * ngroups
            bu, bg = base(n), base(ngroups)

            def score(u):
                g, lane, qt = u // GRP, u % 2, (u % GRP) // 2
                if u >= 2:
                    pe.wait_ge(s["exped"], bu + (u - 1))
                q0 = (g * QT + qt) * P
                for part in range(2):
                    for j in range(NB):
                        mm = pe.matmul(scores2[u % 2][:, j * BLK:(j + 1) * BLK], qS[:, part, lane, q0:q0 + P],
                                       kS[:, lane, j * BLK:(j + 1) * BLK], start=(part == 0), stop=(part == 1))
                mm.then_inc(s["scored"], 1)

            def turn(u):
                pe.wait_ge(s["scaled"], bu + (u + 1))
                for half, bank, filled, drained in ((0, LO, "lo_turned", "lo_drained"),
                                                    (1, HI, "hi_turned", "hi_drained")):
                    if u >= 1:
                        pe.wait_ge(s[drained], bu + u)
                    for k in range(4):
                        kt = 4 * half + k
                        tr = pe.transpose(bank[:, k * P:(k + 1) * P],
                                          prob[:, u % 3, kt * P:(kt + 1) * P], ident[:, :])
                    tr.then_inc(s[filled], 1)

            def values(g, k):
                if k == 0:
                    pe.wait_ge(s["lo_drained"], bu + GRP * (g + 1))
                    pe.wait_ge(s["hi_drained"], bu + GRP * (g + 1))
                    if g >= 1:
                        pe.wait_ge(s["out_drained"], bg + g)
                for lane in range(2):
                    cols = slice(64 * lane, 64 * lane + 64)
                    mm = pe.matmul(OB[64 * lane:64 * lane + 64, :], V[:, (g // 2) * NT + k, cols],
                                   PT[:, g % 2, lane, k, :], start=(k == 0), stop=(k == NT - 1))
                if k == NT - 1:
                    mm.then_inc(s["out_summed"], 1)

            score(0)
            score(1)
            for i in range(n + LAG_Y + 3):
                if i + 2 < n:
                    score(i + 2)
                if 1 <= i <= n:
                    turn(i - 1)
                for g in range(ngroups):
                    k = i - GRP * g - LAG_PV
                    if 0 <= k < NT - 1:
                        values(g, k)
                    if k == NT - 2:
                        values(g, NT - 1)
                    if i == GRP * g + LAG_Y:
                        pe.wait_ge(s["out_drained"], bg + (g + 1))
                        y_of(g, bg)

        @block.tensor
        def _(pe):
            def fill(key, mms):
                n = order[key]
                before = [m for m in range(n) if SIDE[m][1] == SIDE[n][1]]
                if before:
                    side_wait(pe, SIDE[before[-1]][0])
                mms(side_bank(key)).then_inc(side_filled, 1)

            def turn_norm(what, img, k, twice=False):
                pe.wait_ge(normed, k)
                for blk in range(NB):
                    def tr(bank):
                        for j in range(QT):
                            t = blk * QT + j
                            n, src = (P, xn2[:, t].rearrange("p l c -> p (l c)")) if twice \
                                else (C, xn[:, (k - 1) % 2, t, :])
                            m = pe.transpose(bank[0:n, j * P:(j + 1) * P], src, ident[:, :])
                        return m
                    fill((what, img, blk), tr)

            def queries_keys(what, img):
                w = wqk0[:, "qk".index(what)].rearrange("c h l d -> c (h l d)")
                for blk in range(NB):
                    if what == "q":
                        side_wait(pe, ("x", img, blk))
                    fill((what, img, blk), lambda bank: pe.matmul(
                        bank, w, xT[:, img, blk * BLK:(blk + 1) * BLK],
                        start=True, stop=True))

            def value_tiles(img):
                for n, tiles in enumerate((range(NT), range(NT, NT + 2))):
                    def go(bank):
                        for m, j in enumerate(tiles):
                            t0, k = VTILES[j]
                            mm = pe.matmul(bank[0:k, m * C:(m + 1) * C], xT[:, img, t0:t0 + k], wqkv[:, 2, :],
                                           start=True, stop=True)
                        return mm
                    fill(("v", img, n), go)

            def hidden(img, blk):
                side_wait(pe, ("y", img, blk))
                for half in range(2):
                    fill(("h", img, 2 * blk + half), lambda bank: pe.matmul(
                        bank, fc1[:, half * P:(half + 1) * P], xT[0:C, img, blk * BLK:(blk + 1) * BLK],
                        start=True, stop=True))

            def mlp(img, tiles):
                def go(bank):
                    for t in tiles:
                        for half in range(2):
                            mm = pe.matmul(bank[:, t * C:(t + 1) * C], G0[:, half, t * P:(t + 1) * P],
                                           fc2[:, half, :], start=(half == 0), stop=(half == 1))
                    return mm
                if tiles[0] == 0:
                    side_wait(pe, ("h", img, 3))
                if tiles[-1] == NT - 1:
                    go(side_bank(("mlp", img, 0))).then_inc(side_filled, 1)
                else:
                    go(side_bank(("mlp", img, 0)))

            pe.wait_ge(rpb_loaded, 16)
            pe.wait_ge(consts_made, 1)
            for j in range(WW):
                bank, slot = 4 + j // 9, j % 9
                mm = pe.matmul(PS[0:WW, bank, slot * NH0 * REL:(slot + 1) * NH0 * REL],
                               shift[:, :, :].rearrange("c a m -> c (a m)")[:, WW - 1 - j:2 * WW - 1 - j],
                               rpbT[:, :], start=True, stop=True)
            mm.then_inc(bias_expanded, 1)

            pe.wait_ge(ident_made, 1)
            turn_norm("x", 0, 1)
            pe.wait_ge(heads_doubled, 1)
            pe.wait_ge(ones_made, 1)
            queries_keys("q", 0)
            queries_keys("k", 0)
            value_tiles(0)

            side_wait(pe, ("k", 0, 0))
            side_wait(pe, ("v", 0, 1))
            pe.wait_ge(bias_masked, 1)
            pe.wait_ge(w_loaded, W_LOADS)

            def nat_score(u):
                T, h = u // NH0, u % NH0
                img, t = T // NT, T % NT
                first, rows, kind = window_keys(t)
                if u >= 2:
                    pe.wait_ge(c0["biased"], u - 1)
                if u == UN0 // B:
                    side_wait(pe, ("k", 1, 0))
                    side_wait(pe, ("k", 1, 1))
                hr = slice(32 * h, 32 * h + 32)
                for part in range(2):
                    mm = pe.matmul(PS[:, u % 2, 0:rows * WW], q0S[hr, img, part, t * P:(t + 1) * P],
                                   k0S[hr, img, first * WW:(first + rows) * WW],
                                   start=(part == 0), stop=(part == 1))
                mm.then_inc(c0["scored"], 1)

            def nat_turn(u):
                pe.wait_ge(c0["scaled"], u + 1)
                half = ("lo", "hi")[u % 2]
                bank = (LO, HI)[u % 2]
                if u >= 2:
                    pe.wait_ge(c0[half + "_drained"], u // 2)
                for n, (_, k, _) in enumerate(key_chunks(u // NH0 % NT)):
                    tr = pe.transpose(bank[0:k, n * P:(n + 1) * P], prob[:, u % 3, n * P:n * P + k], ident[:, :])
                tr.then_inc(c0[half + "_turned"], 1)

            def nat_values(T):
                for half in ("lo", "hi"):
                    pe.wait_ge(c0[half + "_drained"], NH0 // 2 * (T + 1))
                if T == NT:
                    side_wait(pe, ("v", 1, 1))
                if T >= 1:
                    pe.wait_ge(c0["out_drained"], T)
                chunks = key_chunks(T % NT)
                for n, (_, k, slot) in enumerate(chunks):
                    for h in range(NH0):
                        mm = pe.matmul(OB[32 * h:32 * h + 32, 0:P], V0[0:k, T // NT, slot, h, :],
                                       PT0[0:k, (T * NH0 + h) % (2 * NH0), n, :],
                                       start=(n == 0), stop=(n == len(chunks) - 1))
                mm.then_inc(c0["out_summed"], 1)

            def nat_project(T):
                if T == NT:
                    pe.wait_ge(c0["y_drained"], 1)
                pe.wait_ge(c0["out_drained"], T + 1)
                t = T % NT
                mm = pe.matmul(YB[:, t * C:(t + 1) * C], OT0[:, T % 2, :], pw0[:, :], start=True, stop=True)
                if t == NT - 1:
                    mm.then_inc(c0["y_filled"], 1)

            nat_score(0)
            nat_score(1)
            for i in range(UN0 + LAG_PROJ - NH0 + 1):
                if i + 2 < UN0:
                    nat_score(i + 2)
                if 1 <= i <= UN0:
                    nat_turn(i - 1)
                if i >= LAG_SUM and (i - LAG_SUM) % NH0 == 0 and (i - LAG_SUM) // NH0 < NTILE:
                    nat_values((i - LAG_SUM) // NH0)
                if i >= LAG_PROJ and (i - LAG_PROJ) % NH0 == 0:
                    nat_project((i - LAG_PROJ) // NH0)
                if i == at_step["x", 1][0]:
                    turn_norm("x", 1, 2)
                if i == at_step["q", 1][0]:
                    queries_keys("q", 1)
                if i == at_step["k", 1][0]:
                    queries_keys("k", 1)
                if i == at_step["v", 1][0]:
                    value_tiles(1)
                if i == at_step["y", 0][0]:
                    turn_norm("y", 0, 3)
                if i == at_step["h", 0][0]:
                    hidden(0, 0)
                if i == at_step["H", 0][0]:
                    hidden(0, 1)
                if 0 <= i - at_step["mlp", 0][0] < NT // 2:
                    mlp(0, range(2 * (i - at_step["mlp", 0][0]), 2 * (i - at_step["mlp", 0][0]) + 2))
                if i == at_step["a", 0][0]:
                    turn_norm("a", 0, 4, twice=True)

            pe.wait_ge(weights_loaded, 16 * 8)
            pe.wait_ge(weights_split, 1)

            def project(pair, n, bank):
                what, lane, blk = PIECES[n]
                if what == "v":
                    for j in range(QT):
                        t = blk * QT + j
                        for part in range(2):
                            m = pe.matmul(bank[:, j * P:(j + 1) * P], aS[:, t * P:(t + 1) * P],
                                          wv1[:, part, bass.ds(pair * P, P)], start=(part == 0), stop=(part == 1))
                else:
                    for part in range(2):
                        w = wqk[:, "qk".index(what), part, bass.ds(pair * 2 + lane, 1), :, :]
                        m = pe.matmul(bank, w.rearrange("p h a c -> p (h a c)"), aS[:, blk * BLK:(blk + 1) * BLK],
                                      start=(part == 0), stop=(part == 1))
                m.then_inc(piece_filled, 1)

            pe.wait_ge(c0["biased"], UN0)
            side_wait(pe, ("a", 0, 1))
            for n in range(HALF):
                if n == EARLY:
                    turn_norm("y", 1, 5)
                if n >= 4:
                    pe.wait_ge(piece_drained, n - 3)
                project(0, n, PS[:, n % 4, :])
            hidden(1, 0)
            hidden(1, 1)

            def rest_of_stage1(i):
                if i < MLP_STEPS:
                    k = NT // MLP_STEPS
                    mlp(1, range(k * i, k * i + k))
                if i == INPUT_STEP:
                    turn_norm("a", 1, 6, twice=True)

            def glob_pair(pair, steps=range(UP), cur=True, prev=True, last=False, beside=None):
                bu, bg, bp = (product(pair, k, pe) for k in (UP, GP, NPC))
                nxt = pair + 1 if isinstance(pair, int) else pe.snap(pair + 1)
                before = pair - 1 if isinstance(pair, int) else pe.snap(pair - 1)

                def live(index):
                    return cur if index >= 0 else prev

                for i in steps:
                    if cur:
                        if i in (0, UP // B):
                            pe.wait_ge(piece_drained, bp + (HALF if i == 0 else NPC))
                            pe.sem_inc(gate, 1)
                        if i >= 2 or prev:
                            pe.wait_ge(c1["exped"], bu + (i - 1))
                        lane, q0, k0 = i % 2, i // 2 * P, i // (UP // B) * TOK
                        for part in range(2):
                            for j in range(NB):
                                mm = pe.matmul(scores2[i % 2][:, j * BLK:(j + 1) * BLK], qS[:, part, lane, q0:q0 + P],
                                               kS[:, lane, k0 + j * BLK:k0 + (j + 1) * BLK],
                                               start=(part == 0), stop=(part == 1))
                        mm.then_inc(c1["scored"], 1)
                    u = i - TURN
                    if live(u):
                        pe.wait_ge(c1["exped"], bu + (u + 1))
                        for half, bank, turned, drained in ((0, LO, "lo_turned", "lo_drained"),
                                                            (1, HI, "hi_turned", "hi_drained")):
                            if u >= 1 or prev:
                                pe.wait_ge(c1[drained], bu + u)
                            for k in range(4):
                                kt = 4 * half + k
                                tr = pe.transpose(bank[:, k * P:(k + 1) * P],
                                                  prob[:, u % 4, kt * P:(kt + 1) * P], ident[:, :])
                            tr.then_inc(c1[turned], 1)
                    g = (i - SUM) // GRP
                    k = i - SUM - GRP * g
                    if live(g) and k < NT - 1:
                        if k == 0:
                            pe.wait_ge(c1["lo_drained"], bu + GRP * (g + 1))
                            pe.wait_ge(c1["hi_drained"], bu + GRP * (g + 1))
                            if g >= 1 or prev:
                                pe.wait_ge(c1["out_drained"], bg + g)
                            else:
                                pe.wait_ge(piece_drained, HALF + SHARED)
                        for kt in (k, k + 1)[:2 if k == NT - 2 else 1]:
                            for lane in range(2):
                                cols = slice(64 * lane, 64 * lane + 64)
                                mm = pe.matmul(OB[cols, :], V[:, g % GP // 2 * NT + kt, cols],
                                               PT[:, g % 2, lane, kt, :], start=(kt == 0), stop=(kt == NT - 1))
                        if kt == NT - 1:
                            mm.then_inc(c1["out_summed"], 1)
                    for m in pieces_at(i, pair, last) if cur else ():
                        if isinstance(pair, int) and pair == 0 and m == 0:
                            side_wait(pe, ("a", 1, 0))
                            side_wait(pe, ("a", 1, 1))
                        two = isinstance(pair, int) and pair == 0 and 1 <= m < SHARED
                        pe.wait_ge(piece_drained, bp + (HALF + m - 1 if two else HALF + m))
                        g = (i - PROJ - 1) // GRP
                        if not pieces_at(i - 1, pair, last) and live(g):
                            pe.wait_ge(c1["y_drained"], bg + (g + 1))
                        pe.sem_inc(gate, 1)
                        project(pair if m < HALF else nxt, (HALF + m) % NPC, bank_of(pair, m))
                    g = (i - PROJ) // GRP
                    if (i - PROJ) % GRP == 0 and live(g):
                        pe.wait_ge(c1["out_drained"], bg + (g + 1))
                        if cur:
                            pe.wait_ge(piece_drained, bp + (HALF + pieces_before(i, pair, last)))
                        pe.sem_inc(gate, 1)
                        if g >= 1 or prev:
                            pe.wait_ge(c1["y_drained"], bg + g)
                            pe.sem_inc(gate, 1)
                        p = pair if g >= 0 else before
                        for j in range(QT):
                            mm = pe.matmul(YB[:, j * P:(j + 1) * P], OT[:, g % 2, j * P:(j + 1) * P],
                                           wu1[:, bass.ds(p, 1), :, :].rearrange("p n l c -> p (n l c)"),
                                           start=True, stop=True)
                        mm.then_inc(c1["y_filled"], 1)
                    if beside:
                        beside(i)

            glob_pair(0, prev=False, beside=rest_of_stage1)
            with pe.Fori(1, NPAIR - 1) as pair:
                glob_pair(pair)
            glob_pair(NPAIR - 1, last=True)

            def turn_state(blk):
                which, bank = (("lo", PS[:, 0, :]), ("hi", PS[:, 1, :]), ("lo", LO), ("hi", HI))[blk]
                for j in range(QT):
                    m = pe.transpose(bank[0:C, j * P:(j + 1) * P], xn[:, blk // NB, (blk % NB) * QT + j, :], ident[:, :])
                m.then_inc(r3[which + "_filled"], 1)

            def show_row(bank=YB):
                pe.transpose(bank[0:1, 0:C], aT[:, 0:1], ident[0:C, 0:C]).then_inc(row_turned, 1)

            for i in range(PROJ + GRP * (GP - 1) - UP + 1):
                if i == STATE_STEPS[0]:
                    pe.wait_ge(c1["exped"], NPAIR * UP)
                    pe.wait_ge(normed, 3 * B + 1)
                    turn_state(0)
                    turn_state(1)
                if i == STATE_STEPS[1]:
                    pe.wait_ge(r3["lo_drained"], 1)
                    show_row(PS[:, 2, :])
                glob_pair(NPAIR, steps=(i,), cur=False)

            pe.wait_ge(normed, 3 * B + 2)
            turn_state(2)
            turn_state(3)
            def attend(na, step, slot):
                base = lambda k: pe.snap(na * k)
                bp, bf, by = base(N_SPLIT), base(HALF), base(N2["y"])
                for n in range(HALF):
                    if n == 0 or n >= 4:
                        pe.wait_ge(routed_split, bp + (4 if n == 0 else 4 + n - 3))
                        pe.sem_inc(gate, 1)
                    what, lane, blk = PIECES[n]
                    bank = PS[:, n % 4, :]
                    if what == "v":
                        for j in range(QT):
                            for lane in range(2):
                                t0 = lane * TOK + (blk * QT + j) * P
                                for part in range(2):
                                    m = pe.matmul(bank[:, j * P + C * lane:j * P + C * lane + C], hS[:, t0:t0 + P],
                                                  wsS[:, part, 2, 0, :], start=(part == 0), stop=(part == 1))
                    else:
                        t0 = lane * TOK + blk * BLK
                        for part in range(2):
                            w = wsS[:, part, "kq".index(what)].rearrange("p a c -> p (a c)")
                            m = pe.matmul(bank, w, hS[:, t0:t0 + BLK], start=(part == 0), stop=(part == 1))
                    m.then_inc(routed_filled, 1)
                pe.wait_ge(routed_split, bp + N_SPLIT)
                pe.sem_inc(gate, 1)

                def y_of(g, bg):
                    for lane in range(2):
                        n = 2 * g + lane
                        if n == 0:
                            pe.wait_ge(wo_loaded, base(32) + 32)
                        if n:
                            pe.wait_ge(c2["y_drained"], by + n)
                        pe.sem_inc(gate, 1)
                        pe.matmul(YB[0:C, :], wos[64 * lane:64 * lane + 64, :], OT[64 * lane:64 * lane + 64, g % 2, :],
                                  start=True, stop=True).then_inc(c2["y_filled"], 1)

                pe_attention(pe, c2, base, 2, y_of)
                pe.wait_ge(c2["y_drained"], by + 4)
                pe.sem_inc(gate, 1)

            def feed(nf, step, slot):
                base = lambda k: pe.snap(nf * k)
                blo, bhi = base(NF["lo"]), base(NF["hi"])
                bs = base(N_FSPLIT)
                cnt = [0, 0]

                def piece(mms):
                    side = sum(cnt) % 2
                    which, bank, bs = (("lo", LO, blo), ("hi", HI, bhi))[side]
                    if cnt[side]:
                        pe.wait_ge(rf[which + "_drained"], bs + cnt[side])
                        pe.sem_inc(gate, 1)
                    mms(bank).then_inc(rf[which + "_filled"], 1)
                    cnt[side] += 1
                for blk in range(B * NB):
                    pe.wait_ge(ffn_split, bs + (3 + blk))
                    pe.sem_inc(gate, 1)
                    for half in range(2):
                        def go(bank):
                            for part in range(2):
                                m = pe.matmul(bank, w1S[:, part, half * P:(half + 1) * P],
                                              hS[:, blk * BLK:(blk + 1) * BLK], start=(part == 0), stop=(part == 1))
                            return m
                        piece(go)
                pe.wait_ge(rf["lo_drained"], blo + cnt[0])
                pe.wait_ge(rf["hi_drained"], bhi + cnt[1])
                pe.sem_inc(gate, 1)
                for two, bank in enumerate((LO, HI)):
                    for half in range(2):
                        for n in range(2):
                            blk = 2 * two + n
                            m = pe.matmul(bank[n * C:(n + 1) * C, :], w2s[:, half, :],
                                          Z[:, half, blk * BLK:(blk + 1) * BLK], start=(half == 0), stop=(half == 1))
                    m.then_inc(ffn_out_filled, 1)
                pe.wait_ge(rf["lo_drained"], blo + NF["lo"])
                pe.wait_ge(rf["hi_drained"], bhi + NF["hi"])
                pe.sem_inc(gate, 1)

            scan(pe, attend, feed, lambda now: show_row())

            for blk in range(B * NB):
                which, bank = (("lo", LO), ("hi", HI))[blk % 2]
                if blk >= 2:
                    pe.wait_ge(re[which + "_drained"], blk // 2)
                for j in range(QT):
                    t = blk * QT + j
                    m = pe.transpose(bank[:, j * C:(j + 1) * C], aT[:, t * P:(t + 1) * P], ident[0:C, 0:C])
                m.then_inc(re[which + "_filled"], 1)

        def act_attention(act, s, base, ngroups):
            n = GRP * ngroups
            bu, bg = base(n), base(ngroups)
            for i in range(n + LAG_YD):
                if i < n:
                    act.wait_ge(s["maxed"], bu + (i + 1))
                    if i >= 3:
                        act.wait_ge(s["hi_turned"], bu + (i - 2))
                    act.activation(prob[:, i % 3, :], scores2[i % 2], ACT.Exp, bias=negm[:, i % 4:i % 4 + 1],
                                   scale=1.0, accum_out=rsum[:, i % 4:i % 4 + 1]).then_inc(s["exped"], 1)
                u = i - 2
                if 0 <= u < n:
                    g, lane, qt = u // GRP, u % 2, (u % GRP) // 2
                    act.wait_ge(s["lo_turned"], bu + (u + 1))
                    act.activation(PT[:, g % 2, lane, 0:4, qt * P:(qt + 1) * P],
                                   LO.rearrange("p (k q) -> p k q", k=4), ACT.Copy).then_inc(s["lo_drained"], 1)
                for g in range(ngroups):
                    if i == GRP * g + LAG_OUT:
                        act.wait_ge(s["out_summed"], bg + (g + 1))
                        act.activation(OT[:, g % 2, :], OB, ACT.Copy).then_inc(s["out_drained"], 1)

        @block.scalar
        def _(act):
            def column(name):
                return a[name].rearrange("(c o) -> c o", o=1)
            act.dma_start(rpbT[:, :], a["L0_conv_rpb"].rearrange("h r c -> c (h r)"), allow_slow_non_contiguous=True)\
               .then_inc(rpb_loaded, 16)
            act.dma_start(norm[:, 0:1], column("L0_conv_norm1_g")).then_inc(qkv_loaded, 16)
            act.dma_start(norm[:, 1:2], column("L0_conv_norm1_b")).then_inc(qkv_loaded, 16)
            act.dma_start(norm[:, 2:3], column("L0_conv_norm2_g")).then_inc(w_loaded, 16)
            act.dma_start(norm[:, 3:4], column("L0_conv_norm2_b")).then_inc(w_loaded, 16)
            act.dma_start(fb1[:, :], a["L0_conv_fc1_b"].rearrange("(h p) -> p h", p=P),
                          allow_slow_non_contiguous=True).then_inc(w_loaded, 16)
            act.wait_ge(qkv_loaded, QKV_LOADS)
            for n, sc in enumerate((HD0 ** -0.5, 1.0)):
                ins = act.activation(wqk0[:, n], wqkv[:, n].rearrange("c (h o d) -> c h o d", h=NH0, o=1)
                                     .to_broadcast([C + 1, NH0, 2, HD0]), ACT.Copy, scale=sc)
            ins.then_inc(heads_doubled, 1)

            def drain(key, out, func, **kw):
                act.wait_ge(side_filled, order[key] + 1)
                n = out.shape[0]
                ins = act.activation(out, side_bank(key)[0:n, :], func, **kw)
                ins.then_inc(*((side_high, 1) if key in split else (side_drained["act"], 1)))

            def drain_x(img, what, col):
                drain((what, img, 0), xT[0:C, img, 0:BLK], ACT.Identity, scale=norm[:, col:col + 1],
                      bias=norm[:, col + 1:col + 2])

            def drain_q(img):
                for blk in range(NB):
                    drain(("q", img, blk), q0S[:, img, 0, blk * BLK:(blk + 1) * BLK], ACT.Copy)

            def drain_k(img):
                for blk in range(NB):
                    drain(("k", img, blk), k0S[:, img, blk * BLK:(blk + 1) * BLK], ACT.Copy)

            def drain_h(img, blk):
                for half in range(2):
                    drain(("h", img, 2 * blk + half), G0[:, half, blk * BLK:(blk + 1) * BLK], ACT.Gelu,
                          bias=fb1[:, half:half + 1], scale=1.0)

            def drain_a(img):
                for blk in range(NB):
                    t0 = img * TOK + blk * BLK
                    drain(("a", img, blk), aS[:, t0:t0 + BLK], ACT.Copy)

            drain_x(0, "x", 0)
            act.wait_ge(bias_masked, 1)
            bias_table(lambda di, ins: ins.then_inc(tables_made, 1), act.activation, 0, ACT.Copy)
            drain_q(0)
            drain_k(0)
            bias_table(lambda di, ins: ins.then_inc(last_table_made, 1), act.activation, 2, ACT.Copy)

            for i in range(UN0 + LAG_DRAIN - NH0 + 1):
                if i < UN0:
                    w = window_keys(i // NH0 % NT)[1] * WW
                    act.wait_ge(c0["maxed"], i + 1)
                    if i >= 3:
                        j = i - 3
                        act.wait_ge(c0[("lo", "hi")[j % 2] + "_turned"], j // 2 + 1)
                    act.activation(prob[:, i % 3, 0:w], sbias[:, i % 3, 0:w], ACT.Exp,
                                   bias=negm[:, i % 4:i % 4 + 1], scale=1.0,
                                   accum_out=rsum[:, i % 4:i % 4 + 1]).then_inc(c0["exped"], 1)
                u = i - 2
                if 0 <= u < UN0 and u % 2 == 0:
                    act.wait_ge(c0["lo_turned"], u // 2 + 1)
                    nat_drain(act.activation, ACT.Copy, LO, u).then_inc(c0["lo_drained"], 1)
                if i >= LAG_DRAIN and (i - LAG_DRAIN) % NH0 == 0:
                    T = (i - LAG_DRAIN) // NH0
                    act.wait_ge(c0["out_summed"], T + 1)
                    act.activation(OT0[:, T % 2, :], OB[:, 0:P], ACT.Copy).then_inc(c0["out_drained"], 1)
                if i == at_step["x", 1][1]:
                    drain_x(1, "x", 0)
                if i == at_step["q", 1][1]:
                    drain_q(1)
                if i == at_step["k", 1][1]:
                    drain_k(1)
                if i == at_step["y", 0][1]:
                    drain_x(0, "y", 2)
                if i == at_step["h", 0][1]:
                    drain_h(0, 0)
                if i == at_step["H", 0][1]:
                    drain_h(0, 1)
                if i == at_step["a", 0][1]:
                    drain_a(0)

            def high_part(n, bank, scales=(C ** -0.25, C ** -0.25), made=piece_high):
                what, lane, blk = PIECES[n]
                if what == "v":
                    half = QT // 2
                    ins = act.activation(V[:, blk * QT:blk * QT + half, :],
                                         bank[:, 0:half * P].rearrange("p (t c) -> p t c", t=half), ACT.Copy)
                else:
                    dst = kS[:, lane] if what == "k" else qS[:, 0, lane]
                    ins = act.activation(dst[:, blk * BLK:(blk + 1) * BLK], bank, ACT.Copy,
                                         scale=scales["kq".index(what)])
                ins.then_inc(made, 1)

            for n in range(HALF):
                if n == EARLY:
                    drain_x(1, "y", 2)
                act.wait_ge(piece_filled, n + 1)
                high_part(n, PS[:, n % 4, :])
            drain_h(1, 0)
            drain_h(1, 1)

            def rest_of_stage1(i):
                if i == INPUT_STEP:
                    drain_a(1)

            def glob_pair(pair, steps=range(UP), cur=True, prev=True, last=False, beside=None):
                bu, bg, bp = (product(pair, k, act) for k in (UP, GP, NPC))

                def live(index):
                    return cur if index >= 0 else prev

                for i in steps:
                    if cur:
                        act.wait_ge(c1["maxed"], bu + (i + 1))
                        if i >= 4 or prev:
                            act.wait_ge(c1["hi_turned"], bu + (i - 3))
                        act.activation(prob[:, i % 4, :], scores2[i % 2], ACT.Exp, bias=negm[:, i % 4:i % 4 + 1],
                                       scale=1.0, accum_out=sums[:, i // GRP, (i % GRP) // 2, i % 2:i % 2 + 1])\
                           .then_inc(c1["exped"], 1)
                    for m in pieces_at(i, pair, last) if cur else ():
                        act.wait_ge(piece_filled, bp + (HALF + m + 1))
                        high_part((HALF + m) % NPC, bank_of(pair, m))
                    if beside:
                        beside(i)
                    u = i - DRAIN
                    if live(u):
                        g, lane, qt = u // GRP, u % 2, (u % GRP) // 2
                        act.wait_ge(c1["lo_turned"], bu + (u + 1))
                        act.activation(PT[:, g % 2, lane, 0:4, qt * P:(qt + 1) * P],
                                       LO.rearrange("p (k q) -> p k q", k=4), ACT.Copy).then_inc(c1["lo_drained"], 1)
                    g = (i - OUT_DRAIN) // GRP
                    if (i - OUT_DRAIN) % GRP == 0 and live(g):
                        act.wait_ge(c1["out_summed"], bg + (g + 1))
                        act.activation(OT[:, g % 2, :], OB, ACT.Copy).then_inc(c1["out_drained"], 1)

            glob_pair(0, prev=False, beside=rest_of_stage1)
            with act.Fori(1, NPAIR - 1) as pair:
                glob_pair(pair)
            glob_pair(NPAIR - 1, last=True)

            def drain_state(img, bank):
                act.wait_ge(r3["lo_filled"], img + 1)
                act.activation(aT[:, img * TOK:img * TOK + BLK], bank[0:C, :], ACT.Copy).then_inc(r3["lo_drained"], 1)
            for i in range(OUT_DRAIN + GRP * (GP - 1) - UP + 1):
                glob_pair(NPAIR, steps=(i,), cur=False)
                if i == STATE_STEPS[0]:
                    drain_state(0, PS[:, 0, :])
            drain_state(1, LO)

            def high_state(made, pieces):
                size = B * TOK // pieces
                act.wait_ge(r3["lo_drained"], B)
                act.wait_ge(r3["hi_drained"], B)
                for n in range(pieces):
                    toks = slice(n * size, (n + 1) * size)
                    act.activation(hS[0:C, toks], aT[:, toks], ACT.Copy).then_inc(made, 1)

            def attend(na, step, slot):
                base = lambda k: act.snap(na * k)
                high_state(routed_high, 2)
                act.wait_ge(attn_loaded, base(48) + 48)
                twice = ws[:, :, :].rearrange("c n (o d) -> c n o d", o=1).to_broadcast([C, 3, 2, C])
                for rows in (slice(0, C), slice(C, P)):
                    act.activation(wsS[rows, 0], twice, ACT.Copy).then_inc(routed_high, 1)
                for n in range(HALF):
                    act.wait_ge(routed_filled, base(HALF) + (n + 1))
                    high_part(n, PS[:, n % 4, :], (1.0, C ** -0.5), routed_high)
                act_attention(act, c2, base, 2)
                act.wait_ge(c2["y_drained"], base(N2["y"]) + N2["y"])

            def feed(nf, step, slot):
                blo = act.snap(nf * (B * NB))
                act.wait_ge(ffn_loaded, act.snap(nf * 80) + 80)
                for rows in (slice(0, C), slice(C, P)):
                    act.activation(w1S[rows, 0], w1s[:, :], ACT.Copy).then_inc(ffn_high, 1)
                high_state(ffn_high, B * NB)
                n = 0
                for blk in range(B * NB):
                    n += 1
                    act.wait_ge(rf["lo_filled"], blo + n)
                    act.activation(Z[:, 0, blk * BLK:(blk + 1) * BLK], LO, ACT.Relu, bias=b1s[:, 0:1], scale=1.0)\
                       .then_inc(rf["lo_drained"], 1)
                for two, bank in enumerate((LO, HI)):
                    act.wait_ge(ffn_out_filled, act.snap(nf * 2) + (two + 1))
                    act.activation(aT[:, 2 * two * BLK:(2 * two + 1) * BLK], bank[0:C, :], ACT.Identity,
                                   bias=b2s[0:C, 0:1], scale=1.0).then_inc(rf["lo_drained"], 1)

            scan(act, attend, feed, None)

        @block.gpsimd
        def _(pool):
            chain = [0]

            def link(ins):
                chain[0] += 1
                ins.then_inc(pool_chain, 1)
                pool.wait_ge(pool_chain, chain[0])

            link(pool.memset(pw0[:, :], 0.0))
            pool.sem_inc(zeroed, 1)
            link(pool.memset(shift[:, :, :], 0.0))
            for base in (-(WW - 1 + WIN - 1), 1 - (WIN - 1)):
                link(pool.affine_select(out=shift[:, :, :], in_=shift[:, :, :], compare_op=ALU.not_equal, fill=1.0,
                                        base=base, pattern=[[0, 2], [1, WW]], channel_multiplier=1))
            pool.sem_inc(consts_made, 1)
            link(pool.memset(colmask[:, :], 0.0))
            lo = colmask[:, 0:WW - WIN]
            link(pool.affine_select(out=lo, in_=lo, compare_op=ALU.is_ge, fill=NEG, base=WIN // 2,
                                    pattern=[[1, WW - WIN]], channel_multiplier=-1))
            hi = colmask[:, WIN:WW]
            link(pool.affine_select(out=hi, in_=hi, compare_op=ALU.is_ge, fill=NEG, base=WIN // 2 - WIN,
                                    pattern=[[-1, WW - WIN]], channel_multiplier=1))
            link(pool.memset(tabs[1][:, :, :, :], NEG))
            pool.sem_inc(consts_made, 1)
            link(pool.memset(ident[:, :], 0.0))
            link(pool.affine_select(out=ident[:, :], in_=ident[:, :], compare_op=ALU.not_equal, fill=1.0, base=0,
                                    pattern=[[-1, P]], channel_multiplier=1))
            pool.sem_inc(ident_made, 1)
            link(pool.memset(minus_half[:, :], -0.5))
            link(pool.memset(xT[C:C + 1, :, :], 1.0))
            pool.sem_inc(ones_made, 1)

            def power(k):
                pool.wait_ge(ln_chain, k * LN)
                pool.tensor_tensor(rstd[:, :], var[:, :], minus_half[:, :], ALU.pow).then_inc(rstd_made, 1)

            power(1)
            link(pool.memset(V0[:, :, :, :, :], 0.0))
            pool.sem_inc(consts_made, 1)
            power(2)
            link(pool.memset(wu1[:, :, :, :], 0.0))
            pool.sem_inc(zeroed, 1)
            link(pool.iota(count_i[:, :], [[1, NSTEP]], base=0, channel_multiplier=0))
            link(pool.tensor_copy(steps4[:, :], count_i[:, :]))
            link(pool.tensor_copy(opfrac[:, :], count_i[:, 0:NOPS]))
            link(pool.tensor_scalar(opfrac[:, :], opfrac[:, :], 1 / 64, None, ALU.mult))
            link(pool.tensor_scalar(steps4[:, :], steps4[:, :], 4.0, None, ALU.mult))
            pool.sem_inc(consts_made, 1)

            pool.wait_ge(weights_loaded, 16 * 8)
            twice = [w1[:, n].rearrange("p h (o c) -> p h o c", o=1).to_broadcast([P, NH1, 2, C]) for n in range(2)]
            for n in range(2):
                link(pool.tensor_copy(wqk[:, n, 0], twice[n]))
            wv = w1[:, 2].rearrange("p h c -> p (h c)")
            link(pool.tensor_copy(wv1[:, 0, :], wv))
            for n in range(2):
                link(pool.tensor_tensor(wqk[:, n, 1], twice[n], wqk[:, n, 0], ALU.subtract))
            link(pool.tensor_tensor(wv1[:, 1, :], wv, wv1[:, 0, :], ALU.subtract))
            pool.sem_inc(weights_split, 1)

            for k in range(3, 3 * B + 3):
                power(k)

        def dve_attention(dve, s, base, ngroups, y_out):
            n = GRP * ngroups
            bu, bg = base(n), base(ngroups)
            for i in range(n + LAG_YD + 2):
                if i < n:
                    dve.wait_ge(s["scored"], bu + (i + 1))
                    dve.tensor_reduce(negm[:, i % 4:i % 4 + 1], scores2[i % 2], AX.X, ALU.max, negate=True)\
                       .then_inc(s["maxed"], 1)
                if 1 <= i <= n:
                    u = i - 1
                    dve.wait_ge(s["exped"], bu + (u + 1))
                    dve.reciprocal(rinv[:, u % 4:u % 4 + 1], rsum[:, u % 4:u % 4 + 1]).then_inc(s["inverted"], 1)
                if 1 <= i <= n:
                    u = i - 1
                    dve.wait_ge(s["inverted"], bu + (u + 1))
                    dve.tensor_scalar(prob[:, u % 3, :], prob[:, u % 3, :], rinv[:, u % 4:u % 4 + 1], None,
                                      ALU.mult).then_inc(s["scaled"], 1)
                u = i - 2
                if 0 <= u < n:
                    g, lane, qt = u // GRP, u % 2, (u % GRP) // 2
                    dve.wait_ge(s["hi_turned"], bu + (u + 1))
                    dve.tensor_copy(PT[:, g % 2, lane, 4:8, qt * P:(qt + 1) * P],
                                    HI.rearrange("p (k q) -> p k q", k=4)).then_inc(s["hi_drained"], 1)
                for g in range(ngroups):
                    if i == GRP * g + LAG_YD:
                        y_out(g, bg)

        @block.vector
        def _(dve):
            def bc(v, k=NT):
                return v.rearrange("p (t o) -> p t o", o=1).to_broadcast([P, k, C])

            def rows(v, k=NT):
                return v.rearrange("p (o c) -> p o c", o=1).to_broadcast([P, k, C])

            def moment(k, x, n):
                buf = xn[:, (k - 1) % 2]
                if n:
                    dve.wait_ge(ln_chain, (k - 1) * LN + n)
                if n == 0:
                    ins = dve.tensor_reduce(mean[:, :], x, AX.X, ALU.add)
                elif n == 1:
                    ins = dve.tensor_scalar(mean[:, :], mean[:, :], 1.0 / C, None, ALU.mult)
                elif n == 2:
                    ins = dve.tensor_tensor(buf, x, bc(mean[:, :]), ALU.subtract)
                elif n == 3:
                    ins = dve.tensor_tensor(xsq[:, :, :], buf, buf, ALU.mult)
                elif n == 4:
                    ins = dve.tensor_reduce(var[:, :], xsq[:, :, :], AX.X, ALU.add)
                else:
                    ins = dve.tensor_scalar(var[:, :], var[:, :], 1.0 / C, EPS, ALU.mult, ALU.add)
                ins.then_inc(ln_chain, 1)

            def moments(k, x):
                for n in range(LN):
                    moment(k, x, n)

            def divide(k, twice=False):
                dve.wait_ge(rstd_made, k)
                buf = xn[:, (k - 1) % 2]
                if twice:
                    dve.tensor_tensor(xn2[:, :, 0, :], buf, bc(rstd[:, :]), ALU.mult)
                    dve.tensor_tensor(xn2[:, :, 1, :], buf, bc(rstd[:, :]), ALU.mult).then_inc(normed, 1)
                else:
                    dve.tensor_tensor(buf, buf, bc(rstd[:, :]), ALU.mult).then_inc(normed, 1)

            def filled(key):
                dve.wait_ge(side_filled, order[key] + 1)
                return side_bank(key)

            def tiles_of(img):
                return slice(img * NT, (img + 1) * NT)

            def drain_x(img, what, col):
                bank = filled((what, img, 1))
                dve.tensor_scalar(xT[0:C, img, BLK:TOK], bank[0:C, :], norm[:, col:col + 1], norm[:, col + 1:col + 2],
                                  ALU.mult, ALU.add).then_inc(side_drained["dve"], 1)

            def split_bank(key):
                dve.wait_ge(side_high, split.index(key) + 1)
                return side_bank(key)

            def drain_q(img):
                for blk in range(NB):
                    high, low = (q0S[:, img, part, blk * BLK:(blk + 1) * BLK] for part in range(2))
                    dve.tensor_tensor(low, split_bank(("q", img, blk)), high, ALU.subtract)\
                       .then_inc(side_drained["dve"], 1)

            def drain_k(img):
                for blk in range(NB):
                    k = k0S[:, img, blk * BLK:(blk + 1) * BLK]
                    dve.scalar_tensor_tensor(k, k, low_rows[:, 0:1], split_bank(("k", img, blk)), ALU.mult, ALU.add)\
                       .then_inc(side_drained["dve"], 1)

            def drain_v(img):
                for m, tiles in enumerate((range(NT), range(NT, NT + 2))):
                    bank = filled(("v", img, m))
                    t0, full, k = tiles[0], len(tiles) - 1, VTILES[tiles[-1]][1]
                    for p, lo, n in ((P, 0, full), (k, full, 1)):
                        ins = dve.tensor_copy(
                            V0[0:p, img, t0 + lo:t0 + lo + n, :, 0:HD0],
                            bank[0:p, lo * C:(lo + n) * C].rearrange("p (t h d) -> p t h d", t=n, h=NH0))
                    ins.then_inc(side_drained["dve"], 1)

            def add_projection(img):
                dve.wait_ge(c0["y_filled"], img + 1)
                dve.wait_ge(biased, 2 * img + 1)
                x1 = xall[:, tiles_of(img), :]
                dve.tensor_tensor(x1, xb[:, tiles_of(img), :], YB.rearrange("p (t c) -> p t c", t=NT), ALU.add)\
                   .then_inc(c0["y_drained"], 1)
                dve.wait_ge(c0["y_drained"], img + 1)
                dve.tensor_tensor(xb[:, tiles_of(img), :], x1, rows(fb2[:, :]), ALU.add).then_inc(biased, 1)

            def add_mlp(img):
                bank = filled(("mlp", img, 0))
                dve.wait_ge(biased, 2 * img + 2)
                x1 = xall[:, tiles_of(img), :]
                dve.tensor_tensor(x1, xb[:, tiles_of(img), :], bank.rearrange("p (t c) -> p t c", t=NT), ALU.add)\
                   .then_inc(side_drained["dve"], 1)
                side_wait(dve, ("mlp", img, 0))
                dve.tensor_tensor(x2[:, tiles_of(img), :], x1, rows(bu1[:, :]), ALU.add).then_inc(biased, 1)

            def drain_a(img):
                for blk in range(NB):
                    low = aS[C:P, img * TOK + blk * BLK:img * TOK + (blk + 1) * BLK]
                    dve.tensor_tensor(low, split_bank(("a", img, blk))[C:P, :], low, ALU.subtract)\
                       .then_inc(side_drained["dve"], 1)

            dve.wait_ge(x_loaded[0], 16)
            moments(1, xall[:, tiles_of(0), :])
            divide(1)
            dve.wait_ge(bias_expanded, 1)
            dve.wait_ge(consts_made, 2)
            n = NH0 * REL
            for bank in range(4):
                j0, k = 9 * bank, min(9, WW - 9 * bank)
                last = dve.tensor_tensor(tall[:, :, j0:j0 + k].rearrange("p n j -> p j n"),
                                         PS[0:WW, 4 + bank, 0:k * n].rearrange("p (j n) -> p j n", n=n),
                                         colmask[:, j0:j0 + k].rearrange("p (j o) -> p j o", o=1)
                                         .to_broadcast([WW, k, n]), ALU.add)
            last.then_inc(bias_masked, 1)
            dve.wait_ge(qkv_loaded, QKV_LOADS)
            drain_x(0, "x", 0)
            dve.wait_ge(bias_masked, 1)
            bias_table(lambda di, ins: ins.then_inc(tables_made, 1), dve.tensor_copy, 1)
            dve.wait_ge(ident_made, 1)
            second = ident[:, :].rearrange("p (h l d) -> p h l d", h=NH0, l=2)[:, :, 1, :]
            dve.tensor_reduce(low_rows[:, :], second, AX.XY, ALU.add, negate=True).then_inc(low_rows_made, 1)
            dve.wait_ge(low_rows_made, 1)
            drain_q(0)
            drain_k(0)
            dve.wait_ge(consts_made, 3)
            drain_v(0)

            dve.wait_ge(w_loaded, W_LOADS)
            dve.wait_ge(x_loaded[1], 16)
            dve.tensor_tensor(xb[:, :, :], xall[:, :, :], rows(pb0[:, :], NTILE), ALU.add).then_inc(biased, 1)

            dve.wait_ge(tables_made, 2 * ROWS)
            for i in range(UN0 + 3):
                if i == (NT - 1) * NH0:
                    dve.wait_ge(last_table_made, ROWS)
                if i < UN0:
                    _, nrows, kind = window_keys(i // NH0 % NT)
                    w = nrows * WW
                    dve.wait_ge(c0["scored"], i + 1)
                    if i >= 3:
                        dve.wait_ge(c0["exped"], i - 2)
                    dve.tensor_tensor_reduce(sbias[:, i % 3, 0:w], PS[:, i % 2, 0:w],
                                             tabs[kind][:, i % NH0, :, :].rearrange("p a b -> p (a b)"),
                                             1.0, 3 * NEG, ALU.add, ALU.max, maxp[:, i % 4:i % 4 + 1])\
                       .then_inc(c0["biased"], 1)
                if 1 <= i <= UN0:
                    u = i - 1
                    dve.wait_ge(c0["exped"], u + 1)
                    dve.reciprocal(rinv[:, u % 4:u % 4 + 1], rsum[:, u % 4:u % 4 + 1])\
                       .then_inc(c0["inverted"], 1)
                if i < UN0:
                    dve.wait_ge(c0["biased"], i + 1)
                    dve.tensor_scalar(negm[:, i % 4:i % 4 + 1], maxp[:, i % 4:i % 4 + 1], -1.0, None, ALU.mult)\
                       .then_inc(c0["maxed"], 1)
                if 1 <= i <= UN0:
                    u = i - 1
                    w = window_keys(u // NH0 % NT)[1] * WW
                    dve.wait_ge(c0["inverted"], u + 1)
                    dve.tensor_scalar(prob[:, u % 3, 0:w], prob[:, u % 3, 0:w], rinv[:, u % 4:u % 4 + 1], None,
                                      ALU.mult).then_inc(c0["scaled"], 1)
                u = i - 2
                if 0 <= u < UN0 and u % 2 == 1:
                    dve.wait_ge(c0["hi_turned"], u // 2 + 1)
                    nat_drain(dve.tensor_copy, None, HI, u).then_inc(c0["hi_drained"], 1)
                if 0 <= i - LN1_STEP < LN:
                    moment(2, xall[:, tiles_of(1), :], i - LN1_STEP)
                if i == LN1_STEP + LN + 1:
                    divide(2)
                if i == at_step["x", 1][1]:
                    drain_x(1, "x", 0)
                if i == at_step["q", 1][1]:
                    drain_q(1)
                if i == at_step["k", 1][1]:
                    drain_k(1)
                if i == at_step["v", 1][1]:
                    drain_v(1)
                if i == SUM_STEP:
                    add_projection(0)
                if 0 < i - SUM_STEP <= LN:
                    moment(3, xall[:, tiles_of(0), :], i - SUM_STEP - 1)
                if i == LN2_STEP:
                    divide(3)
                if i == at_step["y", 0][1]:
                    drain_x(0, "y", 2)
                if i == at_step["mlp", 0][1]:
                    add_mlp(0)
                if 0 < i - at_step["mlp", 0][1] <= LN:
                    moment(4, xall[:, tiles_of(0), :], i - at_step["mlp", 0][1] - 1)
                if i == LN3_STEP:
                    divide(4, twice=True)
                if i == at_step["a", 0][1]:
                    drain_a(0)
            add_projection(1)
            moments(5, xall[:, tiles_of(1), :])

            def low_part(n, bank, scales=(C ** -0.25, C ** -0.25), done=piece_drained):
                what, lane, blk = PIECES[n]
                toks = slice(blk * BLK, (blk + 1) * BLK)
                if what == "v":
                    half = QT // 2
                    ins = dve.tensor_copy(V[:, blk * QT + half:(blk + 1) * QT, :],
                                          bank[:, half * P:].rearrange("p (t c) -> p t c", t=half))
                elif what == "k":
                    low = kS[C:P, lane, toks]
                    ins = dve.scalar_tensor_tensor(low, bank[C:P, :], scales[0], low, ALU.mult, ALU.subtract)
                else:
                    ins = dve.scalar_tensor_tensor(qS[:, 1, lane, toks], bank, scales[1], qS[:, 0, lane, toks],
                                                   ALU.mult, ALU.subtract)
                ins.then_inc(done, 1)

            for n in range(HALF):
                if n == 3:
                    divide(5)
                if n == EARLY:
                    drain_x(1, "y", 2)
                dve.wait_ge(piece_high, n + 1)
                low_part(n, PS[:, n % 4, :])

            def rest_of_stage1(i):
                if i == ADD_STEP:
                    add_mlp(1)
                if 0 <= i - ADD_STEP < LN // 2:
                    for n in range(2):
                        moment(6, xall[:, tiles_of(1), :], 2 * (i - ADD_STEP) + n)
                if i == DIVIDE_STEP:
                    divide(6, twice=True)
                if i == INPUT_STEP:
                    drain_a(1)
                    dve.wait_ge(biased, 2 * B + 1)

            def glob_pair(pair, steps=range(UP), cur=True, prev=True, last=False, beside=None):
                bu, bg, bp, bw = (product(pair, k, dve) for k in (UP, GP, NPC, 3 * GP))

                def live(index):
                    return cur if index >= 0 else prev

                for i in steps:
                    if cur:
                        dve.wait_ge(c1["scored"], bu + (i + 1))
                        dve.tensor_reduce(negm[:, i % 4:i % 4 + 1], scores2[i % 2], AX.X, ALU.max, negate=True)\
                           .then_inc(c1["maxed"], 1)
                    for m in pieces_at(i - 1, pair, last) if cur else ():
                        if len(pieces_at(i - 1, pair, last)) == 1:
                            dve.wait_ge(piece_high, bp + (HALF + m + 1))
                            low_part((HALF + m) % NPC, bank_of(pair, m))
                    u = i - DRAIN - 1
                    if live(u):
                        g, lane, qt = u // GRP, u % 2, (u % GRP) // 2
                        dve.wait_ge(c1["hi_turned"], bu + (u + 1))
                        dve.tensor_copy(PT[:, g % 2, lane, 4:8, qt * P:(qt + 1) * P],
                                        HI.rearrange("p (k q) -> p k q", k=4)).then_inc(c1["hi_drained"], 1)
                    g = (i - Y_DRAIN) // GRP
                    if (i - Y_DRAIN) % GRP == 0 and live(g):
                        slot = g % GP
                        dve.reciprocal(weight[:, slot], sums[:, slot]).then_inc(weighed, 1)
                        dve.wait_ge(c1["y_filled"], bg + (g + 1))
                        dve.wait_ge(weighed, bw + (3 * g + 1))
                        dve.tensor_tensor(yw[:, :, :, :], YB.rearrange("p (t l c) -> p t l c", t=QT, l=2),
                                          weight[:, slot].rearrange("p t (l o) -> p t l o", o=1)
                                          .to_broadcast([P, QT, 2, C]), ALU.mult).then_inc(c1["y_drained"], 1)
                        part = x2[:, slot * QT:(slot + 1) * QT, :]
                        dve.wait_ge(c1["y_drained"], bg + (g + 1))
                        dve.tensor_tensor(part, part, yw[:, :, 0, :], ALU.add).then_inc(weighed, 1)
                        dve.wait_ge(weighed, bw + (3 * g + 2))
                        dve.tensor_tensor(part, part, yw[:, :, 1, :], ALU.add).then_inc(weighed, 1)
                    for m in pieces_at(i, pair, last) if cur else ():
                        if len(pieces_at(i, pair, last)) > 1:
                            dve.wait_ge(piece_high, bp + (HALF + m + 1))
                            low_part((HALF + m) % NPC, bank_of(pair, m))
                    if beside:
                        beside(i)

            glob_pair(0, prev=False, beside=rest_of_stage1)
            with dve.Fori(1, NPAIR - 1) as pair:
                glob_pair(pair)
            glob_pair(NPAIR - 1, last=True)

            cn = [0]

            def link(ins):
                cn[0] += 1
                ins.then_inc(codes_made, 1)
                dve.wait_ge(codes_made, cn[0])
            dve.wait_ge(late_loaded, 32)
            dve.wait_ge(consts_made, 4)
            link(dve.tensor_copy(codes[:, :, :], mask8[:, 0, :, :]))
            link(dve.tensor_copy(codew[:, :, :], mask8[:, 1, :, :]))
            link(dve.scalar_tensor_tensor(codes[:, :, :], codes[:, :, :], 2.0, codew[:, :, :], ALU.mult, ALU.add))
            link(dve.memset(nextf[:, :], -4.0))

            def choose(now, bank=YB):
                base = now * NCTL
                n = [0]

                def link(ins):
                    n[0] += 1
                    ins.then_inc(ctl_chain, 1)
                    dve.wait_ge(ctl_chain, base + n[0])
                dve.wait_ge(row_turned, now + 1)
                link(dve.tensor_copy(row[:, :], bank[0:1, 0:C]))
                link(dve.tensor_reduce(top[:, :], row[:, 0:NOPS], AX.X, ALU.max))
                link(dve.scalar_tensor_tensor(cand[:, :], row[:, 0:NOPS], top[:, 0:1], opfrac[:, :],
                                              ALU.is_lt, ALU.add))
                link(dve.tensor_reduce(opf[:, :], cand[:, :], AX.X, ALU.min))
                link(dve.scalar_tensor_tensor(
                    codew[:, :, :], opfrac[:, :].rearrange("p (o n) -> p o n", o=1).to_broadcast([1, NSTEP, NOPS]),
                    opf[:, 0:1], codes[:, :, :], ALU.is_equal, ALU.mult))
                link(dve.tensor_reduce(code[:, :], codew[:, :, :], AX.X, ALU.add))
                link(dve.tensor_scalar(dead[:, :], steps4[:, :], nextf[:, 0:1], float(NONE), ALU.is_le, ALU.mult))
                link(dve.tensor_scalar(key[:, :], code[:, :], 0.0, float(NONE), ALU.is_equal, ALU.mult))
                link(dve.tensor_tensor(key[:, :], key[:, :], dead[:, :], ALU.max))
                link(dve.tensor_tensor(code[:, :], code[:, :], steps4[:, :], ALU.add))
                link(dve.tensor_tensor(key[:, :], key[:, :], code[:, :], ALU.max))
                link(dve.tensor_reduce(nextf[:, :], key[:, :], AX.X, ALU.min))
                assert n[0] == NCTL
                dve.tensor_scalar(control[:, bass.ds(now, 1), 1:2], opf[:, :].rearrange("p (a b) -> p a b", a=1),
                                  64.0, None, ALU.mult)
                dve.tensor_copy(control[:, bass.ds(now, 1), 0:1], nextf[:, :].rearrange("p (a b) -> p a b", a=1))\
                   .then_inc(control_ready, 1)

            def drain_state(img, bank):
                dve.wait_ge(r3["hi_filled"], img + 1)
                dve.tensor_copy(aT[:, img * TOK + BLK:(img + 1) * TOK], bank[0:C, :]).then_inc(r3["hi_drained"], 1)

            dve.wait_ge(weighed, 3 * (GP * (NPAIR - 1) + GP // B))
            moments(3 * B + 1, x2[:, tiles_of(0), :])
            divide(3 * B + 1)
            for i in range(Y_DRAIN + GRP * (GP - 1) - UP + 1):
                glob_pair(NPAIR, steps=(i,), cur=False)
                if i == STATE_STEPS[0]:
                    drain_state(0, PS[:, 1, :])
                if i == STATE_STEPS[1]:
                    choose(0, PS[:, 2, :])
            dve.wait_ge(weighed, 3 * GP * NPAIR)
            moments(3 * B + 2, x2[:, tiles_of(1), :])
            divide(3 * B + 2)
            drain_state(1, HI)


            def low_state(high, done, base, pieces):
                size = B * TOK // pieces
                for n in range(pieces):
                    toks = slice(n * size, (n + 1) * size)
                    dve.wait_ge(high, base + (n + 1))
                    dve.tensor_tensor(hS[C:P, toks], aT[:, toks], hS[0:C, toks], ALU.subtract).then_inc(done, 1)

            def attend(na, step, slot):
                base = lambda k: dve.snap(na * k)
                by, bp = base(N2["y"]), base(N_SPLIT)
                low_state(routed_high, routed_split, bp, 2)
                twice = ws[:, :, :].rearrange("c n (o d) -> c n o d", o=1).to_broadcast([C, 3, 2, C])
                for n, rows in enumerate((slice(0, C), slice(C, P))):
                    dve.wait_ge(routed_high, bp + (3 + n))
                    dve.tensor_tensor(wsS[rows, 1], twice, wsS[0:C, 0], ALU.subtract).then_inc(routed_split, 1)
                for n in range(HALF):
                    dve.wait_ge(routed_high, bp + (4 + n + 1))
                    low_part(n, PS[:, n % 4, :], (1.0, C ** -0.5), routed_split)

                def y_out(g, bg):
                    for lane in range(2):
                        dve.wait_ge(c2["y_filled"], by + (2 * g + lane + 1))
                        dve.tensor_copy(aT[:, lane * TOK + g * BLK:lane * TOK + (g + 1) * BLK], YB[0:C, :])\
                           .then_inc(c2["y_drained"], 1)
                dve_attention(dve, c2, base, 2, y_out)

            def feed(nf, step, slot):
                bhi = dve.snap(nf * (B * NB))
                bs = dve.snap(nf * N_FSPLIT)
                for n, rows in enumerate((slice(0, C), slice(C, P))):
                    dve.wait_ge(ffn_high, bs + (1 + n))
                    dve.tensor_tensor(w1S[rows, 1], w1s[:, :], w1S[0:C, 0], ALU.subtract).then_inc(ffn_split, 1)
                low_state(ffn_high, ffn_split, bs + 2, B * NB)
                n = 0
                for blk in range(B * NB):
                    n += 1
                    dve.wait_ge(rf["hi_filled"], bhi + n)
                    dve.tensor_scalar(Z[:, 1, blk * BLK:(blk + 1) * BLK], HI, b1s[:, 1:2], 0.0, ALU.add, ALU.max)\
                       .then_inc(rf["hi_drained"], 1)
                for two, bank in enumerate((LO, HI)):
                    dve.wait_ge(ffn_out_filled, dve.snap(nf * 2) + (two + 1))
                    dve.tensor_scalar(aT[:, (2 * two + 1) * BLK:(2 * two + 2) * BLK], bank[C:P, :], b2s[C:P, 0:1], None,
                                      ALU.add).then_inc(rf["hi_drained"], 1)

            scan(dve, attend, feed, choose)

            for blk in range(B * NB):
                which, bank = (("lo", LO), ("hi", HI))[blk % 2]
                dve.wait_ge(re[which + "_filled"], blk // 2 + 1)
                part = x2[:, blk * QT:(blk + 1) * QT, :]
                dve.tensor_tensor(part, part, bank[:, 0:QT * C].rearrange("p (t c) -> p t c", t=QT), ALU.add)\
                   .then_inc(re[which + "_drained"], 1)

        @block.sync
        def _(sp):
            x_tok = a["x"].rearrange("b i j c -> (b i j) c").rearrange("(g p) c -> p g c", p=P)
            for img in range(B):
                tiles = slice(img * NT, (img + 1) * NT)
                sp.dma_start(xall[:, tiles, :], x_tok[:, tiles, :]).then_inc(x_loaded[img], 16)
            qkv = a["L0_conv_qkv_w"]

            def row(src):
                return src.rearrange("(o c) -> o c", o=1).to_broadcast([P, C])
            sp.dma_start(wqkv[0:C, :, :].rearrange("c n d -> c (n d)"), qkv).then_inc(qkv_loaded, 16)
            sp.dma_start(wqkv[C:C + 1, :, :].rearrange("c n d -> c (n d)"),
                         a["L0_conv_qkv_b"].rearrange("(o c) -> o c", o=1)).then_inc(qkv_loaded, 16)
            sp.wait_ge(zeroed, 1)

            def load(dst, src, **kw):
                sp.dma_start(dst, src, **kw).then_inc(w_loaded, 16)
            for h in range(NH0):
                load(pw0[32 * h:32 * h + HD0, :], a["L0_conv_proj_w"][h * HD0:(h + 1) * HD0, :])
            for dst, name in ((pb0, "L0_conv_proj_b"), (fb2, "L0_conv_fc2_b"), (bu1, "L1_attn_bu")):
                load(dst[:, :], row(a[name]))
            load(fc1[:, :], a["L0_conv_fc1_w"])
            load(fc2[:, :, :], a["L0_conv_fc2_w"].rearrange("(h p) c -> p h c", p=P))
            sp.dma_start(mask8[:, 0, :, :], a["L1_ffn_attn_mask"].rearrange("(o s) n -> o s n", o=1)).then_inc(late_loaded, 16)
            sp.dma_start(mask8[:, 1, :, :], a["L1_ffn_ffn_mask"].rearrange("(o s) n -> o s n", o=1)).then_inc(late_loaded, 16)
            for n, name in enumerate(("L1_attn_Wq", "L1_attn_Wk", "L1_attn_Wv")):
                for part in range(2):
                    sp.dma_start(w1[part * C:(part + 1) * C, n].rearrange("p h c -> p (h c)"), a[name])\
                      .then_inc(weights_loaded, 16)
            sp.wait_ge(zeroed, 2)
            for lane in range(2):
                sp.dma_start(wu1[lane * C:(lane + 1) * C, :, lane, :],
                             a["L1_attn_Wu"].rearrange("(n l p) c -> l p n c", l=2, p=C)[lane])\
                  .then_inc(weights_loaded, 16)

            def of(step, slot):
                n = sp.value_load(control[0:1, bass.ds(slot, 1), 1:2], min_val=0, max_val=NOPS - 1)
                return lambda name: a["L1_ffn_" + name][bass.ds(step, 1), bass.ds(n, 1)]

            def attend(na, step, slot):
                w = of(step, slot)
                for dst, name in ((ws[:, 0, :], "wk"), (ws[:, 1, :], "wq"), (ws[:, 2, :], "wv")):
                    sp.dma_start(dst, w(name).rearrange("s n c d -> (s n c) d")).then_inc(attn_loaded, 16)
                for part in range(2):
                    sp.dma_start(wos[part * C:(part + 1) * C, :], w("wo").rearrange("s n c d -> (s n c) d"))\
                      .then_inc(wo_loaded, 16)

            def feed(nf, step, slot):
                w = of(step, slot)
                sp.dma_start(w1s[:, :], w("ffn_w1").rearrange("s n c d -> (s n c) d")).then_inc(ffn_loaded, 16)
                sp.dma_start(w2s[:, :, :], w("ffn_w2").rearrange("s n (h p) c -> p (s n h) c", p=P))\
                  .then_inc(ffn_loaded, 16)
                sp.dma_start(b1s[:, :], w("ffn_b1").rearrange("s n (h p) -> p (s n h)", p=P),
                             allow_slow_non_contiguous=True).then_inc(ffn_loaded, 16)
                for part in range(2):
                    sp.dma_start(b2s[part * C:(part + 1) * C, :], w("ffn_b2").rearrange("s n (c o) -> (s n c) o", o=1))\
                      .then_inc(ffn_loaded, 16)
            scan(sp, attend, feed, None)

            out_tok = out.rearrange("b i j c -> (b i j) c").rearrange("(g p) c -> p g c", p=P)
            for blk in range(B * NB):
                which = ("lo", "hi")[blk % 2]
                sp.wait_ge(re[which + "_drained"], blk // 2 + 1)
                sp.dma_start(out_tok[:, blk * QT:(blk + 1) * QT, :], x2[:, blk * QT:(blk + 1) * QT, :])\
                  .then_inc(stored, 16)
            sp.wait_ge(stored, 16 * B * NB)


def kernel(**inputs):
    import numpy as _np
    import concourse.bacc as _bacc
    from concourse import mybir as _mybir
    from concourse.bass_utils import run_bass_kernel_spmd as _run

    nc = _bacc.Bacc("TRN2", target_bir_lowering=False, num_devices=1)
    arrays, args = {}, {}
    for name in inputs:
        v = _np.ascontiguousarray(inputs[name])
        arrays[f"in_{name}_dram"] = v
        args[name] = nc.dram_tensor(f"in_{name}_dram", v.shape, _mybir.dt.from_np(v.dtype), kind="ExternalInput").ap()
    out = nc.dram_tensor("out_0_dram", (2, 32, 32, 64), _mybir.dt.float32, kind="ExternalOutput").ap()
    build(nc, args, out)
    r = _run(nc, [arrays], core_ids=[0])
    return r.results[0]["out_0_dram"]
```
